# Optimizing a Trainium2 kernel written in Bass

```python
import numpy as np
import jax
import jax.numpy as jnp

def _softmax(x, axis=-1):
    return jax.nn.softmax(x, axis=axis)

def _gelu(x):
    return jax.nn.gelu(x, approximate=True)

def _silu(x):
    return jax.nn.silu(x)

def _sigmoid(x):
    return jax.nn.sigmoid(x)

def _layernorm(x, axis=-1, eps=1e-05):
    m = jnp.mean(x, axis=axis, keepdims=True)
    v = jnp.var(x, axis=axis, keepdims=True)
    return (x - m) / jnp.sqrt(v + eps)

def _scatter_add(tgt, idx, src, axis=0):
    return tgt.at[idx].add(src)

def _segment_sum(src, seg, n):
    return jax.ops.segment_sum(src, seg, n)
kernel_name = 'mk_gnn_resnorm_d4_gnn_r64_f2e761'

def setup_inputs(seed: int=0):
    np.random.seed(seed)
    _w = jnp.asarray

    def _rec_inputs():
        import jax
        import jax.numpy as jnp
        _gk = jax.random.key(seed)
        x = -0.0003713 + 1 * jax.random.normal(jax.random.fold_in(_gk, 1), (50000, 256), jnp.float32)
        src = jax.random.randint(jax.random.fold_in(_gk, 2), (25000,), 0, 50000, jnp.int32)
        dst = jnp.minimum((50000 * jax.random.uniform(jax.random.fold_in(_gk, 3), (25000,)) ** 2.0).astype(jnp.int32), 49999)
        _o = jnp.argsort(dst, stable=True)
        src = src[_o]
        dst = dst[_o]
        return (x, src, dst)
    x, src, dst = _rec_inputs()

    def _L0_gnn_setup():
        import jax, jax.numpy as jnp
        import numpy as np
        N_NODES = 50000

        def gcn_conv(x, W, b, src, dst, n_nodes):
            h = x @ W
            ones = jnp.ones(src.shape[0], dtype=h.dtype)
            deg = jax.ops.segment_sum(ones, dst, num_segments=n_nodes) + 1.0
            dinv = jax.lax.rsqrt(deg)
            norm = dinv[src] * dinv[dst]
            msg = h[src] * norm[:, None]
            agg = jax.ops.segment_sum(msg, dst, num_segments=n_nodes)
            agg = agg + h * (dinv * dinv)[:, None]
            return agg + b
        key = jax.random.key(seed)
        k1, k2, k3, k4 = jax.random.split(key, 4)
        embedding = jax.random.normal(k1, (N_NODES, 256), dtype=jnp.float32)
        edge_index = jax.random.randint(k2, (2, 12500), 0, N_NODES, dtype=jnp.int64)
        W1 = jax.random.normal(k3, (256, 64), dtype=jnp.float32) / np.sqrt(256.0)
        b1 = jnp.zeros((64,), dtype=jnp.float32)
        W2 = jax.random.normal(k4, (64, 256), dtype=jnp.float32) / np.sqrt(64.0)
        b2 = jnp.zeros((256,), dtype=jnp.float32)
        return {'embedding': embedding, 'edge_index': edge_index, 'W1': W1, 'b1': b1, 'W2': W2, 'b2': b2}
    _L0_gnn_all = _L0_gnn_setup()
    _L0_gnn_in = {k: v for k, v in _L0_gnn_all.items() if k in ('W1', 'b1', 'W2', 'b2')}
    del _L0_gnn_all

    def _L1_gnn_setup():
        import jax, jax.numpy as jnp
        import numpy as np
        N_NODES = 100000
        F_DIM = 256
        NNZ = 25000

        def _prelu(x, a):
            return jnp.where(x >= 0, x, a * x)

        def _hconv(x, W, b, src, dst, n):
            xt = x @ W
            ones = jnp.ones(src.shape, xt.dtype)
            D = jax.ops.segment_sum(ones, src, num_segments=n)
            B = jax.ops.segment_sum(ones, dst, num_segments=n)
            Dinv = jnp.where(D > 0, 1.0 / D, 0.0)
            Binv = jnp.where(B > 0, 1.0 / B, 0.0)
            m = jax.ops.segment_sum(xt[src], dst, num_segments=n) * Binv[:, None]
            out = jax.ops.segment_sum(m[dst], src, num_segments=n) * Dinv[:, None]
            return out + b
        key = jax.random.key(seed)
        k0, k1, k2, k3 = jax.random.split(key, 4)
        x = jax.random.normal(k0, (N_NODES, F_DIM), dtype=jnp.float32)
        edge_index = jax.random.randint(k1, (2, NNZ), 0, N_NODES, dtype=jnp.int32)
        scale = (2.0 / F_DIM) ** 0.5
        W1 = jax.random.normal(k2, (F_DIM, F_DIM), dtype=jnp.float32) * scale
        W2 = jax.random.normal(k3, (F_DIM, F_DIM), dtype=jnp.float32) * scale
        b1 = jnp.zeros((F_DIM,), jnp.float32)
        b2 = jnp.zeros((F_DIM,), jnp.float32)
        a = jnp.full((1,), 0.25, jnp.float32)
        return {'x': x, 'edge_index': edge_index, 'W1': W1, 'b1': b1, 'W2': W2, 'b2': b2, 'a': a}
    _L1_gnn_all = _L1_gnn_setup()
    _L1_gnn_in = {k: v for k, v in _L1_gnn_all.items() if k in ('W1', 'b1', 'W2', 'b2', 'a')}
    del _L1_gnn_all

    def _L2_gnn_setup():
        import jax, jax.numpy as jnp
        import numpy as np
        N = 100000
        E = 12500
        F_IN = 256
        HID = 64
        H = 4
        NEG_SLOPE = 0.2
        BN_EPS = 1e-05

        def _add_self_loops(edge_index, n):
            loop = jnp.arange(n, dtype=edge_index.dtype)
            src = jnp.concatenate([edge_index[0], loop])
            dst = jnp.concatenate([edge_index[1], loop])
            return (src, dst)

        def _batch_norm(x, g, b):
            m = x.mean(0)
            v = x.var(0)
            return g * (x - m) * jax.lax.rsqrt(v + BN_EPS) + b

        def _gcn_conv(x, src, dst, W, b, n):
            deg = jax.ops.segment_sum(jnp.ones_like(dst, jnp.float32), dst, n)
            dinv = jax.lax.rsqrt(jnp.maximum(deg, 1.0))
            norm = dinv[src] * dinv[dst]
            h = x @ W
            out = jax.ops.segment_sum(h[src] * norm[:, None], dst, n)
            return out + b

        def _gat_conv(x, src, dst, W, a_src, a_dst, b, n):
            h = (x @ W).reshape(n, H, HID)
            alpha_s = jnp.einsum('nhc,hc->nh', h, a_src)
            alpha_d = jnp.einsum('nhc,hc->nh', h, a_dst)
            e = alpha_s[src] + alpha_d[dst]
            e = jnp.where(e > 0, e, NEG_SLOPE * e)
            emax = jax.ops.segment_max(e, dst, n)
            w = jnp.exp(e - emax[dst])
            wsum = jax.ops.segment_sum(w, dst, n)
            att = w / wsum[dst]
            out = jax.ops.segment_sum(att[:, :, None] * h[src], dst, n)
            return out.reshape(n, H * HID) + b
        key = jax.random.key(seed)
        ks = jax.random.split(key, 20)
        s = 0.05
        return {'x': jax.random.normal(ks[0], (N, F_IN), jnp.float32), 'edge_index': jax.random.randint(ks[1], (2, E), 0, N, jnp.int64), 'W_gcn': jax.random.normal(ks[2], (F_IN, HID), jnp.float32) * s, 'b_gcn': jnp.zeros((HID,), jnp.float32), 'g0': jnp.ones((HID,), jnp.float32), 'beta0': jnp.zeros((HID,), jnp.float32), 'W1': jax.random.normal(ks[3], (HID, H * HID), jnp.float32) * s, 'a_src1': jax.random.normal(ks[4], (H, HID), jnp.float32) * s, 'a_dst1': jax.random.normal(ks[5], (H, HID), jnp.float32) * s, 'b1': jnp.zeros((H * HID,), jnp.float32), 'g1': jnp.ones((H * HID,), jnp.float32), 'beta1': jnp.zeros((H * HID,), jnp.float32), 'W2': jax.random.normal(ks[6], (H * HID, H * HID), jnp.float32) * s, 'a_src2': jax.random.normal(ks[7], (H, HID), jnp.float32) * s, 'a_dst2': jax.random.normal(ks[8], (H, HID), jnp.float32) * s, 'b2': jnp.zeros((H * HID,), jnp.float32), 'g2': jnp.ones((H * HID,), jnp.float32), 'beta2': jnp.zeros((H * HID,), jnp.float32)}
    _L2_gnn_all = _L2_gnn_setup()
    _L2_gnn_in = {k: v for k, v in _L2_gnn_all.items() if k in ('W_gcn', 'b_gcn', 'g0', 'beta0', 'W1', 'a_src1', 'a_dst1', 'b1', 'g1', 'beta1', 'W2', 'a_src2', 'a_dst2', 'b2', 'g2', 'beta2')}
    del _L2_gnn_all

    def _L3_gnn_setup():
        import jax, jax.numpy as jnp
        import numpy as np
        N_NODES = 20000
        N_EDGES = 5000
        D = 256
        N_LAYERS = 3
        BN_EPS = 1e-05
        key = jax.random.key(seed)
        ks = jax.random.split(key, 5)
        x = jax.random.normal(ks[0], (N_NODES, D), dtype=jnp.float32)
        src = jax.random.randint(ks[1], (N_EDGES,), 0, N_NODES)
        dst = jax.random.randint(ks[2], (N_EDGES,), 0, N_NODES)
        scale = 1.0 / np.sqrt(D)
        thetas = jax.random.normal(ks[3], (N_LAYERS, D, D), dtype=jnp.float32) * scale
        phis = jax.random.normal(ks[4], (N_LAYERS, D, D), dtype=jnp.float32) * scale
        gammas = jnp.ones((N_LAYERS, D), dtype=jnp.float32)
        betas = jnp.zeros((N_LAYERS, D), dtype=jnp.float32)
        return {'x': x, 'src': src, 'dst': dst, 'thetas': thetas, 'phis': phis, 'gammas': gammas, 'betas': betas}
    _L3_gnn_all = _L3_gnn_setup()
    _L3_gnn_in = {k: v for k, v in _L3_gnn_all.items() if k in ('thetas', 'phis', 'gammas', 'betas')}
    del _L3_gnn_all
    return {'x': x, 'src': src, 'dst': dst, 'L0_gnn_W1': _L0_gnn_in['W1'], 'L0_gnn_b1': _L0_gnn_in['b1'], 'L0_gnn_W2': _L0_gnn_in['W2'], 'L0_gnn_b2': _L0_gnn_in['b2'], 'L1_gnn_W1': _L1_gnn_in['W1'], 'L1_gnn_b1': _L1_gnn_in['b1'], 'L1_gnn_W2': _L1_gnn_in['W2'], 'L1_gnn_b2': _L1_gnn_in['b2'], 'L1_gnn_a': _L1_gnn_in['a'], 'L2_gnn_W_gcn': _L2_gnn_in['W_gcn'], 'L2_gnn_b_gcn': _L2_gnn_in['b_gcn'], 'L2_gnn_g0': _L2_gnn_in['g0'], 'L2_gnn_beta0': _L2_gnn_in['beta0'], 'L2_gnn_W1': _L2_gnn_in['W1'], 'L2_gnn_a_src1': _L2_gnn_in['a_src1'], 'L2_gnn_a_dst1': _L2_gnn_in['a_dst1'], 'L2_gnn_b1': _L2_gnn_in['b1'], 'L2_gnn_g1': _L2_gnn_in['g1'], 'L2_gnn_beta1': _L2_gnn_in['beta1'], 'L2_gnn_W2': _L2_gnn_in['W2'], 'L2_gnn_a_src2': _L2_gnn_in['a_src2'], 'L2_gnn_a_dst2': _L2_gnn_in['a_dst2'], 'L2_gnn_b2': _L2_gnn_in['b2'], 'L2_gnn_g2': _L2_gnn_in['g2'], 'L2_gnn_beta2': _L2_gnn_in['beta2'], 'L3_gnn_thetas': _L3_gnn_in['thetas'], 'L3_gnn_phis': _L3_gnn_in['phis'], 'L3_gnn_gammas': _L3_gnn_in['gammas'], 'L3_gnn_betas': _L3_gnn_in['betas']}

def reference(x, src, dst, L0_gnn_W1, L0_gnn_b1, L0_gnn_W2, L0_gnn_b2, L1_gnn_W1, L1_gnn_b1, L1_gnn_W2, L1_gnn_b2, L1_gnn_a, L2_gnn_W_gcn, L2_gnn_b_gcn, L2_gnn_g0, L2_gnn_beta0, L2_gnn_W1, L2_gnn_a_src1, L2_gnn_a_dst1, L2_gnn_b1, L2_gnn_g1, L2_gnn_beta1, L2_gnn_W2, L2_gnn_a_src2, L2_gnn_a_dst2, L2_gnn_b2, L2_gnn_g2, L2_gnn_beta2, L3_gnn_thetas, L3_gnn_phis, L3_gnn_gammas, L3_gnn_betas):
    import jax
    import jax.numpy as jnp

    def _L0_gnn_ref(embedding, edge_index, W1, b1, W2, b2):
        import jax, jax.numpy as jnp
        import numpy as np
        N_NODES = 50000

        def gcn_conv(x, W, b, src, dst, n_nodes):
            h = x @ W
            ones = jnp.ones(src.shape[0], dtype=h.dtype)
            deg = jax.ops.segment_sum(ones, dst, num_segments=n_nodes) + 1.0
            dinv = jax.lax.rsqrt(deg)
            norm = dinv[src] * dinv[dst]
            msg = h[src] * norm[:, None]
            agg = jax.ops.segment_sum(msg, dst, num_segments=n_nodes)
            agg = agg + h * (dinv * dinv)[:, None]
            return agg + b
        src, dst = (edge_index[0], edge_index[1])
        n = embedding.shape[0]
        h1 = jax.nn.relu(gcn_conv(embedding, W1, b1, src, dst, n))
        h2 = jax.nn.relu(gcn_conv(h1, W2, b2, src, dst, n))
        return h2

    def _L1_gnn_ref(x, edge_index, W1, b1, W2, b2, a):
        import jax, jax.numpy as jnp
        import numpy as np
        N_NODES = 100000
        F_DIM = 256
        NNZ = 25000

        def _prelu(x, a):
            return jnp.where(x >= 0, x, a * x)

        def _hconv(x, W, b, src, dst, n):
            xt = x @ W
            ones = jnp.ones(src.shape, xt.dtype)
            D = jax.ops.segment_sum(ones, src, num_segments=n)
            B = jax.ops.segment_sum(ones, dst, num_segments=n)
            Dinv = jnp.where(D > 0, 1.0 / D, 0.0)
            Binv = jnp.where(B > 0, 1.0 / B, 0.0)
            m = jax.ops.segment_sum(xt[src], dst, num_segments=n) * Binv[:, None]
            out = jax.ops.segment_sum(m[dst], src, num_segments=n) * Dinv[:, None]
            return out + b
        src, dst = (edge_index[0], edge_index[1])
        n = x.shape[0]
        h = _prelu(_hconv(x, W1, b1, src, dst, n), a)
        h = _hconv(h, W2, b2, src, dst, n) + x
        return _prelu(h, a)

    def _L2_gnn_ref(x, edge_index, W_gcn, b_gcn, g0, beta0, W1, a_src1, a_dst1, b1, g1, beta1, W2, a_src2, a_dst2, b2, g2, beta2):
        import jax, jax.numpy as jnp
        import numpy as np
        N = 100000
        E = 12500
        F_IN = 256
        HID = 64
        H = 4
        NEG_SLOPE = 0.2
        BN_EPS = 1e-05

        def _add_self_loops(edge_index, n):
            loop = jnp.arange(n, dtype=edge_index.dtype)
            src = jnp.concatenate([edge_index[0], loop])
            dst = jnp.concatenate([edge_index[1], loop])
            return (src, dst)

        def _batch_norm(x, g, b):
            m = x.mean(0)
            v = x.var(0)
            return g * (x - m) * jax.lax.rsqrt(v + BN_EPS) + b

        def _gcn_conv(x, src, dst, W, b, n):
            deg = jax.ops.segment_sum(jnp.ones_like(dst, jnp.float32), dst, n)
            dinv = jax.lax.rsqrt(jnp.maximum(deg, 1.0))
            norm = dinv[src] * dinv[dst]
            h = x @ W
            out = jax.ops.segment_sum(h[src] * norm[:, None], dst, n)
            return out + b

        def _gat_conv(x, src, dst, W, a_src, a_dst, b, n):
            h = (x @ W).reshape(n, H, HID)
            alpha_s = jnp.einsum('nhc,hc->nh', h, a_src)
            alpha_d = jnp.einsum('nhc,hc->nh', h, a_dst)
            e = alpha_s[src] + alpha_d[dst]
            e = jnp.where(e > 0, e, NEG_SLOPE * e)
            emax = jax.ops.segment_max(e, dst, n)
            w = jnp.exp(e - emax[dst])
            wsum = jax.ops.segment_sum(w, dst, n)
            att = w / wsum[dst]
            out = jax.ops.segment_sum(att[:, :, None] * h[src], dst, n)
            return out.reshape(n, H * HID) + b
        n = x.shape[0]
        src, dst = _add_self_loops(edge_index, n)
        h = jax.nn.relu(_gcn_conv(x, src, dst, W_gcn, b_gcn, n))
        h = _batch_norm(h, g0, beta0)
        h = _gat_conv(h, src, dst, W1, a_src1, a_dst1, b1, n)
        h = jax.nn.elu(_batch_norm(h, g1, beta1))
        h = _gat_conv(h, src, dst, W2, a_src2, a_dst2, b2, n)
        h = jax.nn.elu(_batch_norm(h, g2, beta2))
        return h

    def _L3_gnn_ref(x, src, dst, thetas, phis, gammas, betas):
        import jax, jax.numpy as jnp
        import numpy as np
        N_NODES = 20000
        N_EDGES = 5000
        D = 256
        N_LAYERS = 3
        BN_EPS = 1e-05
        N = x.shape[0]
        for l in range(thetas.shape[0]):
            xi = x[src]
            xj = x[dst]
            e = jax.nn.relu((xj - xi) @ thetas[l].T + xi @ phis[l].T)
            agg = jax.ops.segment_max(e, src, num_segments=N)
            agg = jnp.where(agg < -1e+30, 0.0, agg)
            mu = agg.mean(axis=0)
            var = agg.var(axis=0)
            x = jax.nn.relu((agg - mu) * jax.lax.rsqrt(var + BN_EPS) * gammas[l] + betas[l])
        return x
    edge_index = jnp.stack([src, dst])
    x = _layernorm(x + _L0_gnn_ref(x, edge_index, L0_gnn_W1, L0_gnn_b1, L0_gnn_W2, L0_gnn_b2), axis=-1)
    x = _layernorm(x + _L1_gnn_ref(x, edge_index, L1_gnn_W1, L1_gnn_b1, L1_gnn_W2, L1_gnn_b2, L1_gnn_a), axis=-1)
    x = _layernorm(x + _L2_gnn_ref(x, edge_index, L2_gnn_W_gcn, L2_gnn_b_gcn, L2_gnn_g0, L2_gnn_beta0, L2_gnn_W1, L2_gnn_a_src1, L2_gnn_a_dst1, L2_gnn_b1, L2_gnn_g1, L2_gnn_beta1, L2_gnn_W2, L2_gnn_a_src2, L2_gnn_a_dst2, L2_gnn_b2, L2_gnn_g2, L2_gnn_beta2), axis=-1)
    x = _layernorm(x + _L3_gnn_ref(x, src, dst, L3_gnn_thetas, L3_gnn_phis, L3_gnn_gammas, L3_gnn_betas), axis=-1)
    return x

_drawn_inputs = setup_inputs


def setup_inputs(seed=0):
    import zlib

    import numpy as np

    out = dict(_drawn_inputs(seed))
    spreads = {'L0_gnn_b1': (0.0, 0.1),
     'L0_gnn_b2': (0.0, 0.1),
     'L1_gnn_b1': (0.0, 0.1),
     'L1_gnn_b2': (0.0, 0.1),
     'L2_gnn_b_gcn': (0.0, 0.1),
     'L2_gnn_g0': (1.0, 0.2),
     'L2_gnn_beta0': (0.0, 2.0),
     'L2_gnn_b1': (0.0, 2.0),
     'L2_gnn_g1': (1.0, 0.2),
     'L2_gnn_beta1': (0.0, 0.29),
     'L2_gnn_b2': (0.0, 2.0),
     'L2_gnn_g2': (1.0, 0.2),
     'L2_gnn_beta2': (0.0, 0.1),
     'L3_gnn_gammas': (1.0, 0.2),
     'L3_gnn_betas': (0.0, 0.1)}
    factors = {'L2_gnn_a_src1': 6.738, 'L2_gnn_a_dst1': 21.469, 'L2_gnn_a_dst2': 30.007}
    for name, (base, spread) in spreads.items():
        noise = np.random.default_rng([zlib.crc32(name.encode()), seed]).standard_normal(out[name].shape)
        drawn = base * np.exp(spread * noise) if base else spread * noise
        out[name] = jnp.asarray(drawn.astype(out[name].dtype))
    for name, factor in factors.items():
        out[name] = (out[name] * factor).astype(out[name].dtype)
    return out
```

```python
from contextlib import ExitStack, contextmanager

import concourse.bass as bass
from concourse import mybir
from concourse.alu_op_type import AluOpType as ALU

F32 = mybir.dt.float32
I32 = mybir.dt.int32
ACT = mybir.ActivationFunctionType

P = 128
N = 50000
E = 25000
D = 256
T = 196
B = 14
STEPS = T // B
HALF = B // 2
ROWS = T * P
HID = 64
HEADS = 4
J = 3
GROUP = P * J
PAIRS = N // (2 * GROUP)
TAIL = N - PAIRS * 2 * GROUP
PADKEY = 50175
SKIP = 100000
NEG = -1.0e30
EPS = 1e-5
RADIX = 256


def wait(eng, sem, value):
    if isinstance(value, int) and value <= 0:
        return
    eng.wait_ge(sem, value)


class Chain:

    def __init__(self, eng, sem, gate=None):
        self.eng, self.sem, self.gate, self.base, self.n = eng, sem, gate, 0, 0

    def __call__(self, ins):
        self.n += 1
        ins.then_inc(self.sem, 1)
        self.eng.wait_ge(self.sem, self.base + self.n)

    def mark(self, ins):
        self.n += 1
        ins.then_inc(self.sem, 1)

    def sync(self):
        self.eng.wait_ge(self.sem, self.base + self.n)


def steps(eng, count, body, chain=None):
    n0 = chain.n if chain else 0
    assert not chain or isinstance(chain.base, int)
    body(0)
    if chain:
        per, start = chain.n - n0, chain.base + n0
    with eng.Fori(1, count) as i:
        if chain:
            chain.base, chain.n = i * per + start, 0
        body(i)
        assert not chain or chain.n == per
    if chain:
        chain.base, chain.n = start + count * per, 0


class Sems:

    def __init__(self, nc, ctx, tag):
        self.nc, self.ctx, self.tag, self.all = nc, ctx, tag, []

    def __call__(self, name):
        s = self.ctx.enter_context(self.nc.semaphore(f"{self.tag}_{name}"))
        self.all.append(s)
        return s

    def many(self, name, n):
        return [self(f"{name}{i}") for i in range(n)]


@contextmanager
def phase(nc, tag):
    with ExitStack() as ctx:
        sems = Sems(nc, ctx, tag)

        def sb(name, shape, dt=F32):
            return ctx.enter_context(nc.sbuf_tensor(f"{tag}_{name}", shape, dt))

        def ps(name, shape):
            return ctx.enter_context(nc.psum_tensor(f"{tag}_{name}", shape, F32))

        yield sems, sb, ps
        nc.all_engine_barrier()
        nc.gpsimd.dma_reset()
        for s in sems.all:
            nc.gpsimd.sem_clear(s)
        nc.all_engine_barrier()


def columns(eng, stages, chain=None, per=0):
    def body(i):
        for b in range(B):
            for fn, lag in stages:
                if b >= lag:
                    fn(i, b - lag)
                elif not (isinstance(i, int) and i == 0):
                    fn(i - 1, b - lag + B)

    peel = 2 if max(lag for _, lag in stages) else 1
    for i in range(peel):
        body(i)
    start = (chain.base + chain.n) if chain else 0
    with eng.Fori(peel, STEPS) as i:
        if chain:
            chain.base, chain.n = (i - peel) * per + start, 0
        body(i)
        assert not chain or chain.n == per, chain.n
    if chain:
        chain.base, chain.n = start + (STEPS - peel) * per, 0
    for x in range(max(lag for _, lag in stages)):
        for fn, lag in stages:
            if lag > x:
                fn(STEPS - 1, B - lag + x)


def pairs(eng, stages, chain=None, per=0):
    def step(i, s):
        for fn, lag in stages:
            if lag == 0:
                fn(i, s, P, J)
            elif s == 1:
                fn(i, 0, P, J)
            elif not (isinstance(i, int) and i == 0):
                fn(i - 1, 1, P, J)

    peel = 2 if max(lag for _, lag in stages) else 1
    for i in range(peel):
        step(i, 0)
        step(i, 1)
    start = (chain.base + chain.n) if chain else 0
    with eng.Fori(peel, PAIRS) as i:
        if chain:
            chain.base, chain.n = (i - peel) * per + start, 0
        step(i, 0)
        step(i, 1)
        assert not chain or chain.n == per, chain.n
    if chain:
        chain.base, chain.n = start + (PAIRS - peel) * per, 0
    for fn, lag in stages:
        if lag == 0:
            fn(PAIRS, 0, TAIL, 1)
        else:
            fn(PAIRS - 1, 1, P, J)
    for fn, lag in stages:
        if lag:
            fn(PAIRS, 0, TAIL, 1)


def group(table, i, s, p, j):
    if p == TAIL:
        return table[2 * PAIRS * GROUP:N, :].rearrange("(p j) c -> p j c", j=1)
    return table[bass.ds(i * (2 * GROUP) + s * GROUP, GROUP), :].rearrange("(p j) c -> p j c", j=J)


def settle(eng, gate):
    eng.sem_inc(gate, 1)


class Feed:

    def __init__(self, pool, gate, sem, slots, source, done):
        self.pool, self.sem, self.slots, self.source, self.done = pool, sem, slots, source, done
        self.gate = gate

    def __call__(self, i, h):
        lo, hi = h * HALF, (h + 1) * HALF
        for b in range(lo, hi):
            wait(self.pool, self.done[b], i * 16)
        settle(self.pool, self.gate)
        self.pool.tensor_copy(self.slots[:, lo:hi], self.source[:, bass.ds(i * B + lo, HALF)]).then_inc(self.sem, 1)
        self.pool.wait_ge(self.sem, i * 2 + (h + 1))

    def at(self, b):
        settle(self.pool, self.gate)
        return bass.IndirectOffsetOnAxis(self.slots[:, b:b + 1], 0)


def indexed(pool, gather=None, gather_feeds=(), scatter=None, scatter_feeds=()):
    def half(i, h, j, k):
        for f in gather_feeds:
            f(i, h)
        if j is not None:
            for f in scatter_feeds:
                f(j, k)
        for b in range(HALF):
            if gather:
                gather(i, h * HALF + b)
            if j is not None:
                scatter(j, k * HALF + b)

    def body(i):
        if scatter:
            first = isinstance(i, int)
            half(i, 0, None if first else i - 1, 1)
            half(i, 1, i, 0)
        else:
            half(i, 0, None, 0)
            half(i, 1, None, 0)

    steps(pool, STEPS, body)
    if scatter:
        for f in scatter_feeds:
            f(STEPS - 1, 1)
        for b in range(HALF, B):
            scatter(STEPS - 1, b)


def rstd_steps(chain, v, y, t, u):
    dve = chain.eng
    chain(dve.tensor_scalar(t.bitcast(I32), v.bitcast(I32), 1, None, ALU.logical_shift_right))
    chain(dve.tensor_scalar(y.bitcast(I32), t.bitcast(I32), -1.0, float(0x5F3759DF), ALU.mult, ALU.add))
    for _ in range(3):
        chain(dve.tensor_tensor(t, y, y, ALU.mult))
        chain(dve.scalar_tensor_tensor(u, t, -0.5, v, ALU.mult, ALU.mult))
        chain(dve.scalar_tensor_tensor(y, u, 1.5, y, ALU.add, ALU.mult))


def layer_norm(chain, x, y, st, p, j):
    dve = chain.eng
    for k in range(j):
        chain.mark(dve.bn_stats(st["part"][0:p, k, :], x[0:p, k, :]))
    chain.sync()
    settle(dve, chain.gate)
    for k in range(j):
        chain.mark(dve.bn_aggr(st["mean"][0:p, k, :], st["part"][0:p, k, :]))
    chain.sync()
    chain(dve.tensor_scalar(st["var"][0:p, 0:j], st["mean"][0:p, 0:j, 1], EPS, None, ALU.add))
    rstd_steps(chain, st["var"][0:p, 0:j], st["rstd"][0:p, 0:j], st["t"][0:p, 0:j], st["u"][0:p, 0:j])
    for k in range(j):
        chain.mark(dve.tensor_scalar(y[0:p, k, :], x[0:p, k, :], st["mean"][0:p, k, 0:1], st["rstd"][0:p, k:k + 1], ALU.subtract, ALU.mult))
    chain.sync()


def norm_buffers(sb, j):
    return {"part": sb("part", [P, j, 6]), "mean": sb("mean", [P, j, 2]), "var": sb("var", [P, j]),
            "rstd": sb("rstd", [P, j]), "t": sb("nt", [P, j]), "u": sb("nu", [P, j])}


def program(nc, a, out):
    with ExitStack() as ctx:
        def sb(name, shape, dt=F32):
            return ctx.enter_context(nc.sbuf_tensor(name, shape, dt))

        def dram(name, shape, dt=F32):
            return nc.dram_tensor(name, shape, dt).ap()

        nt = dram("node_counts", (2 * N, 2))
        dm = dram("node_scale", (N, 2))
        srt = {o: [dram(f"sorted_{o}{k}", (ROWS + 2, 2), I32) for k in range(2)] for o in "ds"}

        iota = sb("iota", [P, RADIX])
        pcol = sb("pcol", [P, 1])
        ident = sb("ident", [P, P])
        below = sb("below", [P, P])
        ones = sb("ones", [P, P])
        zeros = sb("zeros", [P, 2 * D])

        agg = [dram(f"agg{k}", (N, HID)) for k in range(3)]
        with phase(nc, "init") as (sem, _, _):
            made, zeroed, stored = sem("made"), sem("zeroed"), sem("stored")
            gate = sem("gate")
            with nc.Block() as block:
                @block.gpsimd
                def _(pool):
                    pool.iota(iota[:], [[1, RADIX]], 0, 0, allow_small_or_imprecise_dtypes=True).then_inc(made, 1)
                    pool.iota(pcol[:], [[0, 1]], 0, 1, allow_small_or_imprecise_dtypes=True).then_inc(made, 1)
                    pool.wait_ge(made, 2)

                @block.vector
                def _(dve):
                    dve.memset(zeros[:], 0.0).then_inc(zeroed, 1)
                    dve.memset(ones[:], 1.0).then_inc(zeroed, 1)
                    dve.wait_ge(made, 2)
                    dve.tensor_scalar(ident[:], iota[:, 0:P], pcol[:], None, ALU.is_equal).then_inc(zeroed, 1)
                    dve.tensor_scalar(below[:], iota[:, 0:P], pcol[:], None, ALU.is_gt).then_inc(zeroed, 1)
                    dve.wait_ge(zeroed, 4)

                @block.sync
                def _(sp):
                    sp.wait_ge(zeroed, 1)
                    for table in agg:
                        rows = table.rearrange("(p r) c -> p r c", p=80)
                        sp.dma_start(rows, zeros[0:80, 0:HID].unsqueeze(1).to_broadcast([80, N // 80, HID])).then_inc(stored, 16)
                    rows = nt.rearrange("(p r) c -> p (r c)", p=80)
                    for k in range(0, 4 * N // 80, 500):
                        sp.dma_start(rows[:, k:k + 500], zeros[0:80, 0:500]).then_inc(stored, 16)
                    sp.wait_ge(stored, 16 * 8)

        def radix_pass(o, k):
            with phase(nc, f"sort_{o}{k}") as (sem, sb, ps):
                kv = sb("kv", [P, T, 2], I32)
                raw = sb("raw", [P, 2, T], I32)
                digit_i = sb("digit_i", [P, T], I32)
                digit = sb("digit", [P, T])
                seen = sb("seen", [P, 2, RADIX])
                total = sb("total", [P, RADIX])
                start = sb("start", [P, RADIX + 1])
                junk = sb("junk", [P, RADIX])
                place = sb("place", [P, B])
                place_i = sb("place_i", [P, B], I32)
                row = sb("row", [P, B, 2], I32)
                edge = sb("edge", [P, 2], I32)
                p_before = ps("before", [P, RADIX])
                p_total = ps("total_ps", [P, RADIX])
                loaded, own, counted, summed = sem("loaded"), sem("own"), sem("counted"), sem("summed")
                ranked, padded = sem("ranked"), sem("padded")
                placed = sem.many("placed", B)
                target = srt[o][k]
                key, other = ("dst", "src") if o == "d" else ("src", "dst")
                whole, rest = E // T, E % T

                gate = sem("gate")
                with nc.Block() as block:
                    @block.sync
                    def _(sp):
                        if k == 0:
                            sp.wait_ge(padded, 1)
                            for c, name in enumerate((key, other)):
                                sp.dma_start(raw[0:whole, c, :], a[name][0:whole * T].rearrange("(p t) -> p t", t=T)).then_inc(loaded, 16)
                                sp.dma_start(raw[whole:whole + 1, c, 0:rest], a[name][whole * T:E].rearrange("(p t) -> p t", p=1)).then_inc(loaded, 16)
                        else:
                            sp.dma_start(kv[:], srt[o][0][1:ROWS + 1, :].rearrange("(p t) c -> p t c", t=T)).then_inc(loaded, 16)
                            sp.wait_ge(padded, 1)
                            sp.dma_start(target[0:1, :], edge[0:1, :]).then_inc(loaded, 16)
                            sp.dma_start(target[ROWS + 1:ROWS + 2, :], edge[0:1, :]).then_inc(loaded, 16)
                            sp.wait_ge(loaded, 48)

                    @block.vector
                    def _(dve):
                        own_ = Chain(dve, own, gate)
                        if k == 0:
                            own_(dve.memset(raw[:, 1, :], 0))
                            dve.memset(raw[:, 0, :], PADKEY).then_inc(padded, 1)
                            dve.wait_ge(loaded, 64)
                            own_(dve.tensor_copy(kv[:, :, 0], raw[:, 0, :]))
                            own_(dve.tensor_copy(kv[:, :, 1], raw[:, 1, :]))
                            own_(dve.tensor_scalar(digit_i[:], kv[:, :, 0], RADIX - 1, None, ALU.bitwise_and))
                        else:
                            dve.memset(edge[:], -1).then_inc(padded, 1)
                            dve.wait_ge(loaded, 16)
                            if k == 1:
                                dve.wait_ge(loaded, 48)
                            own_(dve.tensor_scalar(digit_i[:], kv[:, :, 0], 8, None, ALU.logical_shift_right))
                        own_(dve.tensor_copy(digit[:], digit_i[:]))
                        own_(dve.memset(seen[:], 0.0))

                        def count(i):
                            for b in range(B):
                                d = digit[:, bass.ds(i * B + b, 1)]
                                own_(dve.scalar_tensor_tensor(seen[:, 1 - b % 2, :], iota[:], d, seen[:, b % 2, :], ALU.is_equal, ALU.add))

                        steps(dve, STEPS, count, own_)
                        dve.sem_inc(counted, 1)
                        dve.wait_ge(summed, 1)
                        own_(dve.memset(start[:, 0:1], 0.0))
                        own_(dve.tensor_copy(total[:], p_total[:]))
                        own_(dve.tensor_tensor_scan(start[:, 1:RADIX + 1], ones[:, 0:1].to_broadcast([P, RADIX]), total[:], 0.0, ALU.mult, ALU.add))
                        own_(dve.scalar_tensor_tensor(seen[:, 0, :], start[:, 0:RADIX], 1.0, p_before[:], ALU.add, ALU.add))

                        def rank(i):
                            for b in range(B):
                                t = i * B + b
                                d = digit[:, bass.ds(t, 1)]
                                own_.mark(dve.scalar_tensor_tensor(junk[:], iota[:], d, seen[:, b % 2, :], ALU.is_equal, ALU.mult, accum_out=place[:, b:b + 1]))
                                own_(dve.scalar_tensor_tensor(seen[:, 1 - b % 2, :], iota[:], d, seen[:, b % 2, :], ALU.is_equal, ALU.add))
                                wait(dve, placed[b], i * 16)
                                own_.mark(dve.tensor_copy(row[:, b, :], kv[:, bass.ds(t, 1), :].rearrange("p a c -> p (a c)")))
                                dve.tensor_copy(place_i[:, b:b + 1], place[:, b:b + 1]).then_inc(ranked, 1)
                                own_.sync()

                        steps(dve, STEPS, rank, own_)

                    @block.tensor
                    def _(pe):
                        pe.wait_ge(counted, 1)
                        pe.matmul(p_before[:], below[:], seen[:, 0, :], start=True, stop=True)
                        pe.matmul(p_total[:], ones[:], seen[:, 0, :], start=True, stop=True).then_inc(summed, 1)

                    @block.gpsimd
                    def _(pool):
                        last_row = pool.to_reg(ROWS)

                        def scatter(i):
                            for b in range(B):
                                pool.wait_ge(ranked, i * B + (b + 1))
                                settle(pool, gate)
                                pool.indirect_dma_start(target, bass.IndirectOffsetOnAxis(place_i[:, b:b + 1], 0), row[:, b, :], None,
                                                        bounds_check=last_row, oob_is_err=False).then_inc(placed[b], 16)

                        steps(pool, STEPS, scatter)
                        for s in placed:
                            pool.wait_ge(s, 16 * STEPS)

        for o in "ds":
            for k in range(2):
                radix_pass(o, k)

        def structure(o):
            g = {}
            for n in ("cont", "pen", "rpen", "endm", "count", "inverse"):
                g[n] = sb(f"{n}_{o}", [P, T])
            for n in ("node", "other", "put"):
                g[n] = sb(f"{n}_{o}", [P, T], I32)
            g["whole"] = sb(f"whole_{o}", [P, 2])
            g["carry"] = sb(f"carry_{o}", [P, P])
            g["fix_row"] = sb(f"fix_row_{o}", [P, 1], I32)
            g["fix_node"] = sb(f"fix_node_{o}", [P, 1], I32)
            g["inner"] = sb(f"inner_{o}", [P, T])
            with phase(nc, f"runs_{o}") as (sem, sb_, ps):
                kv = sb_("kv", [P, 3, T, 2], I32)
                at = sb_("at", [P, 3, T])
                same_next = sb_("same_next", [P, T])
                row = sb_("row", [P, T])
                real = sb_("real", [P, T])
                off = sb_("off", [P, T])
                raw = sb_("raw", [P, T])
                small = sb_("small", [P, 8])
                diag = sb_("diag", [P, P])
                put2 = sb_("put2", [P, T], I32)
                pair = sb_("pair", [P, T, 2])
                idx = sb_("idx", [P, B], I32)
                slot = sb_("slot", [P, B, 2])
                p_first = ps("first", [P, P])
                p_carry = ps("carry", [P, 1])
                loaded, own, rows_made = sem("loaded"), sem("own"), sem("rows_made")
                diag_made, first_made, scanned, carried = sem("diag_made"), sem("first_made"), sem("scanned"), sem("carried")
                ready, fed = sem("ready"), sem("fed")
                put_done = sem.many("put_done", B)
                gate = sem("gate")
                with nc.Block() as block:
                    @block.sync
                    def _(sp):
                        for c in range(3):
                            sp.dma_start(kv[:, c], srt[o][1][c:ROWS + c, :].rearrange("(p t) c -> p t c", t=T)).then_inc(loaded, 16)

                    @block.tensor
                    def _(pe):
                        pe.wait_ge(diag_made, 1)
                        pe.matmul(p_first[:], ones[:], diag[:], start=True, stop=True).then_inc(first_made, 1)
                        pe.wait_ge(scanned, 1)
                        pe.matmul(p_carry[:], g["carry"][:], raw[:, T - 1:T], start=True, stop=True).then_inc(carried, 1)

                    @block.vector
                    def _(dve):
                        c_ = Chain(dve, own, gate)
                        dve.wait_ge(loaded, 48)
                        dve.wait_ge(rows_made, 1)
                        for c in range(3):
                            c_(dve.tensor_copy(at[:, c, :], kv[:, c, :, 0]))
                        before, key, after = (at[:, c, :] for c in range(3))
                        c_(dve.tensor_tensor(g["cont"][:], before, key, ALU.is_equal))
                        c_(dve.tensor_tensor(same_next[:], after, key, ALU.is_equal))
                        c_(dve.tensor_scalar(real[:], key, float(N), None, ALU.is_lt))
                        c_(dve.tensor_scalar(off[:], same_next[:], -1.0, 1.0, ALU.mult, ALU.add))
                        c_(dve.tensor_tensor(g["endm"][:], off[:], real[:], ALU.mult))
                        c_(dve.tensor_scalar(g["pen"][:], g["cont"][:], -1.0, -NEG, ALU.add, ALU.mult))
                        c_(dve.tensor_scalar(g["rpen"][:], same_next[:], -1.0, -NEG, ALU.add, ALU.mult))
                        c_(dve.tensor_scalar(off[:], g["endm"][:], -float(SKIP), float(SKIP), ALU.mult, ALU.add))
                        c_(dve.tensor_tensor(real[:], key, off[:], ALU.add))
                        c_(dve.tensor_copy(g["put"][:], real[:]))
                        c_(dve.tensor_scalar(raw[:], real[:], 2.0, 0.0 if o == "d" else 1.0, ALU.mult, ALU.add))
                        c_(dve.tensor_copy(put2[:], raw[:]))
                        c_(dve.tensor_scalar(raw[:], key, float(N - 1), None, ALU.min))
                        c_(dve.tensor_copy(g["node"][:], raw[:]))
                        c_(dve.tensor_copy(g["other"][:], kv[:, 1, :, 1]))
                        c_(dve.tensor_reduce(small[:, 0:1], real[:], mybir.AxisListType.X, ALU.min))
                        c_(dve.tensor_tensor(real[:], row[:], off[:], ALU.add))
                        c_(dve.tensor_reduce(small[:, 1:2], real[:], mybir.AxisListType.X, ALU.min))
                        c_(dve.tensor_scalar(small[:, 2:3], g["cont"][:, 0:1], -float(SKIP), float(SKIP), ALU.mult, ALU.add))
                        c_(dve.tensor_tensor(small[:, 0:1], small[:, 0:1], small[:, 2:3], ALU.add))
                        c_(dve.tensor_tensor(small[:, 1:2], small[:, 1:2], small[:, 2:3], ALU.add))
                        c_(dve.tensor_copy(g["fix_node"][:], small[:, 0:1]))
                        c_(dve.tensor_copy(g["fix_row"][:], small[:, 1:2]))
                        c_(dve.tensor_scalar(real[:], row[:], small[:, 1:2], None, ALU.not_equal))
                        c_(dve.tensor_tensor(g["inner"][:], real[:], g["endm"][:], ALU.mult))
                        c_(dve.tensor_reduce(small[:, 3:4], g["cont"][:], mybir.AxisListType.X, ALU.min))
                        c_(dve.tensor_reduce(small[:, 4:5], same_next[:], mybir.AxisListType.X, ALU.min))
                        c_(dve.tensor_scalar(g["whole"][:], small[:, 3:5], -1.0, -NEG, ALU.add, ALU.mult))
                        dve.tensor_scalar(diag[:], ident[:], key[:, 0:1], None, ALU.mult).then_inc(diag_made, 1)
                        dve.wait_ge(first_made, 1)
                        c_(dve.scalar_tensor_tensor(g["carry"][:], p_first[:], key[:, T - 1:T], below[:], ALU.is_equal, ALU.mult))
                        one = ones[:, 0:1].to_broadcast([P, T])
                        dve.tensor_tensor_scan(raw[:], g["cont"][:], one, 0.0, ALU.mult, ALU.add).then_inc(scanned, 1)
                        dve.wait_ge(carried, 1)
                        c_(dve.tensor_copy(small[:, 5:6], p_carry[:]))
                        c_(dve.tensor_tensor_scan(g["count"][:], g["cont"][:], one, small[:, 5:6], ALU.mult, ALU.add))
                        c_(dve.reciprocal(g["inverse"][:], g["count"][:]))
                        c_(dve.tensor_copy(pair[:, :, 0], g["count"][:]))
                        c_(dve.tensor_copy(pair[:, :, 1], row[:]))
                        dve.sem_inc(ready, 1)

                    @block.gpsimd
                    def _(pool):
                        pool.iota(row[:], [[P, T]], 0, 1, allow_small_or_imprecise_dtypes=True).then_inc(rows_made, 1)
                        last = pool.to_reg(2 * N - 1)
                        pool.wait_ge(ready, 1)

                        def scatter(i):
                            for h in range(2):
                                lo, hi = h * HALF, (h + 1) * HALF
                                for b in range(lo, hi):
                                    wait(pool, put_done[b], i * 16)
                                pool.tensor_copy(idx[:, lo:hi], put2[:, bass.ds(i * B + lo, HALF)]).then_inc(fed, 1)
                                pool.tensor_copy(slot[:, lo:hi, :], pair[:, bass.ds(i * B + lo, HALF), :]).then_inc(fed, 1)
                                pool.wait_ge(fed, i * 4 + (2 * h + 2))
                                settle(pool, gate)
                                for b in range(lo, hi):
                                    pool.indirect_dma_start(nt, bass.IndirectOffsetOnAxis(idx[:, b:b + 1], 0), slot[:, b, :], None,
                                                            bounds_check=last, oob_is_err=False).then_inc(put_done[b], 16)

                        steps(pool, STEPS, scatter)
                        for s in put_done:
                            pool.wait_ge(s, 16 * STEPS)
            return g

        runs = {o: structure(o) for o in "ds"}

        nt4 = nt.rearrange("(n two) c -> n (two c)", two=2)

        def small_rows(tag, table, rows, width, jobs):
            with phase(nc, tag) as (sem, sb_, ps):
                n = len(jobs)
                slot = [sb_(f"slot{k}", [P, B, width]) for k in range(n)]
                idx = [sb_(f"idx{k}", [P, B], I32) for k in range(n)]
                fed = sem.many("fed", n)
                got = [sem.many(f"got{k}_", B) for k in range(n)]
                taken = sem("taken")
                gate = sem("gate")
                with nc.Block() as block:
                    @block.gpsimd
                    def _(pool):
                        last = pool.to_reg(rows - 1)
                        feeds = [Feed(pool, gate, fed[k], idx[k], jobs[k][0], got[k]) for k in range(n)]

                        def gather(i, b):
                            wait(pool, taken, (i * B + (b + 1 - B)) * n)
                            for k in range(n):
                                pool.indirect_dma_start(slot[k][:, b, :], None, table, feeds[k].at(b),
                                                        bounds_check=last, oob_is_err=False).then_inc(got[k][b], 16)

                        indexed(pool, gather, feeds)

                    @block.vector
                    def _(dve):
                        def take(i):
                            for b in range(B):
                                for k in range(n):
                                    dve.wait_ge(got[k][b], i * 16 + 16)
                                    dve.tensor_copy(jobs[k][1][:, bass.ds(i * B + b, 1), :].rearrange("p a c -> p (a c)"),
                                                    slot[k][:, b, :]).then_inc(taken, 1)

                        steps(dve, STEPS, take)
                        dve.wait_ge(taken, T * n)

        inv_other = {o: sb(f"inv_other_{o}", [P, T]) for o in "ds"}
        to_out_row = sb("to_out_row", [P, T], I32)
        to_in_row = sb("to_in_row", [P, T], I32)
        other_row = sb("other_row", [P, T], I32)
        own_row = sb("own_row", [P, T], I32)
        rs_other = sb("rs_other", [P, T])
        with ExitStack() as told_ctx:
            told = {k: told_ctx.enter_context(nc.sbuf_tensor(f"told_{k}", [P, T, 4], F32)) for k in ("d", "s", "own")}
            small_rows("ends_d", nt4, N, 4, [(runs["d"]["other"], told["d"])])
            small_rows("ends_s", nt4, N, 4, [(runs["s"]["other"], told["s"]), (runs["s"]["node"], told["own"])])
            with phase(nc, "scales") as (sem, sb_, ps):
                q, per = 125, N // 125
                counts = sb_("counts", [q, per, 4])
                both = sb_("both", [q, per, 2])
                deg = sb_("deg", [q, per])
                y, t1, t2 = (sb_(n, [q, per]) for n in ("y", "t1", "t2"))
                e0, e1, e2 = (sb_(n, [P, T]) for n in ("e0", "e1", "e2"))
                loaded, own, ready, stored = sem("loaded"), sem("own"), sem("ready"), sem("stored")
                gate = sem("gate")
                with nc.Block() as block:
                    @block.sync
                    def _(sp):
                        sp.dma_start(counts[:], nt4.rearrange("(p r) c -> p r c", p=q)).then_inc(loaded, 16)
                        sp.wait_ge(ready, 1)
                        sp.dma_start(dm.rearrange("(p r) c -> p r c", p=q), both[:]).then_inc(stored, 16)
                        sp.wait_ge(stored, 16)

                    @block.vector
                    def _(dve):
                        c_ = Chain(dve, own, gate)
                        dve.wait_ge(loaded, 16)
                        c_(dve.tensor_scalar(deg[:], counts[:, :, 0], 1.0, None, ALU.add))
                        rstd_steps(c_, deg[:], y[:], t1[:], t2[:])
                        c_(dve.tensor_copy(both[:, :, 0], y[:]))
                        dve.tensor_scalar(both[:, :, 1], counts[:, :, 0], 0.0, None, ALU.is_equal).then_inc(ready, 1)
                        c_(dve.tensor_scalar(e0[:], told["d"][:, :, 0], 1.0, None, ALU.add))
                        rstd_steps(c_, e0[:], rs_other[:], e1[:], e2[:])
                        c_(dve.tensor_scalar(e0[:], told["d"][:, :, 2], 1.0, None, ALU.max))
                        c_(dve.reciprocal(inv_other["d"][:], e0[:]))
                        c_(dve.tensor_scalar(e0[:], told["s"][:, :, 0], 1.0, None, ALU.max))
                        c_(dve.reciprocal(inv_other["s"][:], e0[:]))
                        c_(dve.tensor_copy(to_out_row[:], told["d"][:, :, 3]))
                        c_(dve.tensor_copy(to_in_row[:], told["s"][:, :, 1]))
                        c_(dve.tensor_copy(own_row[:], told["own"][:, :, 3]))
                        c_(dve.tensor_scalar(e0[:], told["s"][:, :, 2], 0.0, float(ROWS), ALU.is_equal, ALU.mult))
                        c_(dve.tensor_tensor(e1[:], e0[:], told["s"][:, :, 3], ALU.add))
                        c_(dve.tensor_copy(other_row[:], e1[:]))
                        dve.wait_ge(ready, 1)

        def row_of(name, width=D):
            return sb(f"row_{name}", [P, width])

        w = {"a1": sb("w_a1", [P, 2, HID]), "a2": sb("w_a2", [HID, D]), "b1": sb("w_b1", [P, 2, D]),
             "b2": sb("w_b2", [P, 2, D]), "g": sb("w_g", [P, 2, HID])}
        bias = {"a1": row_of("a1", HID), "a2": row_of("a2"), "b1": row_of("b1"), "b2": row_of("b2"), "g": row_of("g", HID)}
        slope = sb("slope", [P, 1])
        fall = sb("fall", [P, 1])
        minus_fall = sb("minus_fall", [P, 1])
        with phase(nc, "weights") as (sem, sb_, ps):
            loaded, own = sem("loaded"), sem("own")
            gate = sem("gate")
            with nc.Block() as block:
                @block.sync
                def _(sp):
                    jobs = [(w["a1"][:], a["L0_gnn_W1"].rearrange("(c p) n -> p c n", p=P)), (w["a2"][:], a["L0_gnn_W2"]),
                            (w["b1"][:], a["L1_gnn_W1"].rearrange("(c p) n -> p c n", p=P)),
                            (w["b2"][:], a["L1_gnn_W2"].rearrange("(c p) n -> p c n", p=P)),
                            (w["g"][:], a["L2_gnn_W_gcn"].rearrange("(c p) n -> p c n", p=P)),
                            (slope[:], a["L1_gnn_a"].rearrange("(o n) -> o n", o=1).to_broadcast([P, 1]))]
                    for k, name in (("a1", "L0_gnn_b1"), ("a2", "L0_gnn_b2"), ("b1", "L1_gnn_b1"), ("b2", "L1_gnn_b2"), ("g", "L2_gnn_b_gcn")):
                        width = bias[k].shape[1]
                        jobs.append((bias[k][:], a[name].rearrange("(o n) -> o n", o=1).to_broadcast([P, width])))
                    for target, source in jobs:
                        sp.dma_start(target, source).then_inc(loaded, 16)
                    sp.wait_ge(loaded, 16 * len(jobs))

                @block.vector
                def _(dve):
                    dve.wait_ge(loaded, 16 * 11)
                    dve.tensor_scalar(fall[:], slope[:], -1.0, 1.0, ALU.mult, ALU.add).then_inc(own, 1)
                    dve.wait_ge(own, 1)
                    dve.tensor_scalar(minus_fall[:], fall[:], -1.0, None, ALU.mult).then_inc(own, 1)
                    dve.wait_ge(own, 2)

        def edge_sum(tag, o, table, rows, index, width, target, by_node, scale=None, weights=None, net=None):
            g = runs[o]
            out_w = D if weights is not None else width
            if net is not None:
                layer, bias_row = net
            with phase(nc, tag) as (sem, sb_, ps):
                got_rows = sb_("got_rows", [P, B, width])
                scaled = sb_("scaled", [P, B, out_w]) if scale is not None or weights is not None else got_rows
                if net is not None:
                    xt = sb_("xt", [P, B, 2, P])
                    y = sb_("y", [P, B, D])
                    neg = sb_("neg", [P, B, D])
                    p_t = [ps(f"t{k}", [P, 2, P]) for k in range(2)]
                    p_y = [ps(f"y{k}", [P, 512]) for k in range(2)]
                    turned, evac, product, layered, lowered = sem("turned"), sem("evac"), sem("product"), sem("layered"), sem("lowered")
                total = sb_("total", [P, B, out_w])
                idx = sb_("idx", [P, B], I32)
                put = sb_("put", [P, B], I32)
                fix = sb_("fix", [P, out_w])
                fixed = sb_("fixed", [P, out_w])
                p_carry = ps("carry", [P, out_w])
                got, stored = sem.many("got", B), sem.many("stored", B)
                fed, fed_put, made, summed, own = sem("fed"), sem("fed_put"), sem("made"), sem("summed"), sem("own")
                carried, fix_got, fix_ready, blank = sem("carried"), sem("fix_got"), sem("fix_ready"), sem("blank")
                target_rows = N if by_node else ROWS
                gate = sem("gate")
                with nc.Block() as block:
                    @block.gpsimd
                    def _(pool):
                        last = pool.to_reg(rows - 1)
                        last_out = pool.to_reg(target_rows - 1)
                        feed = Feed(pool, gate, fed, idx, index, got)
                        feed_put = Feed(pool, gate, fed_put, put, g["put"], stored)
                        used = turned if net is not None else made if scaled is not got_rows else summed

                        def gather(i, b):
                            wait(pool, used, i * B + (b + 1 - B))
                            pool.indirect_dma_start(got_rows[:, b, :], None, table, feed.at(b),
                                                    bounds_check=last, oob_is_err=False).then_inc(got[b], 16)

                        def scatter(i, b):
                            pool.wait_ge(summed, i * B + (b + 1))
                            pool.indirect_dma_start(target, feed_put.at(b), total[:, b, :], None,
                                                    bounds_check=last_out, oob_is_err=False).then_inc(stored[b], 16)

                        if by_node:
                            indexed(pool, gather, [feed], scatter, [feed_put])
                        else:
                            indexed(pool, gather, [feed])
                        for s in stored:
                            pool.wait_ge(s, 16 * STEPS)
                        pool.wait_ge(blank, 1)
                        at = bass.IndirectOffsetOnAxis(g["fix_node" if by_node else "fix_row"][:, 0:1], 0)
                        pool.indirect_dma_start(fix[:], None, target, at, bounds_check=last_out, oob_is_err=False).then_inc(fix_got, 16)
                        pool.wait_ge(fix_ready, 1)
                        pool.indirect_dma_start(target, at, fixed[:], None, bounds_check=last_out, oob_is_err=False).then_inc(fix_got, 16)
                        pool.wait_ge(fix_got, 32)

                    if not by_node:
                        @block.sync
                        def _(sp):
                            def store(i):
                                for b in range(B):
                                    sp.wait_ge(summed, i * B + (b + 1))
                                    sp.dma_start(target[bass.ds(i * (B * P) + b * P, P), :], total[:, b, :]).then_inc(stored[b], 16)

                            steps(sp, STEPS, store)

                    if net is not None:
                        @block.scalar
                        def _(act):
                            def copy(i, b):
                                act.wait_ge(turned, i * B + (b + 1))
                                wait(act, product, i * B + (b + 1 - B))
                                act.activation(xt[:, b], p_t[b % 2][:], ACT.Copy).then_inc(evac, 1)

                            def negative(i, b):
                                act.wait_ge(layered, i * B + (b + 1))
                                wait(act, made, i * B + (b + 1 - B))
                                act.activation(neg[:, b, :], y[:, b, :], ACT.Relu, scale=-1.0).then_inc(lowered, 1)

                            columns(act, [(copy, 0), (negative, 2)])

                    elif scale is not None:
                        @block.scalar
                        def _(act):
                            def times(i):
                                for b in range(B):
                                    act.wait_ge(got[b], i * 16 + 16)
                                    wait(act, summed, i * B + (b + 1 - B))
                                    act.activation(scaled[:, b, :], got_rows[:, b, :], ACT.Copy,
                                                   scale=scale[:, bass.ds(i * B + b, 1)]).then_inc(made, 1)

                            steps(act, STEPS, times)

                    @block.vector
                    def _(dve):
                        c_ = Chain(dve, own, gate)
                        c_(dve.memset(total[:, B - 1, :], 0.0))
                        dve.memset(fix[:], 0.0).then_inc(blank, 1)

                        def layer_out(i, b):
                            t = i * B + b
                            dve.wait_ge(product, t + 1)
                            wait(dve, made, i * B + (b + 1 - B))
                            wait(dve, lowered, i * B + (b + 1 - B))
                            dve.scalar_tensor_tensor(y[:, b, :], p_y[b % 2][:, 0:D], scale[:, bass.ds(t, 1)], bias_row[:], ALU.mult, ALU.add).then_inc(layered, 1)

                        def add_net(i, b):
                            t = i * B + b
                            dve.wait_ge(layered, t + 1)
                            dve.wait_ge(lowered, t + 1)
                            wait(dve, summed, i * B + (b + 1 - B))
                            dve.scalar_tensor_tensor(scaled[:, b, :], neg[:, b, :], fall[:], y[:, b, :], ALU.mult, ALU.add).then_inc(made, 1)
                            dve.wait_ge(made, t + 1)
                            wait(dve, stored[b], i * 16)
                            wait(dve, summed, t)
                            dve.scalar_tensor_tensor(total[:, b, :], total[:, (b - 1) % B, :], g["cont"][:, bass.ds(t, 1)],
                                                     scaled[:, b, :], ALU.mult, ALU.add).then_inc(summed, 1)

                        def add(i):
                            for b in range(B):
                                t = i * B + b
                                if weights is not None:
                                    dve.wait_ge(got[b], i * 16 + 16)
                                    rows_in = got_rows[:, b, :].rearrange("p (h c) -> p h c", c=HID)
                                    if width == HID:
                                        rows_in = rows_in.to_broadcast([P, HEADS, HID])
                                    wt = weights[:, bass.ds(t, 1), :].rearrange("p a h -> p (a h)").unsqueeze(2).to_broadcast([P, HEADS, HID])
                                    dve.tensor_tensor(scaled[:, b, :].rearrange("p (h c) -> p h c", c=HID), rows_in, wt, ALU.mult).then_inc(made, 1)
                                if scaled is not got_rows:
                                    dve.wait_ge(made, t + 1)
                                else:
                                    dve.wait_ge(got[b], i * 16 + 16)
                                wait(dve, stored[b], i * 16)
                                dve.scalar_tensor_tensor(total[:, b, :], total[:, (b - 1) % B, :], g["cont"][:, bass.ds(t, 1)],
                                                         scaled[:, b, :], ALU.mult, ALU.add).then_inc(summed, 1)
                                dve.wait_ge(summed, t + 1)

                        if net is not None:
                            columns(dve, [(layer_out, 0), (add_net, 3)])
                        else:
                            steps(dve, STEPS, add)
                        dve.wait_ge(carried, 1)
                        dve.wait_ge(fix_got, 16)
                        dve.tensor_tensor(fixed[:], fix[:], p_carry[:], ALU.add).then_inc(fix_ready, 1)

                    @block.tensor
                    def _(pe):
                        def turn(i, b):
                            pe.wait_ge(got[b], i * 16 + 16)
                            wait(pe, evac, i * B + (b - 1))
                            for c in range(2):
                                m = pe.transpose(p_t[b % 2][:, c, :], got_rows[:, b, c * P:(c + 1) * P], ident[:])
                            m.then_inc(turned, 1)

                        def mul(i, b):
                            pe.wait_ge(evac, i * B + (b + 1))
                            wait(pe, layered, i * B + (b - 1))
                            for c in range(2):
                                m = pe.matmul(p_y[b % 2][:, 0:D], xt[:, b, c, :], layer[:, c, :], start=(c == 0), stop=(c == 1))
                            m.then_inc(product, 1)

                        if net is not None:
                            columns(pe, [(turn, 0), (mul, 1)])
                        pe.wait_ge(summed, T)
                        pe.matmul(p_carry[:], g["carry"][:], total[:, B - 1, :], start=True, stop=True).then_inc(carried, 1)

        h0 = dram("h0", (N, HID))
        with phase(nc, "first") as (sem, sb_, ps):
            x_in = sb_("x_in", [P, 2, J, D])
            sc = sb_("sc", [P, 2, J, 2])
            xt = sb_("xt", [P, 2, J, 2, P])
            ho = sb_("ho", [P, 2, J, HID])
            p_t = [ps(f"t{s}", [P, J + 1, 2, P]) for s in range(2)]
            p_h = [ps(f"h{s}", [P, 512]) for s in range(2)]
            got_x, got_s, stored = sem.many("got_x", 2), sem.many("got_s", 2), sem.many("stored", 2)
            turned, evac, product, made = sem("turned"), sem("evac"), sem("product"), sem("made")
            gate = sem("gate")
            with nc.Block() as block:
                @block.sync
                def _(sp):
                    def load(i, s, p, j):
                        wait(sp, turned, i * 2 + (s - 1))
                        sp.dma_start(x_in[0:p, s, 0:j, :], group(a["x"], i, s, p, j)).then_inc(got_x[s], 16)
                        wait(sp, made, i * 2 + (s - 1))
                        sp.dma_start(sc[0:p, s, 0:j, :], group(dm, i, s, p, j)).then_inc(got_s[s], 16)

                    pairs(sp, [(load, 0)])

                @block.tensor
                def _(pe):
                    def turn(i, s, p, j):
                        pe.wait_ge(got_x[s], i * 16 + 16)
                        wait(pe, evac, i * 2 + (s - 1))
                        for k in range(j):
                            for c in range(2):
                                m = pe.transpose(p_t[s][:, k, c, 0:p], x_in[0:p, s, k, c * P:(c + 1) * P], ident[0:p, 0:p])
                        m.then_inc(turned, 1)

                    def mul(i, s, p, j):
                        pe.wait_ge(evac, i * 2 + (s + 1))
                        wait(pe, made, i * 2 + (s - 1))
                        for k in range(j):
                            for c in range(2):
                                m = pe.matmul(p_h[s][0:p, k * HID:(k + 1) * HID], xt[:, s, k, c, 0:p], w["a1"][:, c, :], start=(c == 0), stop=(c == 1))
                        m.then_inc(product, 1)

                    pairs(pe, [(turn, 0), (mul, 1)])

                @block.scalar
                def _(act):
                    def copy(i, s, p, j):
                        act.wait_ge(turned, i * 2 + (s + 1))
                        wait(act, product, i * 2 + (s - 1))
                        act.activation(xt[:, s, 0:j, :, 0:p], p_t[s][:, 0:j, :, 0:p], ACT.Copy).then_inc(evac, 1)

                    pairs(act, [(copy, 0)])

                @block.vector
                def _(dve):
                    def scale(i, s, p, j):
                        dve.wait_ge(product, i * 2 + (s + 1))
                        dve.wait_ge(got_s[s], i * 16 + 16)
                        wait(dve, stored[s], i * 16)
                        dve.tensor_tensor(ho[0:p, s, 0:j, :], p_h[s][0:p, 0:j * HID].rearrange("p (j c) -> p j c", c=HID),
                                          sc[0:p, s, 0:j, 0:1].to_broadcast([p, j, HID]), ALU.mult).then_inc(made, 1)

                    pairs(dve, [(scale, 0)])

                @block.gpsimd
                def _(pool):
                    def store(i, s, p, j):
                        pool.wait_ge(made, i * 2 + (s + 1))
                        settle(pool, gate)
                        pool.dma_start(group(h0, i, s, p, j), ho[0:p, s, 0:j, :]).then_inc(stored[s], 16)

                    pairs(pool, [(store, 0)])
                    pool.wait_ge(stored[0], 16 * (PAIRS + 1))
                    pool.wait_ge(stored[1], 16 * PAIRS)

        dst_runs = runs["d"]
        edge_sum("sum0", "d", h0, N, dst_runs["other"], HID, agg[0], True)

        def sum_bias_relu(c_, total, own, sc, bias_row, out, tmp, p, j, own_scaled):
            dve = c_.eng
            rs = sc[0:p, 0:j, 0:1].to_broadcast([p, j, HID])
            if not own_scaled:
                c_(dve.tensor_tensor(own, own, rs, ALU.mult))
            c_(dve.tensor_tensor(tmp, total, own, ALU.add))
            c_(dve.tensor_tensor(tmp, tmp, rs, ALU.mult))
            c_(dve.tensor_tensor(tmp, tmp, bias_row[0:p, :].unsqueeze(1).to_broadcast([p, j, HID]), ALU.add))

        h1 = dram("h1", (N, HID))
        with phase(nc, "second") as (sem, sb_, ps):
            sc = sb_("sc", [P, 2, J, 2])
            h_in = sb_("h_in", [P, 2, J, HID])
            a_in = sb_("a_in", [P, 2, J, HID])
            tmp = sb_("tmp", [P, 2, J, HID])
            ho = sb_("ho", [P, 2, J, HID])
            got, stored = [sem.many(f"got{k}_", 2) for k in range(3)], sem.many("stored", 2)
            made, own = sem("made"), sem("own")
            gate = sem("gate")
            with nc.Block() as block:
                @block.sync
                def _(sp):
                    def load(i, s, p, j):
                        wait(sp, made, i * 2 + (s - 1))
                        for k, (buf, table) in enumerate(((sc, dm), (h_in, h0), (a_in, agg[0]))):
                            sp.dma_start(buf[0:p, s, 0:j, :], group(table, i, s, p, j)).then_inc(got[k][s], 16)

                    pairs(sp, [(load, 0)])

                @block.vector
                def _(dve):
                    c_ = Chain(dve, own, gate)

                    def layer(i, s, p, j):
                        for k in range(3):
                            dve.wait_ge(got[k][s], i * 16 + 16)
                        wait(dve, stored[s], i * 16)
                        sum_bias_relu(c_, a_in[0:p, s, 0:j, :], h_in[0:p, s, 0:j, :], sc[:, s], bias["a1"], None, tmp[0:p, s, 0:j, :], p, j, True)
                        dve.scalar_tensor_tensor(ho[0:p, s, 0:j, :], tmp[0:p, s, 0:j, :], 0.0, sc[0:p, s, 0:j, 0:1].to_broadcast([p, j, HID]),
                                                 ALU.max, ALU.mult).then_inc(made, 1)

                    pairs(dve, [(layer, 0)], c_, 6)

                @block.gpsimd
                def _(pool):
                    def store(i, s, p, j):
                        pool.wait_ge(made, i * 2 + (s + 1))
                        settle(pool, gate)
                        pool.dma_start(group(h1, i, s, p, j), ho[0:p, s, 0:j, :]).then_inc(stored[s], 16)

                    pairs(pool, [(store, 0)])
                    pool.wait_ge(stored[0], 16 * (PAIRS + 1))
                    pool.wait_ge(stored[1], 16 * PAIRS)

        edge_sum("sum1", "d", h1, N, dst_runs["other"], HID, agg[1], True)

        x1, x2, g2 = dram("x1", (N, D)), dram("x2", (N, D)), dram("g2", (N, HID))
        with phase(nc, "third") as (sem, sb_, ps):
            sc = sb_("sc", [P, 2, J, 2])
            h_in = sb_("h_in", [P, 2, J, HID])
            a_in = sb_("a_in", [P, 2, J, HID])
            x_in = sb_("x_in", [P, 2, J, D])
            at = sb_("at", [HID, 2, J, P])
            x1o = sb_("x1o", [P, 2, J, D])
            y = sb_("y", [P, J, D])
            z = sb_("z", [P, J, D])
            low = sb_("low", [P, J, D])
            x2o = sb_("x2o", [P, 2, J, D])
            xt = sb_("xt", [P, 2, J, 2, P])
            go = sb_("go", [P, 2, J, HID])
            st = norm_buffers(sb_, J)
            p_a = ps("a", [HID, J, P])
            p_y = [ps(f"y{s}", [P, J + 1, D]) for s in range(2)]
            p_t = ps("t", [P, J + 1, 2, P])
            p_g = ps("g", [P, 512])
            got = [sem.many(f"got{k}_", 2) for k in range(4)]
            st1, st2, st3 = sem.many("st1_", 2), sem.many("st2_", 2), sem.many("st3_", 2)
            own, a_made, a_turned, a_copied, y_made, x1_made, x2_made = (sem(n) for n in
                ("own", "a_made", "a_turned", "a_copied", "y_made", "x1_made", "x2_made"))
            turned, copied, product, g_made, y_used = (sem(n) for n in ("turned", "copied", "product", "g_made", "y_used"))
            gate = sem("gate")
            with nc.Block() as block:
                @block.sync
                def _(sp):
                    def load(i, s, p, j):
                        wait(sp, a_turned, i * 2 + (s - 1))
                        for k, (buf, table) in enumerate(((sc, dm), (h_in, h1), (a_in, agg[1]))):
                            sp.dma_start(buf[0:p, s, 0:j, :], group(table, i, s, p, j)).then_inc(got[k][s], 16)
                        wait(sp, y_used, i * 2 + (s - 1))
                        sp.dma_start(x_in[0:p, s, 0:j, :], group(a["x"], i, s, p, j)).then_inc(got[3][s], 16)

                    pairs(sp, [(load, 0)])

                @block.tensor
                def _(pe):
                    def turn_a(i, s, p, j):
                        pe.wait_ge(a_made, i * 2 + (s + 1))
                        wait(pe, a_copied, i * 2 + s)
                        settle(pe, gate)
                        for k in range(j):
                            m = pe.transpose(p_a[:, k, 0:p], h_in[0:p, s, k, :], ident[0:p, 0:p])
                        m.then_inc(a_turned, 1)

                    def mul_y(i, s, p, j):
                        pe.wait_ge(a_copied, i * 2 + (s + 1))
                        wait(pe, y_used, i * 2 + (s - 1))
                        for k in range(j):
                            m = pe.matmul(p_y[s][0:p, k, :], at[:, s, k, 0:p], w["a2"][:], start=True, stop=True)
                        m.then_inc(y_made, 1)

                    def turn_x(i, s, p, j):
                        pe.wait_ge(x2_made, i * 2 + (s + 1))
                        wait(pe, copied, i * 2 + s)
                        for k in range(j):
                            for c in range(2):
                                m = pe.transpose(p_t[:, k, c, 0:p], x2o[0:p, s, k, c * P:(c + 1) * P], ident[0:p, 0:p])
                        m.then_inc(turned, 1)

                    def mul_g(i, s, p, j):
                        pe.wait_ge(copied, i * 2 + (s + 1))
                        wait(pe, g_made, i * 2 + s)
                        for k in range(j):
                            for c in range(2):
                                m = pe.matmul(p_g[0:p, k * HID:(k + 1) * HID], xt[:, s, k, c, 0:p], w["g"][:, c, :], start=(c == 0), stop=(c == 1))
                        m.then_inc(product, 1)

                    pairs(pe, [(turn_a, 0), (turn_x, 1), (mul_y, 0), (mul_g, 1)])

                @block.scalar
                def _(act):
                    def copy_a(i, s, p, j):
                        act.wait_ge(a_turned, i * 2 + (s + 1))
                        wait(act, y_made, i * 2 + (s - 1))
                        act.activation(at[:, s, 0:j, 0:p], p_a[:, 0:j, 0:p], ACT.Copy).then_inc(a_copied, 1)

                    def copy_x(i, s, p, j):
                        act.wait_ge(turned, i * 2 + (s + 1))
                        wait(act, product, i * 2 + (s - 1))
                        act.activation(xt[:, s, 0:j, :, 0:p], p_t[:, 0:j, :, 0:p], ACT.Copy).then_inc(copied, 1)

                    def copy_g(i, s, p, j):
                        act.wait_ge(product, i * 2 + (s + 1))
                        wait(act, st3[s], i * 16)
                        act.activation(go[0:p, s, 0:j, :], p_g[0:p, 0:j * HID].rearrange("p (j c) -> p j c", c=HID), ACT.Copy).then_inc(g_made, 1)

                    pairs(act, [(copy_a, 0), (copy_x, 1), (copy_g, 1)])

                @block.vector
                def _(dve):
                    c_ = Chain(dve, own, gate)

                    def conv(i, s, p, j):
                        for k in range(3):
                            dve.wait_ge(got[k][s], i * 16 + 16)
                        wait(dve, a_turned, i * 2 + (s - 1))
                        h, t = h_in[0:p, s, 0:j, :], a_in[0:p, s, 0:j, :]
                        c_(dve.tensor_tensor(t, t, h, ALU.add))
                        dve.tensor_tensor(h, t, sc[0:p, s, 0:j, 0:1].to_broadcast([p, j, HID]), ALU.mult).then_inc(a_made, 1)

                    def rest(i, s, p, j):
                        dve.wait_ge(y_made, i * 2 + (s + 1))
                        dve.wait_ge(got[3][s], i * 16 + 16)
                        wait(dve, st1[s], i * 16)
                        wait(dve, st2[s], i * 16)
                        wait(dve, turned, i * 2 + (s - 1))
                        row = lambda r: r[0:p, :].unsqueeze(1).to_broadcast([p, j, D])
                        c_(dve.tensor_tensor(y[0:p, 0:j, :], p_y[s][0:p, 0:j, :], row(bias["a2"]), ALU.add))
                        c_(dve.scalar_tensor_tensor(y[0:p, 0:j, :], y[0:p, 0:j, :], 0.0, x_in[0:p, s, 0:j, :], ALU.max, ALU.add))
                        dve.sem_inc(y_used, 1)
                        layer_norm(c_, y, x1o[:, s], st, p, j)
                        dve.sem_inc(x1_made, 1)
                        c_(dve.tensor_tensor(z[0:p, 0:j, :], x1o[0:p, s, 0:j, :], row(bias["b2"]), ALU.add))
                        c_(dve.tensor_scalar(low[0:p, 0:j, :], z[0:p, 0:j, :], 0.0, minus_fall[0:p], ALU.min, ALU.mult))
                        c_(dve.tensor_tensor(z[0:p, 0:j, :], z[0:p, 0:j, :], low[0:p, 0:j, :], ALU.add))
                        c_(dve.tensor_tensor(z[0:p, 0:j, :], z[0:p, 0:j, :], x1o[0:p, s, 0:j, :], ALU.add))
                        layer_norm(c_, z, x2o[:, s], st, p, j)
                        dve.sem_inc(x2_made, 1)

                    pairs(dve, [(conv, 0), (rest, 1)], c_, 2 * (1 + 2 + 4 + 2 * (3 * J + 12)))

                @block.gpsimd
                def _(pool):
                    def store(i, s, p, j):
                        pool.wait_ge(x1_made, i * 2 + (s + 1))
                        settle(pool, gate)
                        pool.dma_start(group(x1, i, s, p, j), x1o[0:p, s, 0:j, :]).then_inc(st1[s], 16)
                        pool.wait_ge(x2_made, i * 2 + (s + 1))
                        settle(pool, gate)
                        pool.dma_start(group(x2, i, s, p, j), x2o[0:p, s, 0:j, :]).then_inc(st2[s], 16)
                        pool.wait_ge(g_made, i * 2 + (s + 1))
                        settle(pool, gate)
                        pool.dma_start(group(g2, i, s, p, j), go[0:p, s, 0:j, :]).then_inc(st3[s], 16)

                    pairs(pool, [(store, 0)])
                    for q in (st1, st2, st3):
                        pool.wait_ge(q[0], 16 * (PAIRS + 1))
                        pool.wait_ge(q[1], 16 * PAIRS)


        m1, o1, m2, o2 = (dram(n, (ROWS, D)) for n in ("m1", "o1", "m2", "o2"))
        src_runs = runs["s"]
        edge_sum("m1", "d", x1, N, dst_runs["other"], D, m1, False)
        edge_sum("o1", "s", m1, ROWS, to_in_row, D, o1, False, scale=inv_other["s"])
        edge_sum("m2", "d", o1, ROWS, to_out_row, D, m2, False, scale=inv_other["d"], net=(w["b1"], bias["b1"]))
        edge_sum("o2", "s", m2, ROWS, to_in_row, D, o2, False, scale=inv_other["s"])

        with phase(nc, "x2_ends") as (sem, sb_, ps):
            g = src_runs
            o_in = sb_("o_in", [P, B, D])
            xg = sb_("xg", [P, B, D])
            xt = sb_("xt", [P, 2, 2, P])
            y = sb_("y", [P, D])
            z = sb_("z", [P, 1, D])
            low = sb_("low", [P, D])
            x2o = sb_("x2o", [P, B, D])
            xt2 = sb_("xt2", [P, 2, 2, P])
            go = sb_("go", [P, B, HID])
            idx, put1, put2 = (sb_(n, [P, B], I32) for n in ("idx", "put1", "put2"))
            st = norm_buffers(sb_, 1)
            p_t = [ps(f"t{k}", [P, 2, P]) for k in range(2)]
            p_y = [ps(f"y{k}", [P, 512]) for k in range(2)]
            p_u = [ps(f"u{k}", [P, 2, P]) for k in range(2)]
            p_g = [ps(f"g{k}", [P, 512]) for k in range(2)]
            loaded, got, st1, st2 = (sem.many(n, B) for n in ("loaded", "got", "st1_", "st2_"))
            fed, fed1, fed2, own = (sem(n) for n in ("fed", "fed1", "fed2", "own"))
            turned, copied, product, y_used, x2_made = (sem(n) for n in ("turned", "copied", "product", "y_used", "x2_made"))
            turned2, copied2, product2, g_made = (sem(n) for n in ("turned2", "copied2", "product2", "g_made"))
            gate = sem("gate")
            with nc.Block() as block:
                @block.sync
                def _(sp):
                    def load(i, b):
                        wait(sp, turned, i * B + (b + 1 - B))
                        sp.dma_start(o_in[:, b, :], o2[bass.ds(i * (B * P) + b * P, P), :]).then_inc(loaded[b], 16)

                    columns(sp, [(load, 0)])

                @block.gpsimd
                def _(pool):
                    last = pool.to_reg(N - 1)
                    feed = Feed(pool, gate, fed, idx, g["node"], got)
                    feed1 = Feed(pool, gate, fed1, put1, g["put"], st1)
                    feed2 = Feed(pool, gate, fed2, put2, g["put"], st2)

                    def gather(i, b):
                        wait(pool, x2_made, i * B + (b + 1 - B))
                        pool.indirect_dma_start(xg[:, b, :], None, x1, feed.at(b), bounds_check=last, oob_is_err=False).then_inc(got[b], 16)

                    def scatter(i, b):
                        pool.wait_ge(x2_made, i * B + (b + 1))
                        pool.indirect_dma_start(x2, feed1.at(b), x2o[:, b, :], None, bounds_check=last, oob_is_err=False).then_inc(st1[b], 16)
                        pool.wait_ge(g_made, i * B + (b + 1))
                        pool.indirect_dma_start(g2, feed2.at(b), go[:, b, :], None, bounds_check=last, oob_is_err=False).then_inc(st2[b], 16)

                    indexed(pool, gather, [feed], scatter, [feed1, feed2])
                    for q in st1 + st2:
                        pool.wait_ge(q, 16 * STEPS)

                @block.tensor
                def _(pe):
                    def turn(i, b):
                        pe.wait_ge(loaded[b], i * 16 + 16)
                        wait(pe, copied, i * B + (b - 1))
                        for c in range(2):
                            m = pe.transpose(p_t[b % 2][:, c, :], o_in[:, b, c * P:(c + 1) * P], ident[:])
                        m.then_inc(turned, 1)

                    def mul(i, b):
                        pe.wait_ge(copied, i * B + (b + 1))
                        wait(pe, y_used, i * B + (b - 1))
                        for c in range(2):
                            m = pe.matmul(p_y[b % 2][:, 0:D], xt[:, b % 2, c, :], w["b2"][:, c, :], start=(c == 0), stop=(c == 1))
                        m.then_inc(product, 1)

                    def turn2(i, b):
                        pe.wait_ge(x2_made, i * B + (b + 1))
                        wait(pe, copied2, i * B + (b - 1))
                        for c in range(2):
                            m = pe.transpose(p_u[b % 2][:, c, :], x2o[:, b, c * P:(c + 1) * P], ident[:])
                        m.then_inc(turned2, 1)

                    def mul2(i, b):
                        pe.wait_ge(copied2, i * B + (b + 1))
                        wait(pe, g_made, i * B + (b - 1))
                        for c in range(2):
                            m = pe.matmul(p_g[b % 2][:, 0:HID], xt2[:, b % 2, c, :], w["g"][:, c, :], start=(c == 0), stop=(c == 1))
                        m.then_inc(product2, 1)

                    columns(pe, [(turn, 0), (mul, 1), (turn2, 2), (mul2, 3)])

                @block.scalar
                def _(act):
                    def copy(i, b):
                        act.wait_ge(turned, i * B + (b + 1))
                        wait(act, product, i * B + (b - 1))
                        act.activation(xt[:, b % 2], p_t[b % 2][:], ACT.Copy).then_inc(copied, 1)

                    def copy2(i, b):
                        act.wait_ge(turned2, i * B + (b + 1))
                        wait(act, product2, i * B + (b - 1))
                        act.activation(xt2[:, b % 2], p_u[b % 2][:], ACT.Copy).then_inc(copied2, 1)

                    def copy_g(i, b):
                        act.wait_ge(product2, i * B + (b + 1))
                        wait(act, st2[b], i * 16)
                        act.activation(go[:, b, :], p_g[b % 2][:, 0:HID], ACT.Copy).then_inc(g_made, 1)

                    columns(act, [(copy, 0), (copy2, 2), (copy_g, 3)])

                @block.vector
                def _(dve):
                    c_ = Chain(dve, own, gate)

                    def node(i, b):
                        t = i * B + b
                        dve.wait_ge(product, t + 1)
                        dve.wait_ge(got[b], i * 16 + 16)
                        wait(dve, st1[b], i * 16)
                        wait(dve, turned2, i * B + (b + 1 - B))
                        c_(dve.scalar_tensor_tensor(y[:], p_y[b % 2][:, 0:D], g["inverse"][:, bass.ds(t, 1)], bias["b2"][:], ALU.mult, ALU.add))
                        dve.sem_inc(y_used, 1)
                        c_(dve.tensor_tensor(y[:], y[:], xg[:, b, :], ALU.add))
                        c_(dve.tensor_scalar(low[:], y[:], 0.0, minus_fall[:], ALU.min, ALU.mult))
                        c_(dve.tensor_tensor(y[:], y[:], xg[:, b, :], ALU.add))
                        c_(dve.tensor_tensor(z[:, 0, :], y[:], low[:], ALU.add))
                        layer_norm(c_, z, x2o[:, b:b + 1, :], st, P, 1)
                        dve.sem_inc(x2_made, 1)

                    columns(dve, [(node, 1)], c_, B * (5 + 15))

        edge_sum("gcn", "d", g2, N, dst_runs["other"], HID, agg[2], True, scale=rs_other)

        def batch_scale(c_, sums, squares, gamma, beta, b_row, scale, shift, tmp):
            dve = c_.eng
            mean, var, y, t, u, full = tmp
            c_(dve.tensor_scalar(mean, sums, 1.0 / N, None, ALU.mult))
            c_(dve.tensor_scalar(var, squares, 1.0 / N, None, ALU.mult))
            c_(dve.tensor_tensor(t, mean, mean, ALU.mult))
            c_(dve.tensor_tensor(var, var, t, ALU.subtract))
            c_(dve.tensor_scalar(var, var, 0.0, EPS, ALU.max, ALU.add))
            rstd_steps(c_, var, y, t, u)
            c_(dve.tensor_tensor(scale, gamma, y, ALU.mult))
            c_(dve.tensor_tensor(full, mean, b_row, ALU.add))
            c_(dve.tensor_tensor(full, b_row, full, ALU.subtract))
            c_(dve.tensor_tensor(full, full, scale, ALU.mult))
            c_(dve.tensor_tensor(shift, full, beta, ALU.add))

        r0 = dram("r0", (N, HID))
        stat0 = sb("stat0", [HID, 2])
        with phase(nc, "fourth") as (sem, sb_, ps):
            sc = sb_("sc", [P, 2, J, 2])
            h_in = sb_("h_in", [P, 2, J, HID])
            a_in = sb_("a_in", [P, 2, J, HID])
            tmp = sb_("tmp", [P, 2, J, HID])
            ho = sb_("ho", [P, 2, J, HID])
            sq = sb_("sq", [P, 2, J, HID])
            p_s = ps("s", [HID, 512])
            got, stored = [sem.many(f"got{k}_", 2) for k in range(3)], sem.many("stored", 2)
            made, own, squared, summed = sem("made"), sem("own"), sem("squared"), sem("summed")
            gate = sem("gate")
            with nc.Block() as block:
                @block.sync
                def _(sp):
                    def load(i, s, p, j):
                        wait(sp, made, i * 2 + (s - 1))
                        for k, (buf, table) in enumerate(((sc, dm), (h_in, g2), (a_in, agg[2]))):
                            sp.dma_start(buf[0:p, s, 0:j, :], group(table, i, s, p, j)).then_inc(got[k][s], 16)

                    pairs(sp, [(load, 0)])

                @block.vector
                def _(dve):
                    c_ = Chain(dve, own, gate)

                    def layer(i, s, p, j):
                        for k in range(3):
                            dve.wait_ge(got[k][s], i * 16 + 16)
                        wait(dve, stored[s], i * 16)
                        wait(dve, summed, i * 2 + (s - 1))
                        sum_bias_relu(c_, a_in[0:p, s, 0:j, :], h_in[0:p, s, 0:j, :], sc[:, s], bias["g"], None, tmp[0:p, s, 0:j, :], p, j, False)
                        dve.tensor_scalar(ho[0:p, s, 0:j, :], tmp[0:p, s, 0:j, :], 0.0, None, ALU.max).then_inc(made, 1)

                    pairs(dve, [(layer, 0)], c_, 8)
                    dve.wait_ge(summed, 2 * PAIRS + 1)
                    dve.tensor_copy(stat0[:], p_s[:, 0:2]).then_inc(own, 1)

                @block.scalar
                def _(act):
                    def square(i, s, p, j):
                        act.wait_ge(made, i * 2 + (s + 1))
                        wait(act, summed, i * 2 + (s - 1))
                        act.activation(sq[0:p, s, 0:j, :], ho[0:p, s, 0:j, :], ACT.Square).then_inc(squared, 1)

                    pairs(act, [(square, 0)])

                @block.tensor
                def _(pe):
                    def add(i, s, p, j):
                        pe.wait_ge(squared, i * 2 + (s + 1))
                        settle(pe, gate)
                        for k in range(j):
                            for c, buf in enumerate((ho, sq)):
                                m = pe.matmul(p_s[:, c:c + 1], buf[0:p, s, k, :], ones[0:p, 0:1], start=(isinstance(i, int) and i == 0 and s == 0 and k == 0 and c == 0),
                                              stop=(p == TAIL), skip_group_check=True)
                        m.then_inc(summed, 1)

                    pairs(pe, [(add, 0)])

                @block.gpsimd
                def _(pool):
                    def store(i, s, p, j):
                        pool.wait_ge(made, i * 2 + (s + 1))
                        settle(pool, gate)
                        pool.dma_start(group(r0, i, s, p, j), ho[0:p, s, 0:j, :]).then_inc(stored[s], 16)

                    pairs(pool, [(store, 0)])
                    pool.wait_ge(stored[0], 16 * (PAIRS + 1))
                    pool.wait_ge(stored[1], 16 * PAIRS)

        wg1 = sb("wg1", [HID, D])
        wa1 = sb("wa1", [HID, HID + 2 * HEADS])
        wbd = sb("wbd", [P, 2, P])
        wg2 = sb("wg2", [P, 2, D + 2 * HEADS])
        scale0, shift0 = sb("scale0", [HID, 1]), sb("shift0", [HID, 1])
        with phase(nc, "gat_weights") as (sem, sb_, ps):
            arow = sb_("arow", [P, 4, D])
            prod = sb_("prod", [P, D])
            cols = sb_("cols", [HID, 3])
            tmp = sb_("tmp", [HID, 6])
            loaded, own, blank = sem("loaded"), sem("own"), sem("blank")
            gate = sem("gate")
            with nc.Block() as block:
                @block.sync
                def _(sp):
                    jobs = [(arow[:, k, :], a[n].rearrange("h c -> (h c)").rearrange("(o n) -> o n", o=1).to_broadcast([P, D])) for k, n in
                            enumerate(("L2_gnn_a_src1", "L2_gnn_a_dst1", "L2_gnn_a_src2", "L2_gnn_a_dst2"))]
                    jobs.append((wg1[:], a["L2_gnn_W1"]))
                    jobs.append((wg2[:, :, 0:D], a["L2_gnn_W2"].rearrange("(c p) n -> p c n", p=P)))
                    for k, n in enumerate(("L2_gnn_g0", "L2_gnn_beta0", "L2_gnn_b_gcn")):
                        jobs.append((cols[:, k:k + 1], a[n].rearrange("(n o) -> n o", o=1)))
                    for target, source in jobs:
                        sp.dma_start(target, source).then_inc(loaded, 16)
                    sp.wait_ge(blank, 1)
                    for h in range(HEADS):
                        q = (h % 2) * HID
                        sp.dma_start(wbd[q:q + HID, h // 2, q:q + HID], a["L2_gnn_W1"][:, h * HID:(h + 1) * HID]).then_inc(loaded, 16)
                    sp.wait_ge(loaded, 16 * 13)

                @block.vector
                def _(dve):
                    c_ = Chain(dve, own, gate)
                    dve.memset(wbd[:], 0.0).then_inc(blank, 1)
                    dve.wait_ge(loaded, 16 * 13)
                    c_(dve.tensor_copy(wa1[:, 0:HID], ident[0:HID, 0:HID]))
                    for k in range(2):
                        c_(dve.tensor_tensor(prod[0:HID, :], wg1[:], arow[0:HID, k, :], ALU.mult))
                        c_(dve.tensor_reduce(wa1[:, HID + k * HEADS:HID + (k + 1) * HEADS], prod[0:HID, :].rearrange("p (h c) -> p h c", c=HID),
                                             mybir.AxisListType.X, ALU.add))
                        for c in range(2):
                            c_(dve.tensor_tensor(prod[:], wg2[:, c, 0:D], arow[:, 2 + k, :], ALU.mult))
                            c_(dve.tensor_reduce(wg2[:, c, D + k * HEADS:D + (k + 1) * HEADS], prod[:].rearrange("p (h c) -> p h c", c=HID),
                                                 mybir.AxisListType.X, ALU.add))
                    zero = zeros[0:HID, 0:1]
                    batch_scale(c_, stat0[:, 0:1], stat0[:, 1:2], cols[:, 0:1], cols[:, 1:2], zero, scale0[:], shift0[:],
                                [tmp[:, k:k + 1] for k in range(6)])

        hb0, al1 = dram("hb0", (N, HID)), dram("al1", (N, 2 * HEADS))
        gram = sb("gram", [HID, HID + 1])
        with phase(nc, "fifth") as (sem, sb_, ps):
            sc = sb_("sc", [P, 2, J, 2])
            r_in = sb_("r_in", [P, 2, J, HID])
            ht = sb_("ht", [HID, 2, J, P])
            hx = sb_("hx", [P, 2, J, HID + 1])
            ho = sb_("ho", [P, 2, J, HID])
            hm = sb_("hm", [P, 2, J, HID])
            al = sb_("al", [P, 2, J, 2 * HEADS])
            wide = HID + 2 * HEADS
            p_t = [ps(f"t{s}", [HID, 4, P]) for s in range(2)]
            p_h = [ps(f"h{s}", [P, 512]) for s in range(2)]
            p_g = ps("g", [HID, 512])
            got_r, got_s, st1, st2 = (sem.many(n, 2) for n in ("got_r", "got_s", "st1_", "st2_"))
            turned, normed, product, made, masked, summed, own = (sem(n) for n in ("turned", "normed", "product", "made", "masked", "summed", "own"))
            gate = sem("gate")
            with nc.Block() as block:
                @block.sync
                def _(sp):
                    def load(i, s, p, j):
                        wait(sp, turned, i * 2 + (s - 1))
                        sp.dma_start(r_in[0:p, s, 0:j, :], group(r0, i, s, p, j)).then_inc(got_r[s], 16)
                        wait(sp, masked, i * 2 + (s - 1))
                        sp.dma_start(sc[0:p, s, 0:j, :], group(dm, i, s, p, j)).then_inc(got_s[s], 16)

                    pairs(sp, [(load, 0)])

                @block.tensor
                def _(pe):
                    def turn(i, s, p, j):
                        pe.wait_ge(got_r[s], i * 16 + 16)
                        wait(pe, normed, i * 2 + (s - 1))
                        settle(pe, gate)
                        for k in range(j):
                            m = pe.transpose(p_t[s][:, k, 0:p], r_in[0:p, s, k, :], ident[0:p, 0:p])
                        m.then_inc(turned, 1)

                    def mul(i, s, p, j):
                        pe.wait_ge(normed, i * 2 + (s + 1))
                        wait(pe, made, i * 2 + (s - 1))
                        settle(pe, gate)
                        for k in range(j):
                            m = pe.matmul(p_h[s][0:p, k * wide:(k + 1) * wide], ht[:, s, k, 0:p], wa1[:], start=True, stop=True)
                        m.then_inc(product, 1)

                    def add(i, s, p, j):
                        pe.wait_ge(masked, i * 2 + (s + 1))
                        settle(pe, gate)
                        for k in range(j):
                            m = pe.matmul(p_g[:, 0:HID + 1], hm[0:p, s, k, :], hx[0:p, s, k, :], start=(isinstance(i, int) and i == 0 and s == 0 and k == 0),
                                          stop=(p == TAIL), skip_group_check=True)
                        m.then_inc(summed, 1)

                    pairs(pe, [(turn, 0), (mul, 1), (add, 1)])

                @block.scalar
                def _(act):
                    def norm(i, s, p, j):
                        act.wait_ge(turned, i * 2 + (s + 1))
                        wait(act, product, i * 2 + (s - 1))
                        act.activation(ht[:, s, 0:j, 0:p], p_t[s][:, 0:j, 0:p], ACT.Identity, scale=scale0[:], bias=shift0[:]).then_inc(normed, 1)

                    pairs(act, [(norm, 0)])

                @block.vector
                def _(dve):
                    c_ = Chain(dve, own, gate)
                    c_(dve.memset(hx[:], 1.0))

                    def take(i, s, p, j):
                        dve.wait_ge(product, i * 2 + (s + 1))
                        dve.wait_ge(got_s[s], i * 16 + 16)
                        wait(dve, st1[s], i * 16)
                        wait(dve, st2[s], i * 16)
                        wait(dve, summed, i * 2 + (s - 1))
                        both = p_h[s][0:p, 0:j * wide].rearrange("p (j c) -> p j c", c=wide)
                        c_(dve.tensor_copy(ho[0:p, s, 0:j, :], both[:, :, 0:HID]))
                        c_(dve.tensor_copy(hx[0:p, s, 0:j, 0:HID], both[:, :, 0:HID]))
                        c_(dve.tensor_copy(al[0:p, s, 0:j, :], both[:, :, HID:wide]))
                        dve.sem_inc(made, 1)
                        dve.tensor_tensor(hm[0:p, s, 0:j, :], ho[0:p, s, 0:j, :], sc[0:p, s, 0:j, 1:2].to_broadcast([p, j, HID]), ALU.mult).then_inc(masked, 1)

                    pairs(dve, [(take, 0)], c_, 6)
                    dve.wait_ge(summed, 2 * PAIRS + 1)
                    c_(dve.tensor_copy(gram[:], p_g[:, 0:HID + 1]))

                @block.gpsimd
                def _(pool):
                    def store(i, s, p, j):
                        pool.wait_ge(made, i * 2 + (s + 1))
                        settle(pool, gate)
                        pool.dma_start(group(hb0, i, s, p, j), ho[0:p, s, 0:j, :]).then_inc(st1[s], 16)
                        pool.dma_start(group(al1, i, s, p, j), al[0:p, s, 0:j, :]).then_inc(st2[s], 16)

                    pairs(pool, [(store, 0)])
                    for q in (st1, st2):
                        pool.wait_ge(q[0], 16 * (PAIRS + 1))
                        pool.wait_ge(q[1], 16 * PAIRS)

        w_edge, w_self, w_inv = (sb(n, [P, T, HEADS]) for n in ("w_edge", "w_self", "w_inv"))

        def attention(tag, al):
            with ExitStack() as told_ctx:
                t_src, t_dst = (told_ctx.enter_context(nc.sbuf_tensor(f"{tag}_{k}", [P, T, 2 * HEADS], F32)) for k in ("src", "dst"))
                small_rows(f"{tag}_scores", al, N, 2 * HEADS, [(dst_runs["other"], t_src), (dst_runs["node"], t_dst)])
                with phase(nc, tag) as (sem, sb_, ps):
                    g = dst_runs
                    e, es, most, back = (sb_(n, [P, T, HEADS]) for n in ("e", "es", "most", "back"))
                    edge = sb_("edge", [P, 4 * HEADS])
                    rows = sb_("rows", [2 * HEADS, P])
                    flat = sb_("flat", [HEADS, 8, P + 2])
                    carry_f, carry_b, carry_w = (sb_(n, [P, HEADS]) for n in ("carry_f", "carry_b", "carry_w"))
                    p_r = [ps(f"r{k}", [HEADS, 512]) for k in range(4)]
                    p_c = [ps(f"c{k}", [P, 512]) for k in range(3)]
                    own, ends, turned, rowed, colled = (sem(n) for n in ("own", "ends", "turned", "rowed", "colled"))
                    exps, first_w, carried = sem("exps"), sem("first_w"), sem("carried")
                    exp_in, exp_out = sem("exp_in"), sem("exp_out")
                    gate = sem("gate")
                    with nc.Block() as block:
                        @block.tensor
                        def _(pe):
                            pe.wait_ge(ends, 1)
                            for k in range(4):
                                m = pe.transpose(p_r[k][:, 0:P], edge[:, k * HEADS:(k + 1) * HEADS], ident[:])
                            m.then_inc(turned, 1)
                            pe.wait_ge(rowed, 1)
                            pe.transpose(p_c[0][:, 0:HEADS], flat[:, 4, 0:P], ident[0:HEADS, 0:HEADS])
                            pe.transpose(p_c[1][:, 0:HEADS], flat[:, 5, 2:P + 2], ident[0:HEADS, 0:HEADS]).then_inc(colled, 1)
                            pe.wait_ge(first_w, 1)
                            pe.matmul(p_c[2][:, 0:HEADS], g["carry"][:], edge[:, 0:HEADS], start=True, stop=True).then_inc(carried, 1)

                        @block.scalar
                        def _(act):
                            act.wait_ge(exp_in, 1)
                            act.activation(w_edge[:], e[:], ACT.Exp).then_inc(exp_out, 1)
                            act.activation(w_self[:], es[:], ACT.Exp).then_inc(exp_out, 1)

                        @block.vector
                        def _(dve):
                            c_ = Chain(dve, own, gate)
                            c_(dve.tensor_tensor(most[:], t_src[:, :, 0:HEADS], t_dst[:, :, HEADS:2 * HEADS], ALU.add))
                            c_(dve.scalar_tensor_tensor(e[:], most[:], 0.2, most[:], ALU.mult, ALU.max))
                            c_(dve.tensor_tensor(back[:], t_dst[:, :, 0:HEADS], t_dst[:, :, HEADS:2 * HEADS], ALU.add))
                            c_(dve.scalar_tensor_tensor(es[:], back[:], 0.2, back[:], ALU.mult, ALU.max))
                            for h in range(HEADS):
                                c_(dve.tensor_tensor_scan(most[:, :, h], g["pen"][:], e[:, :, h], NEG, ALU.add, ALU.max))
                                c_(dve.tensor_tensor_scan(back[:, ::-1, h], g["rpen"][:, ::-1], e[:, ::-1, h], NEG, ALU.add, ALU.max))
                            c_(dve.tensor_copy(edge[:, 0:HEADS], most[:, T - 1, :]))
                            c_(dve.tensor_copy(edge[:, HEADS:2 * HEADS], back[:, 0, :]))
                            c_(dve.tensor_copy(edge[:, 2 * HEADS:3 * HEADS], g["whole"][:, 0:1].to_broadcast([P, HEADS])))
                            c_(dve.tensor_copy(edge[:, 3 * HEADS:4 * HEADS], g["whole"][:, 1:2].to_broadcast([P, HEADS])))
                            dve.sem_inc(ends, 1)
                            dve.wait_ge(turned, 1)
                            for k in range(4):
                                c_(dve.tensor_copy(flat[:, k, 0:P], p_r[k][:, 0:P]))
                            c_(dve.memset(flat[:, 4:6, :], NEG))
                            c_(dve.tensor_tensor_scan(flat[:, 4, 1:P + 1], flat[:, 2, 0:P], flat[:, 0, 0:P], NEG, ALU.add, ALU.max))
                            c_(dve.tensor_tensor_scan(flat[:, 5, 1:P + 1][:, ::-1], flat[:, 3, 0:P][:, ::-1], flat[:, 1, 0:P][:, ::-1], NEG, ALU.add, ALU.max))
                            dve.sem_inc(rowed, 1)
                            dve.wait_ge(colled, 1)
                            c_(dve.tensor_copy(carry_f[:], p_c[0][:, 0:HEADS]))
                            c_(dve.tensor_copy(carry_b[:], p_c[1][:, 0:HEADS]))
                            for h in range(HEADS):
                                c_(dve.tensor_tensor_scan(most[:, :, h], g["pen"][:], e[:, :, h], carry_f[:, h:h + 1], ALU.add, ALU.max))
                                c_(dve.tensor_tensor_scan(back[:, ::-1, h], g["rpen"][:, ::-1], e[:, ::-1, h], carry_b[:, h:h + 1], ALU.add, ALU.max))
                            c_(dve.tensor_tensor(most[:], most[:], back[:], ALU.max))
                            c_(dve.tensor_tensor(most[:], most[:], es[:], ALU.max))
                            c_(dve.tensor_tensor(e[:], e[:], most[:], ALU.subtract))
                            c_(dve.tensor_tensor(es[:], es[:], most[:], ALU.subtract))
                            dve.sem_inc(exp_in, 1)
                            dve.wait_ge(exp_out, 2)
                            for h in range(HEADS):
                                c_(dve.tensor_tensor_scan(most[:, :, h], g["cont"][:], w_edge[:, :, h], 0.0, ALU.mult, ALU.add))
                            c_(dve.tensor_copy(edge[:, 0:HEADS], most[:, T - 1, :]))
                            dve.sem_inc(first_w, 1)
                            dve.wait_ge(carried, 1)
                            c_(dve.tensor_copy(carry_w[:], p_c[2][:, 0:HEADS]))
                            for h in range(HEADS):
                                c_(dve.tensor_tensor_scan(most[:, :, h], g["cont"][:], w_edge[:, :, h], carry_w[:, h:h + 1], ALU.mult, ALU.add))
                            c_(dve.tensor_tensor(most[:], most[:], w_self[:], ALU.add))
                            c_(dve.tensor_scalar(most[:], most[:], 1.0e-30, None, ALU.max))
                            c_(dve.reciprocal(w_inv[:], most[:]))

        attention("soft1", al1)
        rg1, ue1 = dram("rg1", (ROWS, D)), dram("ue1", (ROWS, D))
        edge_sum("gat1", "d", hb0, N, dst_runs["other"], HID, rg1, False, weights=w_edge)

        stat1 = sb("stat1", [P, 4])

        def attention_ends(tag, rg, table, width, ue, stat, blocks):
            with phase(nc, tag) as (sem, sb_, ps):
                g = dst_runs
                r_in = sb_("r_in", [P, B, D])
                hg = sb_("hg", [P, B, width])
                z = sb_("z", [P, B, D])
                zt = sb_("zt", [P, 2, 2, P])
                u = sb_("u", [P, B, D])
                sq = sb_("sq", [P, 2, D])
                idx = sb_("idx", [P, B], I32)
                p_t = [ps(f"t{k}", [P, 2, P]) for k in range(2)]
                p_y = [ps(f"y{k}", [P, 512]) for k in range(2)]
                p_s = ps("s", [P, 512])
                loaded, got, stored = (sem.many(n, B) for n in ("loaded", "got", "stored"))
                fed, own, z_made, turned, copied, product, made, squared, summed = (sem(n) for n in
                    ("fed", "own", "z_made", "turned", "copied", "product", "made", "squared", "summed"))
                gate = sem("gate")
                with nc.Block() as block:
                    @block.sync
                    def _(sp):
                        def load(i, b):
                            wait(sp, z_made, i * B + (b + 1 - B))
                            sp.dma_start(r_in[:, b, :], rg[bass.ds(i * (B * P) + b * P, P), :]).then_inc(loaded[b], 16)

                        def store(i, b):
                            sp.wait_ge(made, i * B + (b + 1))
                            sp.dma_start(ue[bass.ds(i * (B * P) + b * P, P), :], u[:, b, :]).then_inc(stored[b], 16)

                        columns(sp, [(load, 0), (store, 8)])
                        for q in stored:
                            sp.wait_ge(q, 16 * STEPS)

                    @block.gpsimd
                    def _(pool):
                        last = pool.to_reg(N - 1)
                        feed = Feed(pool, gate, fed, idx, g["node"], got)

                        def gather(i, b):
                            wait(pool, z_made, i * B + (b + 1 - B))
                            pool.indirect_dma_start(hg[:, b, :], None, table, feed.at(b), bounds_check=last, oob_is_err=False).then_inc(got[b], 16)

                        indexed(pool, gather, [feed])

                    @block.vector
                    def _(dve):
                        c_ = Chain(dve, own, gate)
                        heads = lambda x: x.rearrange("p (h c) -> p h c", c=HID)
                        by_head = lambda x, t: x[:, bass.ds(t, 1), :].rearrange("p a h -> p (a h)").unsqueeze(2).to_broadcast([P, HEADS, HID])

                        def mix(i, b):
                            t = i * B + b
                            dve.wait_ge(got[b], i * 16 + 16)
                            dve.wait_ge(loaded[b], i * 16 + 16)
                            wait(dve, turned if blocks is not None else made, i * B + (b + 1 - B))
                            own_row_ = heads(hg[:, b, :])
                            if width == HID:
                                own_row_ = own_row_.to_broadcast([P, HEADS, HID])
                            c_(dve.tensor_tensor(heads(z[:, b, :]), own_row_, by_head(w_self, t), ALU.mult))
                            dve.tensor_tensor(z[:, b, :], z[:, b, :], r_in[:, b, :], ALU.add).then_inc(z_made, 1)

                        def divide(i, b):
                            t = i * B + b
                            if blocks is not None:
                                dve.wait_ge(product, t + 1)
                                of = heads(p_y[b % 2][:, 0:D])
                            else:
                                dve.wait_ge(z_made, t + 1)
                                of = heads(z[:, b, :])
                            wait(dve, stored[b], i * 16)
                            wait(dve, summed, i * B + (b + 1 - B))
                            dve.tensor_tensor(heads(u[:, b, :]), of, by_head(w_inv, t), ALU.mult).then_inc(made, 1)

                        columns(dve, [(mix, 0), (divide, 2)], c_, B)
                        dve.wait_ge(summed, T)
                        c_(dve.tensor_copy(stat[:], p_s[:, 0:4]))

                    @block.scalar
                    def _(act):
                        def copy(i, b):
                            act.wait_ge(turned, i * B + (b + 1))
                            wait(act, product, i * B + (b - 1))
                            act.activation(zt[:, b % 2], p_t[b % 2][:], ACT.Copy).then_inc(copied, 1)

                        def square(i, b):
                            act.wait_ge(made, i * B + (b + 1))
                            wait(act, summed, i * B + (b - 1))
                            act.activation(sq[:, b % 2, :], u[:, b, :], ACT.Square).then_inc(squared, 1)

                        columns(act, ([(copy, 0)] if blocks is not None else []) + [(square, 2)])

                    @block.tensor
                    def _(pe):
                        def turn(i, b):
                            pe.wait_ge(z_made, i * B + (b + 1))
                            wait(pe, copied, i * B + (b - 1))
                            for c in range(2):
                                m = pe.transpose(p_t[b % 2][:, c, :], z[:, b, c * P:(c + 1) * P], ident[:])
                            m.then_inc(turned, 1)

                        def mul(i, b):
                            pe.wait_ge(copied, i * B + (b + 1))
                            wait(pe, made, i * B + (b - 1))
                            for c in range(2):
                                m = pe.matmul(p_y[b % 2][:, c * P:(c + 1) * P], zt[:, b % 2, c, :], blocks[:, c, :], start=True, stop=True)
                            m.then_inc(product, 1)

                        def add(i, b):
                            t = i * B + b
                            pe.wait_ge(squared, t + 1)
                            settle(pe, gate)
                            for k in range(4):
                                buf = u[:, b, (k % 2) * P:(k % 2 + 1) * P] if k < 2 else sq[:, b % 2, (k % 2) * P:(k % 2 + 1) * P]
                                m = pe.matmul(p_s[:, k:k + 1], buf, g["endm"][:, bass.ds(t, 1)], start=(isinstance(i, int) and i == 0 and b == 0 and k == 0),
                                              stop=False, skip_group_check=True)
                            m.then_inc(summed, 1)

                        columns(pe, ([(turn, 0), (mul, 1)] if blocks is not None else []) + [(add, 3)])

        attention_ends("gat1_ends", rg1, hb0, HID, ue1, stat1, wbd)

        scale1, shift1 = sb("scale1", [P, 2]), sb("shift1", [P, 2])
        with phase(nc, "norm1") as (sem, sb_, ps):
            gw = sb_("gw", [HID, D])
            cols1 = sb_("cols1", [P, 3, 2])
            tmp = sb_("tmp", [P, 6, 2])
            stat = sb_("stat", [P, 4])
            p_w = ps("w", [HID, 512])
            p_s = ps("s", [P, 512])
            loaded, own, gw_made, prod_made, done = (sem(n) for n in ("loaded", "own", "gw_made", "prod_made", "done"))
            gate = sem("gate")
            with nc.Block() as block:
                @block.sync
                def _(sp):
                    for k, n in enumerate(("L2_gnn_g1", "L2_gnn_beta1", "L2_gnn_b1")):
                        for c in range(2):
                            sp.dma_start(cols1[:, k, c:c + 1], a[n][c * P:(c + 1) * P].rearrange("(n o) -> n o", o=1)).then_inc(loaded, 16)
                    sp.wait_ge(loaded, 16 * 6)

                @block.tensor
                def _(pe):
                    pe.matmul(p_w[:, 0:D], gram[:, 0:HID], wg1[:], start=True, stop=True).then_inc(gw_made, 1)
                    pe.wait_ge(prod_made, 1)
                    for c in range(2):
                        pe.matmul(p_s[:, c:c + 1], wg1[:, c * P:(c + 1) * P], gram[:, HID:HID + 1], start=(c == 0), stop=False, skip_group_check=True)
                    for c in range(2):
                        m = pe.matmul(p_s[:, 2 + c:3 + c], gw[:, c * P:(c + 1) * P], ones[0:HID, 0:1], start=False, stop=(c == 1), skip_group_check=True)
                    m.then_inc(done, 1)

                @block.vector
                def _(dve):
                    c_ = Chain(dve, own, gate)
                    dve.wait_ge(gw_made, 1)
                    c_(dve.tensor_tensor(gw[:], p_w[:, 0:D], wg1[:], ALU.mult))
                    dve.sem_inc(prod_made, 1)
                    dve.wait_ge(done, 1)
                    dve.wait_ge(loaded, 16 * 6)
                    c_(dve.tensor_tensor(stat[:], p_s[:, 0:4], stat1[:], ALU.add))
                    batch_scale(c_, stat[:, 0:2], stat[:, 2:4], cols1[:, 0, :], cols1[:, 1, :], cols1[:, 2, :], scale1[:], shift1[:],
                                [tmp[:, k, :] for k in range(6)])

        wide2 = D + 2 * HEADS
        hh, al2 = dram("hh", (N, D)), dram("al2", (N, 2 * HEADS))
        stat2a, stat2 = sb("stat2a", [P, 4]), sb("stat2", [P, 4])
        with phase(nc, "sixth") as (sem, sb_, ps):
            sc = sb_("sc", [P, 2, J, 2])
            h_in = sb_("h_in", [P, 2, J, HID])
            ht = sb_("ht", [HID, 2, J, P])
            z, low, ex, e1 = (sb_(n, [P, 2, 2, J, P]) for n in ("z", "low", "ex", "e1"))
            ho = sb_("ho", [P, 2, J, D])
            sq = sb_("sq", [P, 2, J, D])
            al = sb_("al", [P, 2, J, 2 * HEADS])
            p_t = ps("t", [HID, 4, P])
            p_u = [ps(f"u{c}", [P, 4, P]) for c in range(2)]
            p_h = ps("h", [P, J, 512])
            p_s = ps("s", [P, 512])
            got_h, got_s, st1, st2 = (sem.many(n, 2) for n in ("got_h", "got_s", "st1_", "st2_"))
            turned, copied, u_made, z_made, low_made, exped, e_made, h_made, taken, squared, summed, own = (sem(n) for n in
                ("turned", "copied", "u_made", "z_made", "low_made", "exped", "e_made", "h_made", "taken", "squared", "summed", "own"))
            gate = sem("gate")
            with nc.Block() as block:
                @block.sync
                def _(sp):
                    def load(i, s, p, j):
                        wait(sp, turned, i * 2 + (s - 1))
                        sp.dma_start(h_in[0:p, s, 0:j, :], group(hb0, i, s, p, j)).then_inc(got_h[s], 16)
                        wait(sp, summed, i * 2 + (s - 1))
                        sp.dma_start(sc[0:p, s, 0:j, :], group(dm, i, s, p, j)).then_inc(got_s[s], 16)

                    pairs(sp, [(load, 0)])

                @block.tensor
                def _(pe):
                    def turn(i, s, p, j):
                        pe.wait_ge(got_h[s], i * 16 + 16)
                        wait(pe, copied, i * 2 + s)
                        settle(pe, gate)
                        for k in range(j):
                            m = pe.transpose(p_t[:, k, 0:p], h_in[0:p, s, k, :], ident[0:p, 0:p])
                        m.then_inc(turned, 1)

                    def mul_u(i, s, p, j):
                        pe.wait_ge(copied, i * 2 + (s + 1))
                        wait(pe, z_made, i * 2 + s)
                        rows = ht[:, s, 0, 0:p] if j == 1 else ht[:, s].rearrange("p j q -> p (j q)")
                        for c in range(2):
                            to = p_u[c][:, 0, 0:p] if j == 1 else p_u[c][:, 0:j, :].rearrange("p j q -> p (j q)")
                            m = pe.matmul(to, wg1[:, c * P:(c + 1) * P], rows, start=True, stop=True)
                        m.then_inc(u_made, 1)

                    def mul_h(i, s, p, j):
                        pe.wait_ge(e_made, i * 2 + (s + 1))
                        wait(pe, taken, i * 2 + s)
                        for k in range(j):
                            for c in range(2):
                                m = pe.matmul(p_h[0:p, k, 0:wide2], e1[:, s, c, k, 0:p], wg2[:, c, :], start=(c == 0), stop=(c == 1))
                        m.then_inc(h_made, 1)

                    def add(i, s, p, j):
                        pe.wait_ge(squared, i * 2 + (s + 1))
                        pe.wait_ge(got_s[s], i * 16 + 16)
                        settle(pe, gate)
                        for k in range(j):
                            for c in range(4):
                                buf = (ho, sq)[c // 2]
                                m = pe.matmul(p_s[:, c:c + 1], buf[0:p, s, k, (c % 2) * P:(c % 2 + 1) * P], sc[0:p, s, k, 1:2],
                                              start=(isinstance(i, int) and i == 0 and s == 0 and k == 0 and c == 0),
                                              stop=(p == TAIL), skip_group_check=True)
                        m.then_inc(summed, 1)

                    pairs(pe, [(turn, 0), (mul_h, 1), (mul_u, 0), (add, 1)])

                @block.scalar
                def _(act):
                    def copy(i, s, p, j):
                        act.wait_ge(turned, i * 2 + (s + 1))
                        wait(act, u_made, i * 2 + (s - 1))
                        act.activation(ht[:, s, 0:j, 0:p], p_t[:, 0:j, 0:p], ACT.Copy).then_inc(copied, 1)

                    def norm(i, s, p, j):
                        act.wait_ge(u_made, i * 2 + (s + 1))
                        wait(act, e_made, i * 2 + (s - 1))
                        for c in range(2):
                            m = act.activation(z[:, s, c, 0:j, 0:p], p_u[c][:, 0:j, 0:p], ACT.Identity, scale=scale1[:, c:c + 1], bias=shift1[:, c:c + 1])
                        m.then_inc(z_made, 1)

                    def exp(i, s, p, j):
                        act.wait_ge(low_made, i * 2 + (s + 1))
                        wait(act, e_made, i * 2 + (s - 1))
                        for c in range(2):
                            m = act.activation(ex[:, s, c, 0:j, 0:p], low[:, s, c, 0:j, 0:p], ACT.Exp)
                        m.then_inc(exped, 1)

                    def square(i, s, p, j):
                        act.wait_ge(taken, i * 2 + (s + 1))
                        wait(act, summed, i * 2 + (s - 1))
                        act.activation(sq[0:p, s, 0:j, :], ho[0:p, s, 0:j, :], ACT.Square).then_inc(squared, 1)

                    pairs(act, [(copy, 0), (exp, 1), (norm, 0), (square, 1)])

                @block.vector
                def _(dve):
                    def fall_(i, s, p, j):
                        dve.wait_ge(z_made, i * 2 + (s + 1))
                        wait(dve, exped, i * 2 + (s - 1))
                        for c in range(2):
                            m = dve.tensor_scalar(low[:, s, c, 0:j, 0:p], z[:, s, c, 0:j, 0:p], 0.0, None, ALU.min)
                        m.then_inc(low_made, 1)

                    def elu(i, s, p, j):
                        dve.wait_ge(exped, i * 2 + (s + 1))
                        wait(dve, h_made, i * 2 + (s - 1))
                        for c in range(2):
                            m = dve.scalar_tensor_tensor(e1[:, s, c, 0:j, 0:p], ex[:, s, c, 0:j, 0:p], -1.0, z[:, s, c, 0:j, 0:p], ALU.add, ALU.max)
                        m.then_inc(e_made, 1)

                    def take(i, s, p, j):
                        dve.wait_ge(h_made, i * 2 + (s + 1))
                        wait(dve, st1[s], i * 16)
                        wait(dve, st2[s], i * 16)
                        wait(dve, summed, i * 2 + (s - 1))
                        dve.tensor_copy(ho[0:p, s, 0:j, :], p_h[0:p, 0:j, 0:D])
                        dve.tensor_copy(al[0:p, s, 0:j, :], p_h[0:p, 0:j, D:wide2]).then_inc(taken, 1)

                    pairs(dve, [(elu, 1), (fall_, 0), (take, 1)])
                    dve.wait_ge(summed, 2 * PAIRS + 1)
                    dve.tensor_copy(stat2a[:], p_s[:, 0:4]).then_inc(own, 1)

                @block.gpsimd
                def _(pool):
                    def store(i, s, p, j):
                        pool.wait_ge(taken, i * 2 + (s + 1))
                        settle(pool, gate)
                        pool.dma_start(group(hh, i, s, p, j), ho[0:p, s, 0:j, :]).then_inc(st1[s], 16)
                        pool.dma_start(group(al2, i, s, p, j), al[0:p, s, 0:j, :]).then_inc(st2[s], 16)

                    pairs(pool, [(store, 0)])
                    for q in (st1, st2):
                        pool.wait_ge(q[0], 16 * (PAIRS + 1))
                        pool.wait_ge(q[1], 16 * PAIRS)

        with phase(nc, "hh_ends") as (sem, sb_, ps):
            g = dst_runs
            r_in = sb_("r_in", [P, B, D])
            z, low, ex, e1 = (sb_(n, [P, 2, 2, P]) for n in ("z", "low", "ex", "e1"))
            ho = sb_("ho", [P, B, D])
            al = sb_("al", [P, B, 2 * HEADS])
            put1, put2 = (sb_(n, [P, B], I32) for n in ("put1", "put2"))
            p_t = [ps(f"t{k}", [P, 4, P]) for k in range(2)]
            p_h = [ps(f"h{k}", [P, 512]) for k in range(2)]
            loaded, st1, st2 = (sem.many(n, B) for n in ("loaded", "st1_", "st2_"))
            fed1, fed2, turned, z_made, low_made, exped, e_made, h_made, taken = (sem(n) for n in
                ("fed1", "fed2", "turned", "z_made", "low_made", "exped", "e_made", "h_made", "taken"))
            gate = sem("gate")
            with nc.Block() as block:
                @block.sync
                def _(sp):
                    def load(i, b):
                        wait(sp, turned, i * B + (b + 1 - B))
                        sp.dma_start(r_in[:, b, :], ue1[bass.ds(i * (B * P) + b * P, P), :]).then_inc(loaded[b], 16)

                    columns(sp, [(load, 0)])

                @block.tensor
                def _(pe):
                    def turn(i, b):
                        pe.wait_ge(loaded[b], i * 16 + 16)
                        wait(pe, z_made, i * B + (b - 1))
                        for c in range(2):
                            m = pe.transpose(p_t[b % 2][:, c, :], r_in[:, b, c * P:(c + 1) * P], ident[:])
                        m.then_inc(turned, 1)

                    def mul(i, b):
                        pe.wait_ge(e_made, i * B + (b + 1))
                        wait(pe, taken, i * B + (b - 1))
                        for c in range(2):
                            m = pe.matmul(p_h[b % 2][:, 0:wide2], e1[:, b % 2, c, :], wg2[:, c, :], start=(c == 0), stop=(c == 1))
                        m.then_inc(h_made, 1)

                    columns(pe, [(turn, 0), (mul, 2)])

                @block.scalar
                def _(act):
                    def norm(i, b):
                        act.wait_ge(turned, i * B + (b + 1))
                        wait(act, e_made, i * B + (b - 1))
                        for c in range(2):
                            m = act.activation(z[:, b % 2, c, :], p_t[b % 2][:, c, :], ACT.Identity, scale=scale1[:, c:c + 1], bias=shift1[:, c:c + 1])
                        m.then_inc(z_made, 1)

                    def exp(i, b):
                        act.wait_ge(low_made, i * B + (b + 1))
                        wait(act, e_made, i * B + (b - 1))
                        act.activation(ex[:, b % 2], low[:, b % 2], ACT.Exp).then_inc(exped, 1)

                    columns(act, [(norm, 0), (exp, 1)])

                @block.vector
                def _(dve):
                    def fall_(i, b):
                        dve.wait_ge(z_made, i * B + (b + 1))
                        wait(dve, exped, i * B + (b - 1))
                        dve.tensor_scalar(low[:, b % 2], z[:, b % 2], 0.0, None, ALU.min).then_inc(low_made, 1)

                    def elu(i, b):
                        dve.wait_ge(exped, i * B + (b + 1))
                        wait(dve, h_made, i * B + (b - 1))
                        dve.scalar_tensor_tensor(e1[:, b % 2], ex[:, b % 2], -1.0, z[:, b % 2], ALU.add, ALU.max).then_inc(e_made, 1)

                    def take(i, b):
                        dve.wait_ge(h_made, i * B + (b + 1))
                        wait(dve, st1[b], i * 16)
                        wait(dve, st2[b], i * 16)
                        dve.tensor_copy(ho[:, b, :], p_h[b % 2][:, 0:D])
                        dve.tensor_copy(al[:, b, :], p_h[b % 2][:, D:wide2]).then_inc(taken, 1)

                    columns(dve, [(fall_, 0), (elu, 1), (take, 2)])

                @block.gpsimd
                def _(pool):
                    last = pool.to_reg(N - 1)
                    feed1 = Feed(pool, gate, fed1, put1, g["put"], st1)
                    feed2 = Feed(pool, gate, fed2, put2, g["put"], st2)

                    def scatter(i, b):
                        pool.wait_ge(taken, i * B + (b + 1))
                        pool.indirect_dma_start(hh, feed1.at(b), ho[:, b, :], None, bounds_check=last, oob_is_err=False).then_inc(st1[b], 16)
                        pool.indirect_dma_start(al2, feed2.at(b), al[:, b, :], None, bounds_check=last, oob_is_err=False).then_inc(st2[b], 16)

                    indexed(pool, None, [], scatter, [feed1, feed2])
                    for q in st1 + st2:
                        pool.wait_ge(q, 16 * STEPS)

        attention("soft2", al2)
        rg2, ue2 = dram("rg2", (ROWS, D)), dram("ue2", (ROWS, D))
        edge_sum("gat2", "d", hh, N, dst_runs["other"], D, rg2, False, weights=w_edge)
        attention_ends("gat2_ends", rg2, hh, D, ue2, stat2, None)

        def batch_norm(tag, stats, gamma, beta, b, scale, shift, rows):
            with phase(nc, tag) as (sem, sb_, ps):
                tmp = sb_("tmp", [P, 6, 2])
                cols = sb_("cols", [P, 3, 2])
                stat = sb_("stat", [P, 4])
                diag = sb_("diag", [P, 4, P])
                p_r = ps("r", [P, 512])
                loaded, own, diag_made, rowed = (sem(n) for n in ("loaded", "own", "diag_made", "rowed"))
                params = [gamma, beta] + ([b] if b is not None else [])
                gate = sem("gate")
                with nc.Block() as block:
                    @block.sync
                    def _(sp):
                        for k, x in enumerate(params):
                            for c in range(2):
                                sp.dma_start(cols[:, k, c:c + 1], x[c * P:(c + 1) * P].rearrange("(n o) -> n o", o=1)).then_inc(loaded, 16)
                        sp.wait_ge(loaded, 32 * len(params))

                    @block.tensor
                    def _(pe):
                        pe.wait_ge(diag_made, 1)
                        for k in range(4):
                            m = pe.matmul(p_r[:, k * P:(k + 1) * P], ones[:], diag[:, k, :], start=True, stop=True)
                        m.then_inc(rowed, 1)

                    @block.vector
                    def _(dve):
                        c_ = Chain(dve, own, gate)
                        dve.wait_ge(loaded, 32 * len(params))
                        total = stats[0]
                        if len(stats) > 1:
                            c_(dve.tensor_tensor(stat[:], stats[0][:], stats[1][:], ALU.add))
                            total = stat
                        batch_scale(c_, total[:, 0:2], total[:, 2:4], cols[:, 0, :], cols[:, 1, :], cols[:, 2, :] if b is not None else zeros[:, 0:2],
                                    scale[:], shift[:], [tmp[:, k, :] for k in range(6)])
                        for k in range(4):
                            c_(dve.tensor_scalar(diag[:, k, :], ident[:], (scale, shift)[k // 2][:, k % 2:k % 2 + 1], None, ALU.mult))
                        dve.sem_inc(diag_made, 1)
                        dve.wait_ge(rowed, 1)
                        c_(dve.tensor_copy(rows[:].rearrange("p k c -> p (k c)"), p_r[:]))

        scale2, shift2, rows2 = sb("scale2", [P, 2]), sb("shift2", [P, 2]), sb("rows2", [P, 2, D])
        batch_norm("norm2", [stat2a, stat2], a["L2_gnn_g2"], a["L2_gnn_beta2"], a["L2_gnn_b2"], scale2, shift2, rows2)

        x3 = dram("x3", (N, D))
        with phase(nc, "seventh") as (sem, sb_, ps):
            h_in = sb_("h_in", [P, 2, J, D])
            x_in = sb_("x_in", [P, 2, J, D])
            low, ex = sb_("low", [P, 2, J, D]), sb_("ex", [P, 2, J, D])
            y = sb_("y", [P, J, D])
            xo = sb_("xo", [P, 2, J, D])
            st = norm_buffers(sb_, J)
            got_h, got_x, stored = (sem.many(n, 2) for n in ("got_h", "got_x", "stored"))
            own, low_made, exped, made = (sem(n) for n in ("own", "low_made", "exped", "made"))
            gate = sem("gate")
            with nc.Block() as block:
                @block.sync
                def _(sp):
                    def load(i, s, p, j):
                        wait(sp, made, i * 2 + (s - 1))
                        sp.dma_start(h_in[0:p, s, 0:j, :], group(hh, i, s, p, j)).then_inc(got_h[s], 16)
                        sp.dma_start(x_in[0:p, s, 0:j, :], group(x2, i, s, p, j)).then_inc(got_x[s], 16)

                    pairs(sp, [(load, 0)])

                @block.scalar
                def _(act):
                    def exp(i, s, p, j):
                        act.wait_ge(low_made, i * 2 + (s + 1))
                        wait(act, made, i * 2 + (s - 1))
                        act.activation(ex[0:p, s, 0:j, :], low[0:p, s, 0:j, :], ACT.Exp).then_inc(exped, 1)

                    pairs(act, [(exp, 0)])

                @block.vector
                def _(dve):
                    c_ = Chain(dve, own, gate)

                    def norm(i, s, p, j):
                        dve.wait_ge(got_h[s], i * 16 + 16)
                        wait(dve, exped, i * 2 + (s - 1))
                        h = h_in[0:p, s, 0:j, :]
                        row = lambda k: rows2[0:p, k, :].unsqueeze(1).to_broadcast([p, j, D])
                        c_(dve.tensor_tensor(h, h, row(0), ALU.mult))
                        c_(dve.tensor_tensor(h, h, row(1), ALU.add))
                        dve.tensor_scalar(low[0:p, s, 0:j, :], h, 0.0, None, ALU.min).then_inc(low_made, 1)

                    def rest(i, s, p, j):
                        dve.wait_ge(exped, i * 2 + (s + 1))
                        dve.wait_ge(got_x[s], i * 16 + 16)
                        wait(dve, stored[s], i * 16)
                        c_(dve.scalar_tensor_tensor(y[0:p, 0:j, :], ex[0:p, s, 0:j, :], -1.0, h_in[0:p, s, 0:j, :], ALU.add, ALU.max))
                        c_(dve.tensor_tensor(y[0:p, 0:j, :], y[0:p, 0:j, :], x_in[0:p, s, 0:j, :], ALU.add))
                        layer_norm(c_, y, xo[:, s], st, p, j)
                        dve.sem_inc(made, 1)

                    pairs(dve, [(norm, 0), (rest, 1)], c_, 2 * (4 + 3 * J + 12))

                @block.gpsimd
                def _(pool):
                    def store(i, s, p, j):
                        pool.wait_ge(made, i * 2 + (s + 1))
                        settle(pool, gate)
                        pool.dma_start(group(x3, i, s, p, j), xo[0:p, s, 0:j, :]).then_inc(stored[s], 16)

                    pairs(pool, [(store, 0)])
                    pool.wait_ge(stored[0], 16 * (PAIRS + 1))
                    pool.wait_ge(stored[1], 16 * PAIRS)

        def node_ends(tag, g, rows_table, gathered, target, rows, elu):
            with phase(nc, tag) as (sem, sb_, ps):
                r_in = sb_("r_in", [P, B, D])
                xg = sb_("xg", [P, B, D])
                low = sb_("low", [P, 2, D])
                ex = sb_("ex", [P, 2, D])
                y = sb_("y", [P, 1, D])
                xo = sb_("xo", [P, B, D])
                idx, put = sb_("idx", [P, B], I32), sb_("put", [P, B], I32)
                st = norm_buffers(sb_, 1)
                loaded, got, stored = (sem.many(n, B) for n in ("loaded", "got", "stored"))
                fed, fed_put, own, low_made, exped, made = (sem(n) for n in ("fed", "fed_put", "own", "low_made", "exped", "made"))
                gate = sem("gate")
                with nc.Block() as block:
                    @block.sync
                    def _(sp):
                        def load(i, b):
                            wait(sp, made, i * B + (b + 1 - B))
                            sp.dma_start(r_in[:, b, :], rows_table[bass.ds(i * (B * P) + b * P, P), :]).then_inc(loaded[b], 16)

                        columns(sp, [(load, 0)])

                    @block.gpsimd
                    def _(pool):
                        last = pool.to_reg(N - 1)
                        feed = Feed(pool, gate, fed, idx, g["node"], got)
                        feed_put = Feed(pool, gate, fed_put, put, g["put"], stored)

                        def gather(i, b):
                            wait(pool, made, i * B + (b + 1 - B))
                            pool.indirect_dma_start(xg[:, b, :], None, gathered, feed.at(b), bounds_check=last, oob_is_err=False).then_inc(got[b], 16)

                        def scatter(i, b):
                            pool.wait_ge(made, i * B + (b + 1))
                            pool.indirect_dma_start(target, feed_put.at(b), xo[:, b, :], None, bounds_check=last, oob_is_err=False).then_inc(stored[b], 16)

                        indexed(pool, gather, [feed], scatter, [feed_put])
                        for q in stored:
                            pool.wait_ge(q, 16 * STEPS)

                    @block.scalar
                    def _(act):
                        def exp(i, b):
                            act.wait_ge(low_made, i * B + (b + 1))
                            wait(act, made, i * B + (b - 1))
                            act.activation(ex[:, b % 2, :], low[:, b % 2, :], ACT.Exp).then_inc(exped, 1)

                        if elu:
                            columns(act, [(exp, 0)])

                    @block.vector
                    def _(dve):
                        c_ = Chain(dve, own, gate)

                        def norm(i, b):
                            dve.wait_ge(loaded[b], i * 16 + 16)
                            if elu:
                                wait(dve, exped, i * B + (b - 1))
                            c_(dve.tensor_tensor(r_in[:, b, :], r_in[:, b, :], rows[:, 0, :], ALU.mult))
                            c_(dve.tensor_tensor(r_in[:, b, :], r_in[:, b, :], rows[:, 1, :], ALU.add))
                            if elu:
                                dve.tensor_scalar(low[:, b % 2, :], r_in[:, b, :], 0.0, None, ALU.min).then_inc(low_made, 1)

                        def rest(i, b):
                            if elu:
                                dve.wait_ge(exped, i * B + (b + 1))
                            dve.wait_ge(got[b], i * 16 + 16)
                            wait(dve, stored[b], i * 16)
                            if elu:
                                c_(dve.scalar_tensor_tensor(y[:, 0, :], ex[:, b % 2, :], -1.0, r_in[:, b, :], ALU.add, ALU.max))
                                c_(dve.tensor_tensor(y[:, 0, :], y[:, 0, :], xg[:, b, :], ALU.add))
                            else:
                                c_(dve.scalar_tensor_tensor(y[:, 0, :], r_in[:, b, :], 0.0, xg[:, b, :], ALU.max, ALU.add))
                            layer_norm(c_, y, xo[:, b:b + 1, :], st, P, 1)
                            dve.sem_inc(made, 1)

                        columns(dve, [(norm, 0), (rest, 1)], c_, B * (2 + (2 if elu else 1) + 15))

        node_ends("x3_ends", dst_runs, ue2, x2, x3, rows2, True)

        top = [dram(f"top{l}", (ROWS + 1, D)) for l in range(3)]
        wt, wp = sb("wt", [P, 3, 2, D]), sb("wp", [P, 3, 2, D])
        fixes = sb("fixes", [P, 1])
        whole_row = sb("whole_row", [P, P])
        with phase(nc, "maps") as (sem, sb_, ps):
            raw = sb_("raw", [P, 6, 2, D])
            diag = sb_("diag", [P, P])
            p_m = [ps(f"m{k}", [P, 2, D]) for k in range(6)]
            p_w = ps("w", [P, 512])
            loaded, own, turned, diag_made, rowed, stored = (sem(n) for n in ("loaded", "own", "turned", "diag_made", "rowed", "stored"))
            with nc.Block() as block:
                @block.sync
                def _(sp):
                    for l in range(3):
                        for k, n in enumerate(("L3_gnn_thetas", "L3_gnn_phis")):
                            sp.dma_start(raw[:, 2 * l + k], a[n][l].rearrange("(c p) f -> p c f", p=P)).then_inc(loaded, 16)
                    for table in top:
                        sp.dma_start(table[ROWS:ROWS + 1, :], zeros[0:1, 0:D]).then_inc(stored, 16)
                    sp.wait_ge(stored, 48)

                @block.tensor
                def _(pe):
                    pe.wait_ge(diag_made, 1)
                    pe.matmul(p_w[:, 0:P], ones[:], diag[:], start=True, stop=True).then_inc(rowed, 1)
                    pe.wait_ge(loaded, 96)
                    for m in range(6):
                        for c in range(2):
                            for f in range(2):
                                q = pe.transpose(p_m[m][:, f, c * P:(c + 1) * P], raw[:, m, c, f * P:(f + 1) * P], ident[:])
                    q.then_inc(turned, 1)

                @block.vector
                def _(dve):
                    dve.tensor_scalar(diag[:], ident[:], src_runs["whole"][:, 0:1], None, ALU.mult).then_inc(diag_made, 1)
                    dve.tensor_scalar(fixes[:], src_runs["fix_row"][:], float(ROWS), None, ALU.is_lt).then_inc(own, 1)
                    dve.wait_ge(rowed, 1)
                    dve.tensor_copy(whole_row[:], p_w[:, 0:P]).then_inc(own, 1)
                    dve.wait_ge(turned, 1)
                    for m in range(6):
                        dve.tensor_copy((wt, wp)[m % 2][:, m // 2], p_m[m][:]).then_inc(own, 1)
                    dve.wait_ge(own, 8)

        stat3 = sb("stat3", [P, 4])
        scale3, shift3, rows3 = sb("scale3", [P, 2]), sb("shift3", [P, 2]), sb("rows3", [P, 2, D])

        def edge_max(l, table, rows, own_index, other_index, target):
            g = src_runs
            with phase(nc, f"max{l}") as (sem, sb_, ps):
                xi, xj = sb_("xi", [P, B, D]), sb_("xj", [P, B, D])
                xt = sb_("xt", [P, 2, 2, 2, P])
                dt = sb_("dt", [P, 2, 2, P])
                total = sb_("total", [P, B, D])
                sq = sb_("sq", [P, 2, D])
                idx_i, idx_j = sb_("idx_i", [P, B], I32), sb_("idx_j", [P, B], I32)
                fix, fixed, fixed_sq = (sb_(n, [P, D]) for n in ("fix", "fixed", "fixed_sq"))
                flat = sb_("flat", [P, 2, P])
                state = sb_("state", [P, 2, P + 1])
                p_t = [ps(f"t{k}", [P, 2, 2, P]) for k in range(2)]
                p_y = [ps(f"y{k}", [P, 512]) for k in range(2)]
                p_s, p_f, p_c = ps("s", [P, 512]), ps("f", [P, 2, P]), ps("c", [P, 2, P])
                got_i, got_j, stored = (sem.many(n, B) for n in ("got_i", "got_j", "stored"))
                fed_i, fed_j, own, turned, copied, diffed, product, topped, squared, summed = (sem(n) for n in
                    ("fed_i", "fed_j", "own", "turned", "copied", "diffed", "product", "topped", "squared", "summed"))
                blank, fix_got, fix_ready, f_turned, f_scanned, f_back, f_squared = (sem(n) for n in
                    ("blank", "fix_got", "fix_ready", "f_turned", "f_scanned", "f_back", "f_squared"))
                gate = sem("gate")
                with nc.Block() as block:
                    @block.gpsimd
                    def _(pool):
                        last = pool.to_reg(rows - 1)
                        last_out = pool.to_reg(ROWS - 1)
                        feed_i = Feed(pool, gate, fed_i, idx_i, own_index, got_i)
                        feed_j = Feed(pool, gate, fed_j, idx_j, other_index, got_j)

                        def gather(i, b):
                            wait(pool, turned, i * B + (b + 1 - B))
                            pool.indirect_dma_start(xi[:, b, :], None, table, feed_i.at(b), bounds_check=last, oob_is_err=False).then_inc(got_i[b], 16)
                            pool.indirect_dma_start(xj[:, b, :], None, table, feed_j.at(b), bounds_check=last, oob_is_err=False).then_inc(got_j[b], 16)

                        indexed(pool, gather, [feed_i, feed_j])
                        for s in stored:
                            pool.wait_ge(s, 16 * STEPS)
                        pool.wait_ge(blank, 1)
                        at = bass.IndirectOffsetOnAxis(g["fix_row"][:, 0:1], 0)
                        pool.indirect_dma_start(fix[:], None, target, at, bounds_check=last_out, oob_is_err=False).then_inc(fix_got, 16)
                        pool.wait_ge(fix_ready, 1)
                        pool.indirect_dma_start(target, at, fixed[:], None, bounds_check=last_out, oob_is_err=False).then_inc(fix_got, 16)
                        pool.wait_ge(fix_got, 32)

                    @block.sync
                    def _(sp):
                        def store(i):
                            for b in range(B):
                                sp.wait_ge(topped, i * B + (b + 1))
                                sp.dma_start(target[bass.ds(i * (B * P) + b * P, P), :], total[:, b, :]).then_inc(stored[b], 16)

                        steps(sp, STEPS, store)

                    @block.tensor
                    def _(pe):
                        def turn(i, b):
                            pe.wait_ge(got_i[b], i * 16 + 16)
                            pe.wait_ge(got_j[b], i * 16 + 16)
                            wait(pe, copied, i * B + (b - 1))
                            for c in range(2):
                                for k, x in enumerate((xi, xj)):
                                    m = pe.transpose(p_t[b % 2][:, c, k, :], x[:, b, c * P:(c + 1) * P], ident[:])
                            m.then_inc(turned, 1)

                        def mul(i, b):
                            pe.wait_ge(diffed, i * B + (b + 1))
                            wait(pe, topped, i * B + (b - 1))
                            for c in range(2):
                                pe.matmul(p_y[b % 2][:, 0:D], xt[:, b % 2, c, 0, :], wp[:, l, c, :], start=(c == 0), stop=False)
                            for c in range(2):
                                m = pe.matmul(p_y[b % 2][:, 0:D], dt[:, b % 2, c, :], wt[:, l, c, :], start=False, stop=(c == 1))
                            m.then_inc(product, 1)

                        def add(i, b):
                            t = i * B + b
                            pe.wait_ge(squared, t + 1)
                            settle(pe, gate)
                            for k in range(4):
                                buf = total[:, b, (k % 2) * P:(k % 2 + 1) * P] if k < 2 else sq[:, b % 2, (k % 2) * P:(k % 2 + 1) * P]
                                m = pe.matmul(p_s[:, k:k + 1], buf, g["inner"][:, bass.ds(t, 1)], start=(isinstance(i, int) and i == 0 and b == 0 and k == 0),
                                              stop=False, skip_group_check=True)
                            m.then_inc(summed, 1)

                        columns(pe, [(turn, 0), (mul, 1), (add, 3)])
                        pe.wait_ge(topped, T)
                        for c in range(2):
                            m = pe.transpose(p_f[:, c, :], total[:, B - 1, c * P:(c + 1) * P], ident[:])
                        m.then_inc(f_turned, 1)
                        pe.wait_ge(f_scanned, 1)
                        for c in range(2):
                            m = pe.transpose(p_c[:, c, :], state[:, c, 0:P], ident[:])
                        m.then_inc(f_back, 1)
                        pe.wait_ge(f_squared, 1)
                        for k in range(4):
                            buf = (fixed, fixed_sq)[k // 2][:, (k % 2) * P:(k % 2 + 1) * P]
                            m = pe.matmul(p_s[:, k:k + 1], buf, fixes[:], start=False, stop=(k == 3), skip_group_check=True)
                        m.then_inc(summed, 1)

                    @block.scalar
                    def _(act):
                        def copy(i, b):
                            act.wait_ge(turned, i * B + (b + 1))
                            wait(act, product, i * B + (b - 1))
                            if l == 0:
                                act.activation(xt[:, b % 2], p_t[b % 2][:], ACT.Copy).then_inc(copied, 1)
                            else:
                                for c in range(2):
                                    m = act.activation(xt[:, b % 2, c], p_t[b % 2][:, c], ACT.Relu, scale=scale3[:, c:c + 1], bias=shift3[:, c:c + 1])
                                m.then_inc(copied, 1)

                        def square(i, b):
                            act.wait_ge(topped, i * B + (b + 1))
                            wait(act, summed, i * B + (b - 1))
                            act.activation(sq[:, b % 2, :], total[:, b, :], ACT.Square).then_inc(squared, 1)

                        columns(act, [(copy, 0), (square, 3)])
                        act.wait_ge(fix_ready, 1)
                        act.activation(fixed_sq[:], fixed[:], ACT.Square).then_inc(f_squared, 1)

                    @block.vector
                    def _(dve):
                        c_ = Chain(dve, own, gate)
                        c_(dve.memset(total[:, B - 1, :], 0.0))
                        c_(dve.memset(state[:], 0.0))
                        dve.memset(fix[:], 0.0).then_inc(blank, 1)

                        def diff(i, b):
                            dve.wait_ge(copied, i * B + (b + 1))
                            wait(dve, product, i * B + (b - 1))
                            dve.tensor_tensor(dt[:, b % 2], xt[:, b % 2, :, 1, :], xt[:, b % 2, :, 0, :], ALU.subtract).then_inc(diffed, 1)

                        def most(i, b):
                            t = i * B + b
                            dve.wait_ge(product, t + 1)
                            wait(dve, stored[b], i * 16)
                            wait(dve, summed, i * B + (b + 1 - B))
                            wait(dve, topped, t)
                            dve.scalar_tensor_tensor(total[:, b, :], total[:, (b - 1) % B, :], g["cont"][:, bass.ds(t, 1)],
                                                     p_y[b % 2][:, 0:D], ALU.mult, ALU.max).then_inc(topped, 1)

                        columns(dve, [(diff, 0), (most, 2)])
                        dve.wait_ge(f_turned, 1)
                        c_(dve.tensor_copy(flat[:], p_f[:]))
                        for c in range(2):
                            c_(dve.tensor_tensor_scan(state[:, c, 1:P + 1], whole_row[:], flat[:, c, :], 0.0, ALU.add, ALU.max))
                        dve.sem_inc(f_scanned, 1)
                        dve.wait_ge(f_back, 1)
                        dve.wait_ge(fix_got, 16)
                        dve.tensor_tensor(fixed[:], fix[:], p_c[:].rearrange("p c q -> p (c q)"), ALU.max).then_inc(fix_ready, 1)
                        dve.wait_ge(summed, T + 1)
                        c_(dve.tensor_copy(stat3[:], p_s[:, 0:4]))

            batch_norm(f"norm3_{l}", [stat3], a["L3_gnn_gammas"][l], a["L3_gnn_betas"][l], None, scale3, shift3, rows3)

        edge_max(0, x3, N, src_runs["node"], src_runs["other"], top[0])
        edge_max(1, top[0], ROWS + 1, own_row, other_row, top[1])
        edge_max(2, top[1], ROWS + 1, own_row, other_row, top[2])

        with phase(nc, "last") as (sem, sb_, ps):
            x_in = sb_("x_in", [P, 2, J, D])
            xo = sb_("xo", [P, 2, J, D])
            floor = sb_("floor", [P, D])
            st = norm_buffers(sb_, J)
            got, stored = sem.many("got", 2), sem.many("stored", 2)
            own, made = sem("own"), sem("made")
            gate = sem("gate")
            with nc.Block() as block:
                @block.sync
                def _(sp):
                    def load(i, s, p, j):
                        wait(sp, made, i * 2 + (s - 1))
                        sp.dma_start(x_in[0:p, s, 0:j, :], group(x3, i, s, p, j)).then_inc(got[s], 16)

                    pairs(sp, [(load, 0)])

                @block.vector
                def _(dve):
                    c_ = Chain(dve, own, gate)
                    c_(dve.tensor_scalar(floor[:], rows3[:, 1, :], 0.0, None, ALU.max))

                    def node(i, s, p, j):
                        dve.wait_ge(got[s], i * 16 + 16)
                        wait(dve, stored[s], i * 16)
                        x = x_in[0:p, s, 0:j, :]
                        c_(dve.tensor_tensor(x, x, floor[0:p, :].unsqueeze(1).to_broadcast([p, j, D]), ALU.add))
                        layer_norm(c_, x_in[:, s], xo[:, s], st, p, j)
                        dve.sem_inc(made, 1)

                    pairs(dve, [(node, 0)], c_, 2 * (1 + 3 * J + 12))

                @block.gpsimd
                def _(pool):
                    def store(i, s, p, j):
                        pool.wait_ge(made, i * 2 + (s + 1))
                        settle(pool, gate)
                        pool.dma_start(group(out, i, s, p, j), xo[0:p, s, 0:j, :]).then_inc(stored[s], 16)

                    pairs(pool, [(store, 0)])
                    pool.wait_ge(stored[0], 16 * (PAIRS + 1))
                    pool.wait_ge(stored[1], 16 * PAIRS)

        node_ends("out_ends", src_runs, top[2], x3, out, rows3, False)


_NAMES = ['x', 'src', 'dst', 'L0_gnn_W1', 'L0_gnn_b1', 'L0_gnn_W2', 'L0_gnn_b2', 'L1_gnn_W1', 'L1_gnn_b1', 'L1_gnn_W2', 'L1_gnn_b2', 'L1_gnn_a', 'L2_gnn_W_gcn', 'L2_gnn_b_gcn', 'L2_gnn_g0', 'L2_gnn_beta0', 'L2_gnn_W1', 'L2_gnn_a_src1', 'L2_gnn_a_dst1', 'L2_gnn_b1', 'L2_gnn_g1', 'L2_gnn_beta1', 'L2_gnn_W2', 'L2_gnn_a_src2', 'L2_gnn_a_dst2', 'L2_gnn_b2', 'L2_gnn_g2', 'L2_gnn_beta2', 'L3_gnn_thetas', 'L3_gnn_phis', 'L3_gnn_gammas', 'L3_gnn_betas']


def kernel(**inputs):
    import numpy as np
    import concourse.bacc as bacc
    from concourse.bass_utils import run_bass_kernel_spmd

    nc = bacc.Bacc("TRN2", target_bir_lowering=False, num_devices=1)
    arrays, aps = {}, {}
    for name in _NAMES:
        array = np.ascontiguousarray(inputs[name])
        arrays[f"in_{name}"] = array
        aps[name] = nc.dram_tensor(f"in_{name}", array.shape, mybir.dt.from_np(array.dtype), kind="ExternalInput").ap()
    out = nc.dram_tensor("out", (N, D), F32, kind="ExternalOutput").ap()
    program(nc, aps, out)
    result = run_bass_kernel_spmd(nc, [arrays], core_ids=[0])
    return result.results[0]["out"]
```

```python
from contextlib import ExitStack, contextmanager

import concourse.bass as bass
from concourse import mybir
from concourse.alu_op_type import AluOpType as ALU

F32 = mybir.dt.float32
I32 = mybir.dt.int32
ACT = mybir.ActivationFunctionType

P = 128
N = 50000
E = 25000
D = 256
T = 196
B = 14
STEPS = T // B
HALF = B // 2
ROWS = T * P
HID = 64
HEADS = 4
J = 3
JB = 5
GROUP = P * J
PAIRS = N // (2 * GROUP)
TAIL = N - PAIRS * 2 * GROUP
PADKEY = 50175
SKIP = 100000
NEG = -1.0e30
EPS = 1e-5
RADIX = 256


def wait(eng, sem, value):
    if isinstance(value, int) and value <= 0:
        return
    eng.wait_ge(sem, value)


class Chain:

    def __init__(self, eng, sem, gate=None):
        self.eng, self.sem, self.gate, self.base, self.n = eng, sem, gate, 0, 0

    def __call__(self, ins):
        self.n += 1
        ins.then_inc(self.sem, 1)
        self.eng.wait_ge(self.sem, self.base + self.n)

    def mark(self, ins):
        self.n += 1
        ins.then_inc(self.sem, 1)

    def sync(self):
        self.eng.wait_ge(self.sem, self.base + self.n)

    def upto(self, n):
        wait(self.eng, self.sem, self.base + n)


def steps(eng, count, body, chain=None):
    n0 = chain.n if chain else 0
    assert not chain or isinstance(chain.base, int)
    body(0)
    if chain:
        per, start = chain.n - n0, chain.base + n0
    with eng.Fori(1, count) as i:
        if chain:
            chain.base, chain.n = i * per + start, 0
        body(i)
        assert not chain or chain.n == per
    if chain:
        chain.base, chain.n = start + count * per, 0


class Sems:

    def __init__(self, nc, ctx, tag):
        self.nc, self.ctx, self.tag, self.all = nc, ctx, tag, []

    def __call__(self, name):
        s = self.ctx.enter_context(self.nc.semaphore(f"{self.tag}_{name}"))
        self.all.append(s)
        return s

    def many(self, name, n):
        return [self(f"{name}{i}") for i in range(n)]


@contextmanager
def phase(nc, tag):
    with ExitStack() as ctx:
        sems = Sems(nc, ctx, tag)

        def sb(name, shape, dt=F32):
            return ctx.enter_context(nc.sbuf_tensor(f"{tag}_{name}", shape, dt))

        def ps(name, shape):
            return ctx.enter_context(nc.psum_tensor(f"{tag}_{name}", shape, F32))

        yield sems, sb, ps
        nc.all_engine_barrier()
        nc.gpsimd.dma_reset()
        for s in sems.all:
            nc.gpsimd.sem_clear(s)
        nc.all_engine_barrier()


def columns(eng, stages, chain=None, per=0):
    def body(i):
        for b in range(B):
            for fn, lag in stages:
                if b >= lag:
                    fn(i, b - lag)
                elif not (isinstance(i, int) and i == 0):
                    fn(i - 1, b - lag + B)

    peel = 2 if max(lag for _, lag in stages) else 1
    for i in range(peel):
        body(i)
    start = (chain.base + chain.n) if chain else 0
    with eng.Fori(peel, STEPS) as i:
        if chain:
            chain.base, chain.n = (i - peel) * per + start, 0
        body(i)
        assert not chain or chain.n == per, chain.n
    if chain:
        chain.base, chain.n = start + (STEPS - peel) * per, 0
    for x in range(max(lag for _, lag in stages)):
        for fn, lag in stages:
            if lag > x:
                fn(STEPS - 1, B - lag + x)


def pairs(eng, stages, chain=None, per=0, j=J):
    count = pair_count(j)

    def step(i, s):
        for fn, lag in stages:
            back, s_ = (s - lag) // 2, (s - lag) % 2
            if not (isinstance(i, int) and i + back < 0):
                fn(i + back if back else i, s_, P, j)

    most = max(lag for _, lag in stages)
    peel = 1 + (most + 1) // 2
    for i in range(peel):
        step(i, 0)
        step(i, 1)
    start = (chain.base + chain.n) if chain else 0
    with eng.Fori(peel, count) as i:
        if chain:
            chain.base, chain.n = (i - peel) * per + start, 0
        step(i, 0)
        step(i, 1)
        assert not chain or chain.n == per, chain.n
    if chain:
        chain.base, chain.n = start + (count - peel) * per, 0
    for x in range(most + 1):
        for fn, lag in stages:
            at = 2 * count + x - lag
            if x <= lag:
                fn(at // 2, at % 2, *((TAIL, 1) if x == lag else (P, j)))


def pair_count(j):
    return N // (2 * P * j)


def group(table, i, s, p, j):
    if p == TAIL:
        return table[N - TAIL:N, :].rearrange("(p j) c -> p j c", j=1)
    return table[bass.ds(i * (2 * P * j) + s * (P * j), P * j), :].rearrange("(p j) c -> p j c", j=j)


def settle(eng, gate):
    eng.sem_inc(gate, 1)


class Feed:

    def __init__(self, pool, gate, sem, slots, source, done):
        self.pool, self.sem, self.slots, self.source, self.done = pool, sem, slots, source, done
        self.gate = gate

    def __call__(self, i, h):
        lo, hi = h * HALF, (h + 1) * HALF
        for b in range(lo, hi):
            wait(self.pool, self.done[b], i * 16)
        settle(self.pool, self.gate)
        self.pool.tensor_copy(self.slots[:, lo:hi], self.source[:, bass.ds(i * B + lo, HALF)]).then_inc(self.sem, 1)
        self.pool.wait_ge(self.sem, i * 2 + (h + 1))

    def at(self, b):
        settle(self.pool, self.gate)
        return bass.IndirectOffsetOnAxis(self.slots[:, b:b + 1], 0)


def indexed(pool, gather=None, gather_feeds=(), scatter=None, scatter_feeds=(), behind=1):
    def half(i, h, j, k):
        for f in gather_feeds:
            f(i, h)
        if j is not None:
            for f in scatter_feeds:
                f(j, k)
        for b in range(HALF):
            if gather:
                gather(i, h * HALF + b)
            if j is not None:
                scatter(j, k * HALF + b)

    def body(i):
        if scatter:
            first = isinstance(i, int)
            if behind == 1:
                half(i, 0, None if first else i - 1, 1)
                half(i, 1, i, 0)
            else:
                for h in range(2):
                    half(i, h, None if first else i - 1, h)
        else:
            half(i, 0, None, 0)
            half(i, 1, None, 0)

    steps(pool, STEPS, body)
    if scatter:
        for h in range(2 - behind, 2):
            for f in scatter_feeds:
                f(STEPS - 1, h)
            for b in range(h * HALF, (h + 1) * HALF):
                scatter(STEPS - 1, b)


def rstd_steps(chain, v, y, t, u):
    dve = chain.eng
    chain(dve.tensor_scalar(t.bitcast(I32), v.bitcast(I32), 1, None, ALU.logical_shift_right))
    chain(dve.tensor_scalar(y.bitcast(I32), t.bitcast(I32), -1.0, float(0x5F3759DF), ALU.mult, ALU.add))
    for _ in range(3):
        chain(dve.tensor_tensor(t, y, y, ALU.mult))
        chain(dve.scalar_tensor_tensor(u, t, -0.5, v, ALU.mult, ALU.mult))
        chain(dve.scalar_tensor_tensor(y, u, 1.5, y, ALU.add, ALU.mult))


def layer_norm(chain, x, y, st, p, j):
    dve = chain.eng
    for k in range(j):
        chain.mark(dve.bn_stats(st["part"][0:p, k, :], x[0:p, k, :]))
    chain.sync()
    settle(dve, chain.gate)
    for k in range(j):
        chain.mark(dve.bn_aggr(st["mean"][0:p, k, :], st["part"][0:p, k, :]))
    chain.sync()
    chain(dve.tensor_scalar(st["var"][0:p, 0:j], st["mean"][0:p, 0:j, 1], EPS, None, ALU.add))
    rstd_steps(chain, st["var"][0:p, 0:j], st["rstd"][0:p, 0:j], st["t"][0:p, 0:j], st["u"][0:p, 0:j])
    for k in range(j):
        chain.mark(dve.tensor_scalar(y[0:p, k, :], x[0:p, k, :], st["mean"][0:p, k, 0:1], st["rstd"][0:p, k:k + 1], ALU.subtract, ALU.mult))
    chain.sync()


def norm_slots(sb, name, j):
    return {"part": sb(name + "part", [P, j, 6]), "mean": sb(name + "mean", [P, j, 2]), "var": sb(name + "var", [P, j]),
            "t": sb(name + "t", [P, j]), "u": sb(name + "u", [P, j]), "rstd": sb(name + "rstd", [P, 2, j]), "bias": sb(name + "bias", [P, 2, j])}


def norm_stats(chain, x, st, s, p, j):
    dve = chain.eng
    for k in range(j):
        chain.mark(dve.bn_stats(st["part"][0:p, k, :], x[0:p, k, :]))
    chain.sync()
    settle(dve, chain.gate)
    for k in range(j):
        chain.mark(dve.bn_aggr(st["mean"][0:p, k, :], st["part"][0:p, k, :]))
    chain.sync()
    rstd = st["rstd"][0:p, s, 0:j]
    chain(dve.tensor_scalar(st["var"][0:p, 0:j], st["mean"][0:p, 0:j, 1], EPS, None, ALU.add))
    rstd_steps(chain, st["var"][0:p, 0:j], rstd, st["t"][0:p, 0:j], st["u"][0:p, 0:j])
    chain(dve.scalar_tensor_tensor(st["bias"][0:p, s, 0:j], st["mean"][0:p, 0:j, 0], -1.0, rstd, ALU.mult, ALU.mult))


def normalize(act, x, y, st, s, p, j):
    for k in range(j):
        m = act.activation(y[0:p, k, :], x[0:p, k, :], ACT.Identity, scale=st["rstd"][0:p, s, k:k + 1], bias=st["bias"][0:p, s, k:k + 1])
    return m


def norm_buffers(sb, j):
    return {"part": sb("part", [P, j, 6]), "mean": sb("mean", [P, j, 2]), "var": sb("var", [P, j]),
            "rstd": sb("rstd", [P, j]), "t": sb("nt", [P, j]), "u": sb("nu", [P, j])}


def program(nc, a, out):
    with ExitStack() as ctx:
        def sb(name, shape, dt=F32):
            return ctx.enter_context(nc.sbuf_tensor(name, shape, dt))

        def dram(name, shape, dt=F32):
            return nc.dram_tensor(name, shape, dt).ap()

        nt = dram("node_counts", (2 * N, 2))
        dm = dram("node_scale", (N, 2))
        srt = {o: [dram(f"sorted_{o}{k}", (ROWS + 2, 2), I32) for k in range(2)] for o in "ds"}

        iota = sb("iota", [P, RADIX])
        pcol = sb("pcol", [P, 1])
        ident = sb("ident", [P, P])
        below = sb("below", [P, P])
        ones = sb("ones", [P, P])
        zeros = sb("zeros", [P, 2 * D])

        agg = [dram(f"agg{k}", (N, HID)) for k in range(3)]
        with phase(nc, "init") as (sem, _, _):
            made, zeroed = sem("made"), sem("zeroed")
            gate = sem("gate")
            with nc.Block() as block:
                @block.gpsimd
                def _(pool):
                    pool.iota(iota[:], [[1, RADIX]], 0, 0, allow_small_or_imprecise_dtypes=True).then_inc(made, 1)
                    pool.iota(pcol[:], [[0, 1]], 0, 1, allow_small_or_imprecise_dtypes=True).then_inc(made, 1)
                    pool.wait_ge(made, 2)

                @block.vector
                def _(dve):
                    dve.memset(zeros[:], 0.0).then_inc(zeroed, 1)
                    dve.memset(ones[:], 1.0).then_inc(zeroed, 1)
                    dve.wait_ge(made, 2)
                    dve.tensor_scalar(ident[:], iota[:, 0:P], pcol[:], None, ALU.is_equal).then_inc(zeroed, 1)
                    dve.tensor_scalar(below[:], iota[:, 0:P], pcol[:], None, ALU.is_gt).then_inc(zeroed, 1)
                    dve.wait_ge(zeroed, 4)

        def radix_pass(k):
            with phase(nc, f"sort{k}") as (sem, sb, ps):
                both = lambda make: {o: make(o) for o in "ds"}
                kv = both(lambda o: sb(f"kv_{o}", [P, T, 2], I32))
                raw = both(lambda o: sb(f"raw_{o}", [P, 2, T], I32))
                digit_i = both(lambda o: sb(f"digit_i_{o}", [P, T], I32))
                digit = both(lambda o: sb(f"digit_{o}", [P, T]))
                seen = both(lambda o: sb(f"seen_{o}", [P, 2, RADIX]))
                total = both(lambda o: sb(f"total_{o}", [P, RADIX]))
                start = both(lambda o: sb(f"start_{o}", [P, RADIX + 1]))
                junk = both(lambda o: sb(f"junk_{o}", [P, RADIX]))
                place = both(lambda o: sb(f"place_{o}", [P, B]))
                place_i = both(lambda o: sb(f"place_i_{o}", [P, B], I32))
                row = both(lambda o: sb(f"row_{o}", [P, B, 2], I32))
                edge = sb("edge", [P, 2], I32)
                p_before = both(lambda o: ps(f"before_{o}", [P, 512]))
                p_total = both(lambda o: ps(f"total_ps_{o}", [P, 512]))
                own, counted, padded = sem("own"), sem("counted"), sem("padded")
                loaded = both(lambda o: sem(f"loaded_{o}"))
                edged, cleared = sem("edged"), sem("cleared")
                summed = both(lambda o: sem(f"summed_{o}"))
                ranked = both(lambda o: sem(f"ranked_{o}"))
                placed = both(lambda o: sem.many(f"placed_{o}", B))
                ends = {"d": ("dst", "src"), "s": ("src", "dst")}
                whole, rest = E // T, E % T

                gate = sem("gate")
                with nc.Block() as block:
                    @block.sync
                    def _(sp):
                        if k == 0:
                            sp.wait_ge(padded, 2)
                            for o in "ds":
                                for c, name in enumerate(ends[o]):
                                    sp.dma_start(raw[o][0:whole, c, :], a[name][0:whole * T].rearrange("(p t) -> p t", t=T)).then_inc(loaded[o], 16)
                                    sp.dma_start(raw[o][whole:whole + 1, c, 0:rest], a[name][whole * T:E].rearrange("(p t) -> p t", p=1)).then_inc(loaded[o], 16)
                            for table in agg:
                                rows = table.rearrange("(p r) c -> p r c", p=80)
                                sp.dma_start(rows, zeros[0:80, 0:HID].unsqueeze(1).to_broadcast([80, N // 80, HID])).then_inc(cleared, 16)
                            rows = nt.rearrange("(p r) c -> p (r c)", p=80)
                            for q in range(0, 4 * N // 80, 500):
                                sp.dma_start(rows[:, q:q + 500], zeros[0:80, 0:500]).then_inc(cleared, 16)
                            sp.wait_ge(cleared, 16 * 8)
                        else:
                            for o in "ds":
                                sp.dma_start(kv[o][:], srt[o][0][1:ROWS + 1, :].rearrange("(p t) c -> p t c", t=T)).then_inc(loaded[o], 16)
                            sp.wait_ge(padded, 1)
                            for o in "ds":
                                for at in (0, ROWS + 1):
                                    sp.dma_start(srt[o][1][at:at + 1, :], edge[0:1, :]).then_inc(edged, 16)
                            sp.wait_ge(edged, 64)

                    @block.vector
                    def _(dve):
                        own_ = Chain(dve, own, gate)
                        if k == 0:
                            for o in "ds":
                                own_(dve.memset(raw[o][:, 1, :], 0))
                                dve.memset(raw[o][:, 0, :], PADKEY).then_inc(padded, 1)
                            for o in "ds":
                                dve.wait_ge(loaded[o], 64)
                                own_(dve.tensor_copy(kv[o][:, :, 0], raw[o][:, 0, :]))
                                own_(dve.tensor_copy(kv[o][:, :, 1], raw[o][:, 1, :]))
                                own_(dve.tensor_scalar(digit_i[o][:], kv[o][:, :, 0], RADIX - 1, None, ALU.bitwise_and))
                        else:
                            dve.memset(edge[:], -1).then_inc(padded, 1)
                            for o in "ds":
                                dve.wait_ge(loaded[o], 16)
                                own_(dve.tensor_scalar(digit_i[o][:], kv[o][:, :, 0], 8, None, ALU.logical_shift_right))
                        for o in "ds":
                            own_(dve.tensor_copy(digit[o][:], digit_i[o][:]))
                            own_(dve.memset(seen[o][:], 0.0))

                        def count(i):
                            for b in range(B):
                                for o in "ds":
                                    own_.mark(dve.scalar_tensor_tensor(seen[o][:, 1 - b % 2, :], iota[:], digit[o][:, bass.ds(i * B + b, 1)],
                                                                       seen[o][:, b % 2, :], ALU.is_equal, ALU.add))
                                    own_.upto(own_.n - 1)
                            own_.sync()

                        steps(dve, STEPS, count, own_)
                        dve.sem_inc(counted, 1)
                        for o in "ds":
                            dve.wait_ge(summed[o], 1)
                            own_(dve.memset(start[o][:, 0:1], 0.0))
                            own_(dve.tensor_copy(total[o][:], p_total[o][:, 0:RADIX]))
                            own_(dve.tensor_tensor_scan(start[o][:, 1:RADIX + 1], ones[:, 0:1].to_broadcast([P, RADIX]), total[o][:], 0.0, ALU.mult, ALU.add))
                            own_(dve.scalar_tensor_tensor(seen[o][:, 0, :], start[o][:, 0:RADIX], 1.0, p_before[o][:, 0:RADIX], ALU.add, ALU.add))

                        def rank(i):
                            for b in range(B):
                                t = i * B + b
                                d = {o: digit[o][:, bass.ds(t, 1)] for o in "ds"}
                                for o in "ds":
                                    own_.mark(dve.scalar_tensor_tensor(junk[o][:], iota[:], d[o], seen[o][:, b % 2, :], ALU.is_equal, ALU.mult, accum_out=place[o][:, b:b + 1]))
                                for o in "ds":
                                    own_.mark(dve.scalar_tensor_tensor(seen[o][:, 1 - b % 2, :], iota[:], d[o], seen[o][:, b % 2, :], ALU.is_equal, ALU.add))
                                for o in "ds":
                                    wait(dve, placed[o][b], i * 16)
                                    own_.mark(dve.tensor_copy(row[o][:, b, :], kv[o][:, bass.ds(t, 1), :].rearrange("p a c -> p (a c)")))
                                own_.upto(own_.n - 4)
                                for o in "ds":
                                    dve.tensor_copy(place_i[o][:, b:b + 1], place[o][:, b:b + 1]).then_inc(ranked[o], 1)
                                own_.upto(own_.n - 2)
                            own_.sync()

                        steps(dve, STEPS, rank, own_)

                    @block.tensor
                    def _(pe):
                        pe.wait_ge(counted, 1)
                        for o in "ds":
                            pe.matmul(p_before[o][:, 0:RADIX], below[:], seen[o][:, 0, :], start=True, stop=True)
                            pe.matmul(p_total[o][:, 0:RADIX], ones[:], seen[o][:, 0, :], start=True, stop=True).then_inc(summed[o], 1)

                    @block.gpsimd
                    def _(pool):
                        last_row = pool.to_reg(ROWS)

                        def scatter(i):
                            for b in range(B):
                                for o in "ds":
                                    pool.wait_ge(ranked[o], i * B + (b + 1))
                                    settle(pool, gate)
                                    pool.indirect_dma_start(srt[o][k], bass.IndirectOffsetOnAxis(place_i[o][:, b:b + 1], 0), row[o][:, b, :], None,
                                                            bounds_check=last_row, oob_is_err=False).then_inc(placed[o][b], 16)

                        steps(pool, STEPS, scatter)
                        for s in placed["d"] + placed["s"]:
                            pool.wait_ge(s, 16 * STEPS)

        for k in range(2):
            radix_pass(k)

        def structure(o):
            g = {}
            for n in ("cont", "pen", "rpen", "endm", "count", "inverse"):
                g[n] = sb(f"{n}_{o}", [P, T])
            for n in ("node", "other", "put"):
                g[n] = sb(f"{n}_{o}", [P, T], I32)
            g["whole"] = sb(f"whole_{o}", [P, 2])
            g["carry"] = sb(f"carry_{o}", [P, P])
            g["fix_row"] = sb(f"fix_row_{o}", [P, 1], I32)
            g["fix_node"] = sb(f"fix_node_{o}", [P, 1], I32)
            g["inner"] = sb(f"inner_{o}", [P, T])
            with phase(nc, f"runs_{o}") as (sem, sb_, ps):
                kv = sb_("kv", [P, 3, T, 2], I32)
                at = sb_("at", [P, 3, T])
                same_next = sb_("same_next", [P, T])
                row = sb_("row", [P, T])
                real = sb_("real", [P, T])
                off = sb_("off", [P, T])
                raw = sb_("raw", [P, T])
                small = sb_("small", [P, 8])
                diag = sb_("diag", [P, P])
                put2 = sb_("put2", [P, T], I32)
                pair = sb_("pair", [P, T, 2])
                idx = sb_("idx", [P, B], I32)
                slot = sb_("slot", [P, B, 2])
                p_first = ps("first", [P, P])
                p_carry = ps("carry", [P, 1])
                loaded, own, rows_made = sem("loaded"), sem("own"), sem("rows_made")
                diag_made, first_made, scanned, carried = sem("diag_made"), sem("first_made"), sem("scanned"), sem("carried")
                ready, fed = sem("ready"), sem("fed")
                put_done = sem.many("put_done", B)
                gate = sem("gate")
                with nc.Block() as block:
                    @block.sync
                    def _(sp):
                        for c in range(3):
                            sp.dma_start(kv[:, c], srt[o][1][c:ROWS + c, :].rearrange("(p t) c -> p t c", t=T)).then_inc(loaded, 16)

                    @block.tensor
                    def _(pe):
                        pe.wait_ge(diag_made, 1)
                        pe.matmul(p_first[:], ones[:], diag[:], start=True, stop=True).then_inc(first_made, 1)
                        pe.wait_ge(scanned, 1)
                        pe.matmul(p_carry[:], g["carry"][:], raw[:, T - 1:T], start=True, stop=True).then_inc(carried, 1)

                    @block.vector
                    def _(dve):
                        c_ = Chain(dve, own, gate)
                        dve.wait_ge(loaded, 48)
                        dve.wait_ge(rows_made, 1)
                        for c in range(3):
                            c_(dve.tensor_copy(at[:, c, :], kv[:, c, :, 0]))
                        before, key, after = (at[:, c, :] for c in range(3))
                        c_(dve.tensor_tensor(g["cont"][:], before, key, ALU.is_equal))
                        c_(dve.tensor_tensor(same_next[:], after, key, ALU.is_equal))
                        c_(dve.tensor_scalar(real[:], key, float(N), None, ALU.is_lt))
                        c_(dve.tensor_scalar(off[:], same_next[:], -1.0, 1.0, ALU.mult, ALU.add))
                        c_(dve.tensor_tensor(g["endm"][:], off[:], real[:], ALU.mult))
                        c_(dve.tensor_scalar(g["pen"][:], g["cont"][:], -1.0, -NEG, ALU.add, ALU.mult))
                        c_(dve.tensor_scalar(g["rpen"][:], same_next[:], -1.0, -NEG, ALU.add, ALU.mult))
                        c_(dve.tensor_scalar(off[:], g["endm"][:], -float(SKIP), float(SKIP), ALU.mult, ALU.add))
                        c_(dve.tensor_tensor(real[:], key, off[:], ALU.add))
                        c_(dve.tensor_copy(g["put"][:], real[:]))
                        c_(dve.tensor_scalar(raw[:], real[:], 2.0, 0.0 if o == "d" else 1.0, ALU.mult, ALU.add))
                        c_(dve.tensor_copy(put2[:], raw[:]))
                        c_(dve.tensor_scalar(raw[:], key, float(N - 1), None, ALU.min))
                        c_(dve.tensor_copy(g["node"][:], raw[:]))
                        c_(dve.tensor_copy(g["other"][:], kv[:, 1, :, 1]))
                        c_(dve.tensor_reduce(small[:, 0:1], real[:], mybir.AxisListType.X, ALU.min))
                        c_(dve.tensor_tensor(real[:], row[:], off[:], ALU.add))
                        c_(dve.tensor_reduce(small[:, 1:2], real[:], mybir.AxisListType.X, ALU.min))
                        c_(dve.tensor_scalar(small[:, 2:3], g["cont"][:, 0:1], -float(SKIP), float(SKIP), ALU.mult, ALU.add))
                        c_(dve.tensor_tensor(small[:, 0:1], small[:, 0:1], small[:, 2:3], ALU.add))
                        c_(dve.tensor_tensor(small[:, 1:2], small[:, 1:2], small[:, 2:3], ALU.add))
                        c_(dve.tensor_copy(g["fix_node"][:], small[:, 0:1]))
                        c_(dve.tensor_copy(g["fix_row"][:], small[:, 1:2]))
                        c_(dve.tensor_scalar(real[:], row[:], small[:, 1:2], None, ALU.not_equal))
                        c_(dve.tensor_tensor(g["inner"][:], real[:], g["endm"][:], ALU.mult))
                        c_(dve.tensor_reduce(small[:, 3:4], g["cont"][:], mybir.AxisListType.X, ALU.min))
                        c_(dve.tensor_reduce(small[:, 4:5], same_next[:], mybir.AxisListType.X, ALU.min))
                        c_(dve.tensor_scalar(g["whole"][:], small[:, 3:5], -1.0, -NEG, ALU.add, ALU.mult))
                        dve.tensor_scalar(diag[:], ident[:], key[:, 0:1], None, ALU.mult).then_inc(diag_made, 1)
                        dve.wait_ge(first_made, 1)
                        c_(dve.scalar_tensor_tensor(g["carry"][:], p_first[:], key[:, T - 1:T], below[:], ALU.is_equal, ALU.mult))
                        one = ones[:, 0:1].to_broadcast([P, T])
                        dve.tensor_tensor_scan(raw[:], g["cont"][:], one, 0.0, ALU.mult, ALU.add).then_inc(scanned, 1)
                        dve.wait_ge(carried, 1)
                        c_(dve.tensor_copy(small[:, 5:6], p_carry[:]))
                        c_(dve.tensor_tensor_scan(g["count"][:], g["cont"][:], one, small[:, 5:6], ALU.mult, ALU.add))
                        c_(dve.reciprocal(g["inverse"][:], g["count"][:]))
                        c_(dve.tensor_copy(pair[:, :, 0], g["count"][:]))
                        c_(dve.tensor_copy(pair[:, :, 1], row[:]))
                        dve.sem_inc(ready, 1)

                    @block.gpsimd
                    def _(pool):
                        pool.iota(row[:], [[P, T]], 0, 1, allow_small_or_imprecise_dtypes=True).then_inc(rows_made, 1)
                        last = pool.to_reg(2 * N - 1)
                        pool.wait_ge(ready, 1)

                        def scatter(i):
                            for h in range(2):
                                lo, hi = h * HALF, (h + 1) * HALF
                                for b in range(lo, hi):
                                    wait(pool, put_done[b], i * 16)
                                pool.tensor_copy(idx[:, lo:hi], put2[:, bass.ds(i * B + lo, HALF)]).then_inc(fed, 1)
                                pool.tensor_copy(slot[:, lo:hi, :], pair[:, bass.ds(i * B + lo, HALF), :]).then_inc(fed, 1)
                                pool.wait_ge(fed, i * 4 + (2 * h + 2))
                                settle(pool, gate)
                                for b in range(lo, hi):
                                    pool.indirect_dma_start(nt, bass.IndirectOffsetOnAxis(idx[:, b:b + 1], 0), slot[:, b, :], None,
                                                            bounds_check=last, oob_is_err=False).then_inc(put_done[b], 16)

                        steps(pool, STEPS, scatter)
                        for s in put_done:
                            pool.wait_ge(s, 16 * STEPS)
            return g

        runs = {o: structure(o) for o in "ds"}

        nt4 = nt.rearrange("(n two) c -> n (two c)", two=2)

        def small_rows(tag, table, rows, width, jobs):
            with phase(nc, tag) as (sem, sb_, ps):
                n = len(jobs)
                slot = [sb_(f"slot{k}", [P, B, width]) for k in range(n)]
                idx = [sb_(f"idx{k}", [P, B], I32) for k in range(n)]
                fed = sem.many("fed", n)
                got = [sem.many(f"got{k}_", B) for k in range(n)]
                taken = sem("taken")
                gate = sem("gate")
                with nc.Block() as block:
                    @block.gpsimd
                    def _(pool):
                        last = pool.to_reg(rows - 1)
                        feeds = [Feed(pool, gate, fed[k], idx[k], jobs[k][0], got[k]) for k in range(n)]

                        def gather(i, b):
                            wait(pool, taken, (i * B + (b + 1 - B)) * n)
                            for k in range(n):
                                pool.indirect_dma_start(slot[k][:, b, :], None, table, feeds[k].at(b),
                                                        bounds_check=last, oob_is_err=False).then_inc(got[k][b], 16)

                        indexed(pool, gather, feeds)

                    @block.vector
                    def _(dve):
                        def take(i):
                            for b in range(B):
                                for k in range(n):
                                    dve.wait_ge(got[k][b], i * 16 + 16)
                                    dve.tensor_copy(jobs[k][1][:, bass.ds(i * B + b, 1), :].rearrange("p a c -> p (a c)"),
                                                    slot[k][:, b, :]).then_inc(taken, 1)

                        steps(dve, STEPS, take)
                        dve.wait_ge(taken, T * n)

        inv_other = {o: sb(f"inv_other_{o}", [P, T]) for o in "ds"}
        to_out_row = sb("to_out_row", [P, T], I32)
        to_in_row = sb("to_in_row", [P, T], I32)
        other_row = sb("other_row", [P, T], I32)
        own_row = sb("own_row", [P, T], I32)
        rs_other = sb("rs_other", [P, T])
        with ExitStack() as told_ctx:
            told = {k: told_ctx.enter_context(nc.sbuf_tensor(f"told_{k}", [P, T, 4], F32)) for k in ("d", "s", "own")}
            small_rows("ends_d", nt4, N, 4, [(runs["d"]["other"], told["d"])])
            small_rows("ends_s", nt4, N, 4, [(runs["s"]["other"], told["s"]), (runs["s"]["node"], told["own"])])
            with phase(nc, "scales") as (sem, sb_, ps):
                q, per = 125, N // 125
                counts = sb_("counts", [q, per, 4])
                both = sb_("both", [q, per, 2])
                deg = sb_("deg", [q, per])
                y, t1, t2 = (sb_(n, [q, per]) for n in ("y", "t1", "t2"))
                e0, e1, e2 = (sb_(n, [P, T]) for n in ("e0", "e1", "e2"))
                loaded, own, ready, stored = sem("loaded"), sem("own"), sem("ready"), sem("stored")
                gate = sem("gate")
                with nc.Block() as block:
                    @block.sync
                    def _(sp):
                        sp.dma_start(counts[:], nt4.rearrange("(p r) c -> p r c", p=q)).then_inc(loaded, 16)
                        sp.wait_ge(ready, 1)
                        sp.dma_start(dm.rearrange("(p r) c -> p r c", p=q), both[:]).then_inc(stored, 16)
                        sp.wait_ge(stored, 16)

                    @block.vector
                    def _(dve):
                        c_ = Chain(dve, own, gate)
                        dve.wait_ge(loaded, 16)
                        c_(dve.tensor_scalar(deg[:], counts[:, :, 0], 1.0, None, ALU.add))
                        rstd_steps(c_, deg[:], y[:], t1[:], t2[:])
                        c_(dve.tensor_copy(both[:, :, 0], y[:]))
                        dve.tensor_scalar(both[:, :, 1], counts[:, :, 0], 0.0, None, ALU.is_equal).then_inc(ready, 1)
                        c_(dve.tensor_scalar(e0[:], told["d"][:, :, 0], 1.0, None, ALU.add))
                        rstd_steps(c_, e0[:], rs_other[:], e1[:], e2[:])
                        c_(dve.tensor_scalar(e0[:], told["d"][:, :, 2], 1.0, None, ALU.max))
                        c_(dve.reciprocal(inv_other["d"][:], e0[:]))
                        c_(dve.tensor_scalar(e0[:], told["s"][:, :, 0], 1.0, None, ALU.max))
                        c_(dve.reciprocal(inv_other["s"][:], e0[:]))
                        c_(dve.tensor_copy(to_out_row[:], told["d"][:, :, 3]))
                        c_(dve.tensor_copy(to_in_row[:], told["s"][:, :, 1]))
                        c_(dve.tensor_copy(own_row[:], told["own"][:, :, 3]))
                        c_(dve.tensor_scalar(e0[:], told["s"][:, :, 2], 0.0, float(ROWS), ALU.is_equal, ALU.mult))
                        c_(dve.tensor_tensor(e1[:], e0[:], told["s"][:, :, 3], ALU.add))
                        c_(dve.tensor_copy(other_row[:], e1[:]))
                        dve.wait_ge(ready, 1)

        def row_of(name, width=D):
            return sb(f"row_{name}", [P, width])

        w = {"a1": sb("w_a1", [P, 2, HID]), "a2": sb("w_a2", [HID + 1, D]), "b1": sb("w_b1", [P, 2, D]),
             "b2": sb("w_b2", [P, 2, D]), "g": sb("w_g", [P, 2, HID])}
        bias = {"a1": row_of("a1", HID), "b1": row_of("b1"), "b2": row_of("b2"), "g": row_of("g", HID)}
        slope = sb("slope", [P, 1])
        fall = sb("fall", [P, 1])
        minus_fall = sb("minus_fall", [P, 1])
        with phase(nc, "weights") as (sem, sb_, ps):
            loaded, own = sem("loaded"), sem("own")
            gate = sem("gate")
            with nc.Block() as block:
                @block.sync
                def _(sp):
                    jobs = [(w["a1"][:], a["L0_gnn_W1"].rearrange("(c p) n -> p c n", p=P)), (w["a2"][0:HID, :], a["L0_gnn_W2"]), (w["a2"][HID:HID + 1, :], a["L0_gnn_b2"].rearrange("(o n) -> o n", o=1)),
                            (w["b1"][:], a["L1_gnn_W1"].rearrange("(c p) n -> p c n", p=P)),
                            (w["b2"][:], a["L1_gnn_W2"].rearrange("(c p) n -> p c n", p=P)),
                            (w["g"][:], a["L2_gnn_W_gcn"].rearrange("(c p) n -> p c n", p=P)),
                            (slope[:], a["L1_gnn_a"].rearrange("(o n) -> o n", o=1).to_broadcast([P, 1]))]
                    for k, name in (("a1", "L0_gnn_b1"), ("b1", "L1_gnn_b1"), ("b2", "L1_gnn_b2"), ("g", "L2_gnn_b_gcn")):
                        width = bias[k].shape[1]
                        jobs.append((bias[k][:], a[name].rearrange("(o n) -> o n", o=1).to_broadcast([P, width])))
                    for target, source in jobs:
                        sp.dma_start(target, source).then_inc(loaded, 16)
                    sp.wait_ge(loaded, 16 * len(jobs))

                @block.vector
                def _(dve):
                    dve.wait_ge(loaded, 16 * 11)
                    dve.tensor_scalar(fall[:], slope[:], -1.0, 1.0, ALU.mult, ALU.add).then_inc(own, 1)
                    dve.wait_ge(own, 1)
                    dve.tensor_scalar(minus_fall[:], fall[:], -1.0, None, ALU.mult).then_inc(own, 1)
                    dve.wait_ge(own, 2)

        def edge_sum(tag, o, table, rows, index, width, target, by_node, scale=None, weights=None, net=None):
            g = runs[o]
            out_w = D if weights is not None else width
            if net is not None:
                layer, bias_row = net
            with phase(nc, tag) as (sem, sb_, ps):
                got_rows = sb_("got_rows", [P, B, width])
                scaled = sb_("scaled", [P, B, out_w]) if scale is not None or weights is not None else got_rows
                if net is not None:
                    xt = sb_("xt", [P, B, 2, P])
                    y = sb_("y", [P, B, D])
                    neg = sb_("neg", [P, B, D])
                    p_t = [ps(f"t{k}", [P, 2, P]) for k in range(2)]
                    p_y = [ps(f"y{k}", [P, 512]) for k in range(2)]
                    turned, evac, product, layered, lowered = sem("turned"), sem("evac"), sem("product"), sem("layered"), sem("lowered")
                total = sb_("total", [P, B, out_w])
                idx = sb_("idx", [P, B], I32)
                put = sb_("put", [P, B], I32)
                fix = sb_("fix", [P, out_w])
                fixed = sb_("fixed", [P, out_w])
                p_carry = ps("carry", [P, out_w])
                got, stored = sem.many("got", B), sem.many("stored", B)
                fed, fed_put, made, summed, own = sem("fed"), sem("fed_put"), sem("made"), sem("summed"), sem("own")
                carried, fix_got, fix_ready, blank = sem("carried"), sem("fix_got"), sem("fix_ready"), sem("blank")
                target_rows = N if by_node else ROWS
                gate = sem("gate")
                with nc.Block() as block:
                    @block.gpsimd
                    def _(pool):
                        last = pool.to_reg(rows - 1)
                        last_out = pool.to_reg(target_rows - 1)
                        feed = Feed(pool, gate, fed, idx, index, got)
                        feed_put = Feed(pool, gate, fed_put, put, g["put"], stored)
                        used = turned if net is not None else made if scaled is not got_rows else summed

                        def gather(i, b):
                            wait(pool, used, i * B + (b + 1 - B))
                            pool.indirect_dma_start(got_rows[:, b, :], None, table, feed.at(b),
                                                    bounds_check=last, oob_is_err=False).then_inc(got[b], 16)

                        def scatter(i, b):
                            pool.wait_ge(summed, i * B + (b + 1))
                            pool.indirect_dma_start(target, feed_put.at(b), total[:, b, :], None,
                                                    bounds_check=last_out, oob_is_err=False).then_inc(stored[b], 16)

                        if by_node:
                            indexed(pool, gather, [feed], scatter, [feed_put])
                        else:
                            indexed(pool, gather, [feed])
                        for s in stored:
                            pool.wait_ge(s, 16 * STEPS)
                        pool.wait_ge(blank, 1)
                        at = bass.IndirectOffsetOnAxis(g["fix_node" if by_node else "fix_row"][:, 0:1], 0)
                        pool.indirect_dma_start(fix[:], None, target, at, bounds_check=last_out, oob_is_err=False).then_inc(fix_got, 16)
                        pool.wait_ge(fix_ready, 1)
                        pool.indirect_dma_start(target, at, fixed[:], None, bounds_check=last_out, oob_is_err=False).then_inc(fix_got, 16)
                        pool.wait_ge(fix_got, 32)

                    if not by_node:
                        @block.sync
                        def _(sp):
                            def store(i):
                                for b in range(B):
                                    sp.wait_ge(summed, i * B + (b + 1))
                                    sp.dma_start(target[bass.ds(i * (B * P) + b * P, P), :], total[:, b, :]).then_inc(stored[b], 16)

                            steps(sp, STEPS, store)

                    if net is not None:
                        @block.scalar
                        def _(act):
                            def copy(i, b):
                                act.wait_ge(turned, i * B + (b + 1))
                                wait(act, product, i * B + (b + 1 - B))
                                act.activation(xt[:, b], p_t[b % 2][:], ACT.Copy).then_inc(evac, 1)

                            def negative(i, b):
                                act.wait_ge(layered, i * B + (b + 1))
                                wait(act, made, i * B + (b + 1 - B))
                                act.activation(neg[:, b, :], y[:, b, :], ACT.Relu, scale=-1.0).then_inc(lowered, 1)

                            columns(act, [(copy, 0), (negative, 2)])

                    elif scale is not None:
                        @block.scalar
                        def _(act):
                            def times(i):
                                for b in range(B):
                                    act.wait_ge(got[b], i * 16 + 16)
                                    wait(act, summed, i * B + (b + 1 - B))
                                    act.activation(scaled[:, b, :], got_rows[:, b, :], ACT.Copy,
                                                   scale=scale[:, bass.ds(i * B + b, 1)]).then_inc(made, 1)

                            steps(act, STEPS, times)

                    @block.vector
                    def _(dve):
                        c_ = Chain(dve, own, gate)
                        c_(dve.memset(total[:, B - 1, :], 0.0))
                        dve.memset(fix[:], 0.0).then_inc(blank, 1)

                        def layer_out(i, b):
                            t = i * B + b
                            dve.wait_ge(product, t + 1)
                            wait(dve, made, i * B + (b + 1 - B))
                            wait(dve, lowered, i * B + (b + 1 - B))
                            dve.scalar_tensor_tensor(y[:, b, :], p_y[b % 2][:, 0:D], scale[:, bass.ds(t, 1)], bias_row[:], ALU.mult, ALU.add).then_inc(layered, 1)

                        def add_net(i, b):
                            t = i * B + b
                            dve.wait_ge(layered, t + 1)
                            dve.wait_ge(lowered, t + 1)
                            wait(dve, summed, i * B + (b + 1 - B))
                            dve.scalar_tensor_tensor(scaled[:, b, :], neg[:, b, :], fall[:], y[:, b, :], ALU.mult, ALU.add).then_inc(made, 1)
                            dve.wait_ge(made, t + 1)
                            wait(dve, stored[b], i * 16)
                            wait(dve, summed, t)
                            dve.scalar_tensor_tensor(total[:, b, :], total[:, (b - 1) % B, :], g["cont"][:, bass.ds(t, 1)],
                                                     scaled[:, b, :], ALU.mult, ALU.add).then_inc(summed, 1)

                        def add(i):
                            for b in range(B):
                                t = i * B + b
                                if weights is not None:
                                    dve.wait_ge(got[b], i * 16 + 16)
                                    rows_in = got_rows[:, b, :].rearrange("p (h c) -> p h c", c=HID)
                                    if width == HID:
                                        rows_in = rows_in.to_broadcast([P, HEADS, HID])
                                    wt = weights[:, bass.ds(t, 1), :].rearrange("p a h -> p (a h)").unsqueeze(2).to_broadcast([P, HEADS, HID])
                                    dve.tensor_tensor(scaled[:, b, :].rearrange("p (h c) -> p h c", c=HID), rows_in, wt, ALU.mult).then_inc(made, 1)
                                if scaled is not got_rows:
                                    dve.wait_ge(made, t + 1)
                                else:
                                    dve.wait_ge(got[b], i * 16 + 16)
                                wait(dve, stored[b], i * 16)
                                dve.scalar_tensor_tensor(total[:, b, :], total[:, (b - 1) % B, :], g["cont"][:, bass.ds(t, 1)],
                                                         scaled[:, b, :], ALU.mult, ALU.add).then_inc(summed, 1)
                                dve.wait_ge(summed, t + 1)

                        if net is not None:
                            columns(dve, [(layer_out, 0), (add_net, 3)])
                        else:
                            steps(dve, STEPS, add)
                        dve.wait_ge(carried, 1)
                        dve.wait_ge(fix_got, 16)
                        dve.tensor_tensor(fixed[:], fix[:], p_carry[:], ALU.add).then_inc(fix_ready, 1)

                    @block.tensor
                    def _(pe):
                        def turn(i, b):
                            pe.wait_ge(got[b], i * 16 + 16)
                            wait(pe, evac, i * B + (b - 1))
                            for c in range(2):
                                m = pe.transpose(p_t[b % 2][:, c, :], got_rows[:, b, c * P:(c + 1) * P], ident[:])
                            m.then_inc(turned, 1)

                        def mul(i, b):
                            pe.wait_ge(evac, i * B + (b + 1))
                            wait(pe, layered, i * B + (b - 1))
                            for c in range(2):
                                m = pe.matmul(p_y[b % 2][:, 0:D], xt[:, b, c, :], layer[:, c, :], start=(c == 0), stop=(c == 1))
                            m.then_inc(product, 1)

                        if net is not None:
                            columns(pe, [(turn, 0), (mul, 1)])
                        pe.wait_ge(summed, T)
                        pe.matmul(p_carry[:], g["carry"][:], total[:, B - 1, :], start=True, stop=True).then_inc(carried, 1)

        h0 = dram("h0", (N, HID))
        with phase(nc, "first") as (sem, sb_, ps):
            x_in = sb_("x_in", [P, 2, JB, D])
            sc = sb_("sc", [P, 2, JB, 2])
            xt = sb_("xt", [P, 2, JB, 2, P])
            ho = sb_("ho", [P, 2, JB, HID])
            p_t = [ps(f"t{s}", [P, JB + 1, 2, P]) for s in range(2)]
            p_h = [ps(f"h{s}", [P, 512]) for s in range(2)]
            got_x, got_s, stored = sem.many("got_x", 2), sem.many("got_s", 2), sem.many("stored", 2)
            turned, evac, product, made = sem("turned"), sem("evac"), sem("product"), sem("made")
            gate = sem("gate")
            with nc.Block() as block:
                @block.sync
                def _(sp):
                    def load(i, s, p, j):
                        wait(sp, turned, i * 2 + (s - 1))
                        sp.dma_start(x_in[0:p, s, 0:j, :], group(a["x"], i, s, p, j)).then_inc(got_x[s], 16)
                        wait(sp, made, i * 2 + (s - 1))
                        sp.dma_start(sc[0:p, s, 0:j, :], group(dm, i, s, p, j)).then_inc(got_s[s], 16)

                    def store(i, s, p, j):
                        sp.wait_ge(made, i * 2 + (s + 1))
                        sp.dma_start(group(h0, i, s, p, j), ho[0:p, s, 0:j, :]).then_inc(stored[s], 16)

                    pairs(sp, [(load, 0), (store, 2)], j=JB)
                    sp.wait_ge(stored[0], 16 * (pair_count(JB) + 1))
                    sp.wait_ge(stored[1], 16 * pair_count(JB))

                @block.tensor
                def _(pe):
                    def turn(i, s, p, j):
                        pe.wait_ge(got_x[s], i * 16 + 16)
                        wait(pe, evac, i * 2 + (s - 1))
                        for k in range(j):
                            for c in range(2):
                                m = pe.transpose(p_t[s][:, k, c, 0:p], x_in[0:p, s, k, c * P:(c + 1) * P], ident[0:p, 0:p])
                        m.then_inc(turned, 1)

                    def mul(i, s, p, j):
                        pe.wait_ge(evac, i * 2 + (s + 1))
                        wait(pe, made, i * 2 + (s - 1))
                        for k in range(j):
                            for c in range(2):
                                m = pe.matmul(p_h[s][0:p, k * HID:(k + 1) * HID], xt[:, s, k, c, 0:p], w["a1"][:, c, :], start=(c == 0), stop=(c == 1))
                        m.then_inc(product, 1)

                    pairs(pe, [(turn, 0), (mul, 1)], j=JB)

                @block.scalar
                def _(act):
                    def copy(i, s, p, j):
                        act.wait_ge(turned, i * 2 + (s + 1))
                        wait(act, product, i * 2 + (s - 1))
                        act.activation(xt[:, s, 0:j, :, 0:p], p_t[s][:, 0:j, :, 0:p], ACT.Copy).then_inc(evac, 1)

                    pairs(act, [(copy, 0)], j=JB)

                @block.vector
                def _(dve):
                    def scale(i, s, p, j):
                        dve.wait_ge(product, i * 2 + (s + 1))
                        dve.wait_ge(got_s[s], i * 16 + 16)
                        wait(dve, stored[s], i * 16)
                        dve.tensor_tensor(ho[0:p, s, 0:j, :], p_h[s][0:p, 0:j * HID].rearrange("p (j c) -> p j c", c=HID),
                                          sc[0:p, s, 0:j, 0:1].to_broadcast([p, j, HID]), ALU.mult).then_inc(made, 1)

                    pairs(dve, [(scale, 0)], j=JB)

        dst_runs = runs["d"]
        edge_sum("sum0", "d", h0, N, dst_runs["other"], HID, agg[0], True)

        def sum_bias(c_, total, own, sc, bias_row, tmp, p, j, own_scaled):
            dve = c_.eng
            rs = sc[0:p, 0:j, 0:1].to_broadcast([p, j, HID])
            if not own_scaled:
                c_(dve.tensor_tensor(own, own, rs, ALU.mult))
            c_(dve.tensor_tensor(tmp, total, own, ALU.add))
            c_(dve.tensor_tensor(tmp, tmp, rs, ALU.mult))
            c_(dve.tensor_tensor(tmp, tmp, bias_row[0:p, :].unsqueeze(1).to_broadcast([p, j, HID]), ALU.add))

        h1 = dram("h1", (N, HID))
        with phase(nc, "second") as (sem, sb_, ps):
            sc = sb_("sc", [P, 2, JB, 2])
            h_in = sb_("h_in", [P, 2, JB, HID])
            a_in = sb_("a_in", [P, 2, JB, HID])
            tmp = sb_("tmp", [P, 2, JB, HID])
            ho = sb_("ho", [P, 2, JB, HID])
            got, stored = [sem.many(f"got{k}_", 2) for k in range(3)], sem.many("stored", 2)
            made, own = sem("made"), sem("own")
            gate = sem("gate")
            with nc.Block() as block:
                @block.sync
                def _(sp):
                    def load(i, s, p, j):
                        wait(sp, made, i * 2 + (s - 1))
                        for k, (buf, table) in enumerate(((sc, dm), (h_in, h0), (a_in, agg[0]))):
                            sp.dma_start(buf[0:p, s, 0:j, :], group(table, i, s, p, j)).then_inc(got[k][s], 16)

                    def store(i, s, p, j):
                        sp.wait_ge(made, i * 2 + (s + 1))
                        sp.dma_start(group(h1, i, s, p, j), ho[0:p, s, 0:j, :]).then_inc(stored[s], 16)

                    pairs(sp, [(load, 0), (store, 2)], j=JB)
                    sp.wait_ge(stored[0], 16 * (pair_count(JB) + 1))
                    sp.wait_ge(stored[1], 16 * pair_count(JB))

                @block.vector
                def _(dve):
                    c_ = Chain(dve, own, gate)

                    def layer(i, s, p, j):
                        for k in range(3):
                            dve.wait_ge(got[k][s], i * 16 + 16)
                        wait(dve, stored[s], i * 16)
                        sum_bias(c_, a_in[0:p, s, 0:j, :], h_in[0:p, s, 0:j, :], sc[:, s], bias["a1"], tmp[0:p, s, 0:j, :], p, j, True)
                        dve.scalar_tensor_tensor(ho[0:p, s, 0:j, :], tmp[0:p, s, 0:j, :], 0.0, sc[0:p, s, 0:j, 0:1].to_broadcast([p, j, HID]),
                                                 ALU.max, ALU.mult).then_inc(made, 1)

                    pairs(dve, [(layer, 0)], c_, 6, j=JB)

        edge_sum("sum1", "d", h1, N, dst_runs["other"], HID, agg[1], True)

        x1, x2, g2 = dram("x1", (N, D)), dram("x2", (N, D)), dram("g2", (N, HID))
        with phase(nc, "third") as (sem, sb_, ps):
            sc = sb_("sc", [P, 2, JB, 2])
            h_in = sb_("h_in", [P, 2, JB, HID])
            a_in = sb_("a_in", [P, 2, JB, HID])
            go = sb_("go", [P, 2, JB, HID])
            at = sb_("at", [HID + 1, 2, JB, P])
            x_in, y, x1o, z, neg, u, x2o = (sb_(n, [P, 2, JB, D]) for n in ("x_in", "y", "x1o", "z", "neg", "u", "x2o"))
            xt = sb_("xt", [P, 2, JB, 2, P])
            st1_, st2_ = norm_slots(sb_, "n1", JB), norm_slots(sb_, "n2", JB)
            p_m = ps("m", [P, 1024])
            p_a = p_m[0:HID, 0:JB * P].rearrange("p (j q) -> p j q", q=P)
            p_g = p_m[:, JB * P:JB * (P + HID)].rearrange("p (j c) -> p j c", c=HID)
            p_y = ps("py", [P, JB + 1, D])
            p_t = ps("t", [P, JB + 1, 2, P])
            got = [sem.many(f"got{k}_", 2) for k in range(4)]
            st1, st2, st3 = sem.many("st1_", 2), sem.many("st2_", 2), sem.many("st3_", 2)
            own, a_made, a_turned, a_copied, y_made, x1_made, x2_made = (sem(n) for n in
                ("own", "a_made", "a_turned", "a_copied", "y_made", "x1_made", "x2_made"))
            turned, copied, product, g_made, y_used = (sem(n) for n in ("turned", "copied", "product", "g_made", "y_used"))
            stats1, stats2, z_made, neg_made = (sem(n) for n in ("stats1", "stats2", "z_made", "neg_made"))
            gate = sem("gate")
            with nc.Block() as block:
                @block.sync
                def _(sp):
                    def load(i, s, p, j):
                        wait(sp, a_turned, i * 2 + (s - 1))
                        for k, (buf, table) in enumerate(((sc, dm), (h_in, h1), (a_in, agg[1]))):
                            sp.dma_start(buf[0:p, s, 0:j, :], group(table, i, s, p, j)).then_inc(got[k][s], 16)
                        wait(sp, y_used, i * 2 + (s - 1))
                        sp.dma_start(x_in[0:p, s, 0:j, :], group(a["x"], i, s, p, j)).then_inc(got[3][s], 16)

                    def store_x1(i, s, p, j):
                        sp.wait_ge(x1_made, i * 2 + (s + 1))
                        sp.dma_start(group(x1, i, s, p, j), x1o[0:p, s, 0:j, :]).then_inc(st1[s], 16)

                    def store_x2(i, s, p, j):
                        sp.wait_ge(x2_made, i * 2 + (s + 1))
                        sp.dma_start(group(x2, i, s, p, j), x2o[0:p, s, 0:j, :]).then_inc(st2[s], 16)

                    def store_g(i, s, p, j):
                        sp.wait_ge(g_made, i * 2 + (s + 1))
                        sp.dma_start(group(g2, i, s, p, j), go[0:p, s, 0:j, :]).then_inc(st3[s], 16)

                    pairs(sp, [(load, 0), (store_x1, 2), (store_x2, 3), (store_g, 5)], j=JB)
                    for q in (st1, st2, st3):
                        sp.wait_ge(q[0], 16 * (pair_count(JB) + 1))
                        sp.wait_ge(q[1], 16 * pair_count(JB))

                @block.tensor
                def _(pe):
                    def turn_a(i, s, p, j):
                        pe.wait_ge(a_made, i * 2 + (s + 1))
                        wait(pe, g_made, i * 2 + (s - 4))
                        settle(pe, gate)
                        for k in range(j):
                            m = pe.transpose(p_a[:, k, 0:p], h_in[0:p, s, k, :], ident[0:p, 0:p])
                        m.then_inc(a_turned, 1)

                    def mul_y(i, s, p, j):
                        pe.wait_ge(a_copied, i * 2 + (s + 1))
                        wait(pe, y_used, i * 2 + s)
                        for k in range(j):
                            m = pe.matmul(p_y[0:p, k, :], at[:, s, k, 0:p], w["a2"][:], start=True, stop=True)
                        m.then_inc(y_made, 1)

                    def turn_x(i, s, p, j):
                        pe.wait_ge(x2_made, i * 2 + (s + 1))
                        wait(pe, copied, i * 2 + s)
                        for k in range(j):
                            for c in range(2):
                                m = pe.transpose(p_t[:, k, c, 0:p], x2o[0:p, s, k, c * P:(c + 1) * P], ident[0:p, 0:p])
                        m.then_inc(turned, 1)

                    def mul_g(i, s, p, j):
                        pe.wait_ge(copied, i * 2 + (s + 1))
                        wait(pe, g_made, i * 2 + s)
                        for k in range(j):
                            for c in range(2):
                                m = pe.matmul(p_g[0:p, k, :], xt[:, s, k, c, 0:p], w["g"][:, c, :], start=(c == 0), stop=(c == 1))
                        m.then_inc(product, 1)

                    pairs(pe, [(turn_a, 0), (turn_x, 3), (mul_y, 0), (mul_g, 4)], j=JB)

                @block.scalar
                def _(act):
                    def copy_a(i, s, p, j):
                        act.wait_ge(a_turned, i * 2 + (s + 1))
                        wait(act, y_made, i * 2 + (s - 1))
                        act.activation(at[0:HID, s, 0:j, 0:p], p_a[:, 0:j, 0:p], ACT.Copy).then_inc(a_copied, 1)

                    def norm1(i, s, p, j):
                        act.wait_ge(stats1, i * 2 + (s + 1))
                        wait(act, stats2, i * 2 + (s - 1))
                        wait(act, st1[s], i * 16)
                        normalize(act, y[:, s], x1o[:, s], st1_, s, p, j).then_inc(x1_made, 1)

                    def fall_(i, s, p, j):
                        act.wait_ge(z_made, i * 2 + (s + 1))
                        wait(act, stats2, i * 2 + (s - 1))
                        act.activation(neg[0:p, s, 0:j, :], z[0:p, s, 0:j, :], ACT.Relu, scale=-1.0).then_inc(neg_made, 1)

                    def norm2(i, s, p, j):
                        act.wait_ge(stats2, i * 2 + (s + 1))
                        wait(act, turned, i * 2 + (s - 1))
                        wait(act, st2[s], i * 16)
                        normalize(act, u[:, s], x2o[:, s], st2_, s, p, j).then_inc(x2_made, 1)

                    def copy_x(i, s, p, j):
                        act.wait_ge(turned, i * 2 + (s + 1))
                        wait(act, product, i * 2 + (s - 1))
                        act.activation(xt[:, s, 0:j, :, 0:p], p_t[:, 0:j, :, 0:p], ACT.Copy).then_inc(copied, 1)

                    def copy_g(i, s, p, j):
                        act.wait_ge(product, i * 2 + (s + 1))
                        wait(act, st3[s], i * 16)
                        act.activation(go[0:p, s, 0:j, :], p_g[0:p, 0:j, :], ACT.Copy).then_inc(g_made, 1)

                    pairs(act, [(copy_a, 0), (fall_, 2), (copy_x, 3), (norm1, 1), (copy_g, 4), (norm2, 2)], j=JB)

                @block.vector
                def _(dve):
                    c_ = Chain(dve, own, gate)
                    c_(dve.memset(at[HID:HID + 1], 1.0))

                    def conv(i, s, p, j):
                        for k in range(3):
                            dve.wait_ge(got[k][s], i * 16 + 16)
                        wait(dve, a_turned, i * 2 + (s - 1))
                        h, t = h_in[0:p, s, 0:j, :], a_in[0:p, s, 0:j, :]
                        c_(dve.tensor_tensor(t, t, h, ALU.add))
                        dve.tensor_tensor(h, t, sc[0:p, s, 0:j, 0:1].to_broadcast([p, j, HID]), ALU.mult).then_inc(a_made, 1)

                    def first(i, s, p, j):
                        dve.wait_ge(y_made, i * 2 + (s + 1))
                        dve.wait_ge(got[3][s], i * 16 + 16)
                        wait(dve, x1_made, i * 2 + (s - 1))
                        c_(dve.scalar_tensor_tensor(y[0:p, s, 0:j, :], p_y[0:p, 0:j, :], 0.0, x_in[0:p, s, 0:j, :], ALU.max, ALU.add))
                        dve.sem_inc(y_used, 1)
                        norm_stats(c_, y[:, s], st1_, s, p, j)
                        dve.sem_inc(stats1, 1)

                    def second(i, s, p, j):
                        dve.wait_ge(neg_made, i * 2 + (s + 1))
                        wait(dve, x2_made, i * 2 + (s - 1))
                        t = u[0:p, s, 0:j, :]
                        c_(dve.tensor_tensor(t, z[0:p, s, 0:j, :], x1o[0:p, s, 0:j, :], ALU.add))
                        c_(dve.scalar_tensor_tensor(t, neg[0:p, s, 0:j, :], fall[0:p], t, ALU.mult, ALU.add))
                        norm_stats(c_, u[:, s], st2_, s, p, j)
                        dve.sem_inc(stats2, 1)

                    pairs(dve, [(conv, 0), (first, 1), (second, 2)], c_, 2 * (4 + 2 * (2 * JB + 13)), j=JB)

                @block.gpsimd
                def _(pool):
                    def biased(i, s, p, j):
                        pool.wait_ge(x1_made, i * 2 + (s + 1))
                        wait(pool, stats2, i * 2 + (s - 1))
                        pool.tensor_tensor(z[0:p, s, 0:j, :], x1o[0:p, s, 0:j, :], bias["b2"][0:p, :].unsqueeze(1).to_broadcast([p, j, D]), ALU.add).then_inc(z_made, 1)

                    pairs(pool, [(biased, 1)], j=JB)


        m1, o1, m2, o2 = (dram(n, (ROWS, D)) for n in ("m1", "o1", "m2", "o2"))
        src_runs = runs["s"]
        edge_sum("m1", "d", x1, N, dst_runs["other"], D, m1, False)
        edge_sum("o1", "s", m1, ROWS, to_in_row, D, o1, False, scale=inv_other["s"])
        edge_sum("m2", "d", o1, ROWS, to_out_row, D, m2, False, scale=inv_other["d"], net=(w["b1"], bias["b1"]))
        edge_sum("o2", "s", m2, ROWS, to_in_row, D, o2, False, scale=inv_other["s"])

        with phase(nc, "x2_ends") as (sem, sb_, ps):
            g = src_runs
            o_in = sb_("o_in", [P, B, D])
            xg = sb_("xg", [P, B, D])
            xt = sb_("xt", [P, 2, 2, P])
            y = sb_("y", [P, B, D])
            low = sb_("low", [P, HALF, D])
            x2o = sb_("x2o", [P, B, D])
            xt2 = sb_("xt2", [P, 2, 2, P])
            go = sb_("go", [P, B, HID])
            idx, put1, put2 = (sb_(n, [P, B], I32) for n in ("idx", "put1", "put2"))
            st = norm_buffers(sb_, HALF)
            p_t = [ps(f"t{k}", [P, 2, P]) for k in range(2)]
            p_y = [ps(f"y{k}", [P, 512]) for k in range(2)]
            p_u = [ps(f"u{k}", [P, 2, P]) for k in range(2)]
            p_g = [ps(f"g{k}", [P, 512]) for k in range(2)]
            loaded, got, st1, st2 = (sem.many(n, B) for n in ("loaded", "got", "st1_", "st2_"))
            fed, fed1, fed2, own = (sem(n) for n in ("fed", "fed1", "fed2", "own"))
            turned, copied, product, y_used, x2_made = (sem(n) for n in ("turned", "copied", "product", "y_used", "x2_made"))
            turned2, copied2, product2, g_made = (sem(n) for n in ("turned2", "copied2", "product2", "g_made"))
            gate = sem("gate")
            with nc.Block() as block:
                @block.sync
                def _(sp):
                    def load(i, b):
                        wait(sp, turned, i * B + (b + 1 - B))
                        sp.dma_start(o_in[:, b, :], o2[bass.ds(i * (B * P) + b * P, P), :]).then_inc(loaded[b], 16)

                    columns(sp, [(load, 0)])

                @block.gpsimd
                def _(pool):
                    last = pool.to_reg(N - 1)
                    feed = Feed(pool, gate, fed, idx, g["node"], got)
                    feed1 = Feed(pool, gate, fed1, put1, g["put"], st1)
                    feed2 = Feed(pool, gate, fed2, put2, g["put"], st2)

                    def gather(i, b):
                        wait(pool, x2_made, i * B + (b + 1 - B))
                        pool.indirect_dma_start(xg[:, b, :], None, x1, feed.at(b), bounds_check=last, oob_is_err=False).then_inc(got[b], 16)

                    def scatter(i, b):
                        pool.wait_ge(x2_made, i * B + (b + 1))
                        pool.indirect_dma_start(x2, feed1.at(b), x2o[:, b, :], None, bounds_check=last, oob_is_err=False).then_inc(st1[b], 16)
                        pool.wait_ge(g_made, i * B + (b + 1))
                        pool.indirect_dma_start(g2, feed2.at(b), go[:, b, :], None, bounds_check=last, oob_is_err=False).then_inc(st2[b], 16)

                    indexed(pool, gather, [feed], scatter, [feed1, feed2], behind=2)
                    for q in st1 + st2:
                        pool.wait_ge(q, 16 * STEPS)

                @block.tensor
                def _(pe):
                    def turn(i, b):
                        pe.wait_ge(loaded[b], i * 16 + 16)
                        wait(pe, copied, i * B + (b - 1))
                        for c in range(2):
                            m = pe.transpose(p_t[b % 2][:, c, :], o_in[:, b, c * P:(c + 1) * P], ident[:])
                        m.then_inc(turned, 1)

                    def mul(i, b):
                        pe.wait_ge(copied, i * B + (b + 1))
                        wait(pe, y_used, i * B + (b - 1))
                        for c in range(2):
                            m = pe.matmul(p_y[b % 2][:, 0:D], xt[:, b % 2, c, :], w["b2"][:, c, :], start=(c == 0), stop=(c == 1))
                        m.then_inc(product, 1)

                    def turn2(i, b):
                        pe.wait_ge(x2_made, i * B + (b + 1))
                        wait(pe, copied2, i * B + (b - 1))
                        for c in range(2):
                            m = pe.transpose(p_u[b % 2][:, c, :], x2o[:, b, c * P:(c + 1) * P], ident[:])
                        m.then_inc(turned2, 1)

                    def mul2(i, b):
                        pe.wait_ge(copied2, i * B + (b + 1))
                        wait(pe, g_made, i * B + (b - 1))
                        for c in range(2):
                            m = pe.matmul(p_g[b % 2][:, 0:HID], xt2[:, b % 2, c, :], w["g"][:, c, :], start=(c == 0), stop=(c == 1))
                        m.then_inc(product2, 1)

                    columns(pe, [(turn, 0), (mul, 1), (turn2, HALF + 2), (mul2, HALF + 3)])

                @block.scalar
                def _(act):
                    def copy(i, b):
                        act.wait_ge(turned, i * B + (b + 1))
                        wait(act, product, i * B + (b - 1))
                        act.activation(xt[:, b % 2], p_t[b % 2][:], ACT.Copy).then_inc(copied, 1)

                    def copy2(i, b):
                        act.wait_ge(turned2, i * B + (b + 1))
                        wait(act, product2, i * B + (b - 1))
                        act.activation(xt2[:, b % 2], p_u[b % 2][:], ACT.Copy).then_inc(copied2, 1)

                    def copy_g(i, b):
                        act.wait_ge(product2, i * B + (b + 1))
                        wait(act, st2[b], i * 16)
                        act.activation(go[:, b, :], p_g[b % 2][:, 0:HID], ACT.Copy).then_inc(g_made, 1)

                    columns(act, [(copy, 0), (copy2, HALF + 2), (copy_g, HALF + 3)])

                @block.vector
                def _(dve):
                    c_ = Chain(dve, own, gate)

                    def node(i, b):
                        t = i * B + b
                        dve.wait_ge(product, t + 1)
                        wait(dve, x2_made, i * B + (b + 1 - B))
                        dve.scalar_tensor_tensor(y[:, b, :], p_y[b % 2][:, 0:D], g["inverse"][:, bass.ds(t, 1)], bias["b2"][:], ALU.mult, ALU.add).then_inc(y_used, 1)
                        if b % HALF == HALF - 1:
                            half(i, b + 1 - HALF, b + 1)

                    def half(i, lo, hi):
                        for b in range(lo, hi):
                            dve.wait_ge(got[b], i * 16 + 16)
                            wait(dve, st1[b], i * 16)
                        dve.wait_ge(y_used, i * B + hi)
                        wait(dve, turned2, i * B + (hi - B))
                        z, x = y[:, lo:hi, :], xg[:, lo:hi, :]
                        c_(dve.tensor_tensor(z, z, x, ALU.add))
                        c_(dve.tensor_scalar(low[:], z, 0.0, minus_fall[:], ALU.min, ALU.mult))
                        c_(dve.tensor_tensor(z, z, x, ALU.add))
                        c_(dve.tensor_tensor(z, z, low[:], ALU.add))
                        layer_norm(c_, z, x2o[:, lo:hi, :], st, P, HALF)
                        dve.sem_inc(x2_made, HALF)

                    columns(dve, [(node, 1)], c_, 2 * (4 + 3 * HALF + 12))

        edge_sum("gcn", "d", g2, N, dst_runs["other"], HID, agg[2], True, scale=rs_other)

        def batch_scale(c_, sums, squares, gamma, beta, b_row, scale, shift, tmp):
            dve = c_.eng
            mean, var, y, t, u, full = tmp
            c_(dve.tensor_scalar(mean, sums, 1.0 / N, None, ALU.mult))
            c_(dve.tensor_scalar(var, squares, 1.0 / N, None, ALU.mult))
            c_(dve.tensor_tensor(t, mean, mean, ALU.mult))
            c_(dve.tensor_tensor(var, var, t, ALU.subtract))
            c_(dve.tensor_scalar(var, var, 0.0, EPS, ALU.max, ALU.add))
            rstd_steps(c_, var, y, t, u)
            c_(dve.tensor_tensor(scale, gamma, y, ALU.mult))
            c_(dve.tensor_tensor(full, mean, b_row, ALU.add))
            c_(dve.tensor_tensor(full, b_row, full, ALU.subtract))
            c_(dve.tensor_tensor(full, full, scale, ALU.mult))
            c_(dve.tensor_tensor(shift, full, beta, ALU.add))

        r0 = dram("r0", (N, HID))
        stat0 = sb("stat0", [HID, 2])
        with phase(nc, "fourth") as (sem, sb_, ps):
            sc = sb_("sc", [P, 2, JB, 2])
            h_in = sb_("h_in", [P, 2, JB, HID])
            a_in = sb_("a_in", [P, 2, JB, HID])
            tmp = sb_("tmp", [P, 2, JB, HID])
            ho = sb_("ho", [P, 2, JB, HID])
            sq = sb_("sq", [P, 2, JB, HID])
            p_s = ps("s", [HID, 512])
            got, stored = [sem.many(f"got{k}_", 2) for k in range(3)], sem.many("stored", 2)
            made, own, squared, summed = sem("made"), sem("own"), sem("squared"), sem("summed")
            gate = sem("gate")
            with nc.Block() as block:
                @block.sync
                def _(sp):
                    def load(i, s, p, j):
                        wait(sp, made, i * 2 + (s - 1))
                        for k, (buf, table) in enumerate(((sc, dm), (h_in, g2), (a_in, agg[2]))):
                            sp.dma_start(buf[0:p, s, 0:j, :], group(table, i, s, p, j)).then_inc(got[k][s], 16)

                    def store(i, s, p, j):
                        sp.wait_ge(made, i * 2 + (s + 1))
                        sp.dma_start(group(r0, i, s, p, j), ho[0:p, s, 0:j, :]).then_inc(stored[s], 16)

                    pairs(sp, [(load, 0), (store, 2)], j=JB)
                    sp.wait_ge(stored[0], 16 * (pair_count(JB) + 1))
                    sp.wait_ge(stored[1], 16 * pair_count(JB))

                @block.vector
                def _(dve):
                    c_ = Chain(dve, own, gate)

                    def layer(i, s, p, j):
                        for k in range(3):
                            dve.wait_ge(got[k][s], i * 16 + 16)
                        wait(dve, stored[s], i * 16)
                        wait(dve, summed, i * 2 + (s - 1))
                        sum_bias(c_, a_in[0:p, s, 0:j, :], h_in[0:p, s, 0:j, :], sc[:, s], bias["g"], tmp[0:p, s, 0:j, :], p, j, False)
                        dve.tensor_scalar(ho[0:p, s, 0:j, :], tmp[0:p, s, 0:j, :], 0.0, None, ALU.max).then_inc(made, 1)

                    pairs(dve, [(layer, 0)], c_, 8, j=JB)
                    dve.wait_ge(summed, 2 * pair_count(JB) + 1)
                    dve.tensor_copy(stat0[:], p_s[:, 0:2]).then_inc(own, 1)

                @block.scalar
                def _(act):
                    def square(i, s, p, j):
                        act.wait_ge(made, i * 2 + (s + 1))
                        wait(act, summed, i * 2 + (s - 1))
                        act.activation(sq[0:p, s, 0:j, :], ho[0:p, s, 0:j, :], ACT.Square).then_inc(squared, 1)

                    pairs(act, [(square, 0)], j=JB)

                @block.tensor
                def _(pe):
                    def add(i, s, p, j):
                        pe.wait_ge(squared, i * 2 + (s + 1))
                        settle(pe, gate)
                        for k in range(j):
                            for c, buf in enumerate((ho, sq)):
                                m = pe.matmul(p_s[:, c:c + 1], buf[0:p, s, k, :], ones[0:p, 0:1], start=(isinstance(i, int) and i == 0 and s == 0 and k == 0 and c == 0),
                                              stop=(p == TAIL), skip_group_check=True)
                        m.then_inc(summed, 1)

                    pairs(pe, [(add, 0)], j=JB)

        wg1 = sb("wg1", [HID, D])
        wa1 = sb("wa1", [HID, HID + 2 * HEADS])
        wbd = sb("wbd", [P, 2, P])
        wg2 = sb("wg2", [P, 2, D + 2 * HEADS])
        scale0, shift0 = sb("scale0", [HID, 1]), sb("shift0", [HID, 1])
        with phase(nc, "gat_weights") as (sem, sb_, ps):
            arow = sb_("arow", [P, 4, D])
            prod = sb_("prod", [P, D])
            cols = sb_("cols", [HID, 3])
            tmp = sb_("tmp", [HID, 6])
            loaded, own, blank = sem("loaded"), sem("own"), sem("blank")
            gate = sem("gate")
            with nc.Block() as block:
                @block.sync
                def _(sp):
                    jobs = [(arow[:, k, :], a[n].rearrange("h c -> (h c)").rearrange("(o n) -> o n", o=1).to_broadcast([P, D])) for k, n in
                            enumerate(("L2_gnn_a_src1", "L2_gnn_a_dst1", "L2_gnn_a_src2", "L2_gnn_a_dst2"))]
                    jobs.append((wg1[:], a["L2_gnn_W1"]))
                    jobs.append((wg2[:, :, 0:D], a["L2_gnn_W2"].rearrange("(c p) n -> p c n", p=P)))
                    for k, n in enumerate(("L2_gnn_g0", "L2_gnn_beta0", "L2_gnn_b_gcn")):
                        jobs.append((cols[:, k:k + 1], a[n].rearrange("(n o) -> n o", o=1)))
                    for target, source in jobs:
                        sp.dma_start(target, source).then_inc(loaded, 16)
                    sp.wait_ge(blank, 1)
                    for h in range(HEADS):
                        q = (h % 2) * HID
                        sp.dma_start(wbd[q:q + HID, h // 2, q:q + HID], a["L2_gnn_W1"][:, h * HID:(h + 1) * HID]).then_inc(loaded, 16)
                    sp.wait_ge(loaded, 16 * 13)

                @block.vector
                def _(dve):
                    c_ = Chain(dve, own, gate)
                    dve.memset(wbd[:], 0.0).then_inc(blank, 1)
                    dve.wait_ge(loaded, 16 * 13)
                    c_(dve.tensor_copy(wa1[:, 0:HID], ident[0:HID, 0:HID]))
                    for k in range(2):
                        c_(dve.tensor_tensor(prod[0:HID, :], wg1[:], arow[0:HID, k, :], ALU.mult))
                        c_(dve.tensor_reduce(wa1[:, HID + k * HEADS:HID + (k + 1) * HEADS], prod[0:HID, :].rearrange("p (h c) -> p h c", c=HID),
                                             mybir.AxisListType.X, ALU.add))
                        for c in range(2):
                            c_(dve.tensor_tensor(prod[:], wg2[:, c, 0:D], arow[:, 2 + k, :], ALU.mult))
                            c_(dve.tensor_reduce(wg2[:, c, D + k * HEADS:D + (k + 1) * HEADS], prod[:].rearrange("p (h c) -> p h c", c=HID),
                                                 mybir.AxisListType.X, ALU.add))
                    zero = zeros[0:HID, 0:1]
                    batch_scale(c_, stat0[:, 0:1], stat0[:, 1:2], cols[:, 0:1], cols[:, 1:2], zero, scale0[:], shift0[:],
                                [tmp[:, k:k + 1] for k in range(6)])

        hb0, al1 = dram("hb0", (N, HID)), dram("al1", (N, 2 * HEADS))
        gram = sb("gram", [HID, HID + 1])
        with phase(nc, "fifth") as (sem, sb_, ps):
            sc = sb_("sc", [P, 2, JB, 2])
            r_in = sb_("r_in", [P, 2, JB, HID])
            ht = sb_("ht", [HID, 2, JB, P])
            hx = sb_("hx", [P, 2, JB, HID + 1])
            ho = sb_("ho", [P, 2, JB, HID])
            hm = sb_("hm", [P, 2, JB, HID])
            al = sb_("al", [P, 2, JB, 2 * HEADS])
            wide = HID + 2 * HEADS
            p_t = [ps(f"t{s}", [HID, 8, P]) for s in range(2)]
            p_h = [ps(f"h{s}", [P, 512]) for s in range(2)]
            p_g = ps("g", [HID, 512])
            got_r, got_s, st1, st2 = (sem.many(n, 2) for n in ("got_r", "got_s", "st1_", "st2_"))
            turned, normed, product, made, masked, summed, own = (sem(n) for n in ("turned", "normed", "product", "made", "masked", "summed", "own"))
            gate = sem("gate")
            with nc.Block() as block:
                @block.sync
                def _(sp):
                    def load(i, s, p, j):
                        wait(sp, turned, i * 2 + (s - 1))
                        sp.dma_start(r_in[0:p, s, 0:j, :], group(r0, i, s, p, j)).then_inc(got_r[s], 16)
                        wait(sp, masked, i * 2 + (s - 1))
                        sp.dma_start(sc[0:p, s, 0:j, :], group(dm, i, s, p, j)).then_inc(got_s[s], 16)

                    def store(i, s, p, j):
                        sp.wait_ge(made, i * 2 + (s + 1))
                        sp.dma_start(group(hb0, i, s, p, j), ho[0:p, s, 0:j, :]).then_inc(st1[s], 16)
                        sp.dma_start(group(al1, i, s, p, j), al[0:p, s, 0:j, :]).then_inc(st2[s], 16)

                    pairs(sp, [(load, 0), (store, 2)], j=JB)
                    for q in (st1, st2):
                        sp.wait_ge(q[0], 16 * (pair_count(JB) + 1))
                        sp.wait_ge(q[1], 16 * pair_count(JB))

                @block.tensor
                def _(pe):
                    def turn(i, s, p, j):
                        pe.wait_ge(got_r[s], i * 16 + 16)
                        wait(pe, normed, i * 2 + (s - 1))
                        settle(pe, gate)
                        for k in range(j):
                            m = pe.transpose(p_t[s][:, k, 0:p], r_in[0:p, s, k, :], ident[0:p, 0:p])
                        m.then_inc(turned, 1)

                    def mul(i, s, p, j):
                        pe.wait_ge(normed, i * 2 + (s + 1))
                        wait(pe, made, i * 2 + (s - 1))
                        settle(pe, gate)
                        for k in range(j):
                            m = pe.matmul(p_h[s][0:p, k * wide:(k + 1) * wide], ht[:, s, k, 0:p], wa1[:], start=True, stop=True)
                        m.then_inc(product, 1)

                    def add(i, s, p, j):
                        pe.wait_ge(masked, i * 2 + (s + 1))
                        settle(pe, gate)
                        for k in range(j):
                            m = pe.matmul(p_g[:, 0:HID + 1], hm[0:p, s, k, :], hx[0:p, s, k, :], start=(isinstance(i, int) and i == 0 and s == 0 and k == 0),
                                          stop=(p == TAIL), skip_group_check=True)
                        m.then_inc(summed, 1)

                    pairs(pe, [(turn, 0), (mul, 1), (add, 2)], j=JB)

                @block.scalar
                def _(act):
                    def norm(i, s, p, j):
                        act.wait_ge(turned, i * 2 + (s + 1))
                        wait(act, product, i * 2 + (s - 1))
                        act.activation(ht[:, s, 0:j, 0:p], p_t[s][:, 0:j, 0:p], ACT.Identity, scale=scale0[:], bias=shift0[:]).then_inc(normed, 1)

                    pairs(act, [(norm, 0)], j=JB)

                @block.vector
                def _(dve):
                    c_ = Chain(dve, own, gate)
                    c_(dve.memset(hx[:], 1.0))

                    def take(i, s, p, j):
                        dve.wait_ge(product, i * 2 + (s + 1))
                        dve.wait_ge(got_s[s], i * 16 + 16)
                        wait(dve, st1[s], i * 16)
                        wait(dve, st2[s], i * 16)
                        wait(dve, summed, i * 2 + (s - 1))
                        both = p_h[s][0:p, 0:j * wide].rearrange("p (j c) -> p j c", c=wide)
                        c_(dve.tensor_copy(ho[0:p, s, 0:j, :], both[:, :, 0:HID]))
                        c_(dve.tensor_copy(hx[0:p, s, 0:j, 0:HID], both[:, :, 0:HID]))
                        c_(dve.tensor_copy(al[0:p, s, 0:j, :], both[:, :, HID:wide]))
                        dve.sem_inc(made, 1)
                        dve.tensor_tensor(hm[0:p, s, 0:j, :], ho[0:p, s, 0:j, :], sc[0:p, s, 0:j, 1:2].to_broadcast([p, j, HID]), ALU.mult).then_inc(masked, 1)

                    pairs(dve, [(take, 0)], c_, 6, j=JB)
                    dve.wait_ge(summed, 2 * pair_count(JB) + 1)
                    c_(dve.tensor_copy(gram[:], p_g[:, 0:HID + 1]))

        w_edge, w_self, w_inv = (sb(n, [P, T, HEADS]) for n in ("w_edge", "w_self", "w_inv"))

        def attention(tag, al):
            with ExitStack() as told_ctx:
                t_src, t_dst = (told_ctx.enter_context(nc.sbuf_tensor(f"{tag}_{k}", [P, T, 2 * HEADS], F32)) for k in ("src", "dst"))
                small_rows(f"{tag}_scores", al, N, 2 * HEADS, [(dst_runs["other"], t_src), (dst_runs["node"], t_dst)])
                with phase(nc, tag) as (sem, sb_, ps):
                    g = dst_runs
                    e, es, most, back = (sb_(n, [P, T, HEADS]) for n in ("e", "es", "most", "back"))
                    edge = sb_("edge", [P, 4 * HEADS])
                    rows = sb_("rows", [2 * HEADS, P])
                    flat = sb_("flat", [HEADS, 8, P + 2])
                    carry_f, carry_b, carry_w = (sb_(n, [P, HEADS]) for n in ("carry_f", "carry_b", "carry_w"))
                    p_r = [ps(f"r{k}", [HEADS, 512]) for k in range(4)]
                    p_c = [ps(f"c{k}", [P, 512]) for k in range(3)]
                    own, ends, turned, rowed, colled = (sem(n) for n in ("own", "ends", "turned", "rowed", "colled"))
                    exps, first_w, carried = sem("exps"), sem("first_w"), sem("carried")
                    exp_in, exp_out = sem("exp_in"), sem("exp_out")
                    gate = sem("gate")
                    with nc.Block() as block:
                        @block.tensor
                        def _(pe):
                            pe.wait_ge(ends, 1)
                            for k in range(4):
                                m = pe.transpose(p_r[k][:, 0:P], edge[:, k * HEADS:(k + 1) * HEADS], ident[:])
                            m.then_inc(turned, 1)
                            pe.wait_ge(rowed, 1)
                            pe.transpose(p_c[0][:, 0:HEADS], flat[:, 4, 0:P], ident[0:HEADS, 0:HEADS])
                            pe.transpose(p_c[1][:, 0:HEADS], flat[:, 5, 2:P + 2], ident[0:HEADS, 0:HEADS]).then_inc(colled, 1)
                            pe.wait_ge(first_w, 1)
                            pe.matmul(p_c[2][:, 0:HEADS], g["carry"][:], edge[:, 0:HEADS], start=True, stop=True).then_inc(carried, 1)

                        @block.scalar
                        def _(act):
                            act.wait_ge(exp_in, 1)
                            act.activation(w_edge[:], e[:], ACT.Exp).then_inc(exp_out, 1)
                            act.activation(w_self[:], es[:], ACT.Exp).then_inc(exp_out, 1)

                        @block.vector
                        def _(dve):
                            c_ = Chain(dve, own, gate)
                            c_(dve.tensor_tensor(most[:], t_src[:, :, 0:HEADS], t_dst[:, :, HEADS:2 * HEADS], ALU.add))
                            c_(dve.scalar_tensor_tensor(e[:], most[:], 0.2, most[:], ALU.mult, ALU.max))
                            c_(dve.tensor_tensor(back[:], t_dst[:, :, 0:HEADS], t_dst[:, :, HEADS:2 * HEADS], ALU.add))
                            c_(dve.scalar_tensor_tensor(es[:], back[:], 0.2, back[:], ALU.mult, ALU.max))
                            for h in range(HEADS):
                                c_(dve.tensor_tensor_scan(most[:, :, h], g["pen"][:], e[:, :, h], NEG, ALU.add, ALU.max))
                                c_(dve.tensor_tensor_scan(back[:, ::-1, h], g["rpen"][:, ::-1], e[:, ::-1, h], NEG, ALU.add, ALU.max))
                            c_(dve.tensor_copy(edge[:, 0:HEADS], most[:, T - 1, :]))
                            c_(dve.tensor_copy(edge[:, HEADS:2 * HEADS], back[:, 0, :]))
                            c_(dve.tensor_copy(edge[:, 2 * HEADS:3 * HEADS], g["whole"][:, 0:1].to_broadcast([P, HEADS])))
                            c_(dve.tensor_copy(edge[:, 3 * HEADS:4 * HEADS], g["whole"][:, 1:2].to_broadcast([P, HEADS])))
                            dve.sem_inc(ends, 1)
                            dve.wait_ge(turned, 1)
                            for k in range(4):
                                c_(dve.tensor_copy(flat[:, k, 0:P], p_r[k][:, 0:P]))
                            c_(dve.memset(flat[:, 4:6, :], NEG))
                            c_(dve.tensor_tensor_scan(flat[:, 4, 1:P + 1], flat[:, 2, 0:P], flat[:, 0, 0:P], NEG, ALU.add, ALU.max))
                            c_(dve.tensor_tensor_scan(flat[:, 5, 1:P + 1][:, ::-1], flat[:, 3, 0:P][:, ::-1], flat[:, 1, 0:P][:, ::-1], NEG, ALU.add, ALU.max))
                            dve.sem_inc(rowed, 1)
                            dve.wait_ge(colled, 1)
                            c_(dve.tensor_copy(carry_f[:], p_c[0][:, 0:HEADS]))
                            c_(dve.tensor_copy(carry_b[:], p_c[1][:, 0:HEADS]))
                            for h in range(HEADS):
                                c_(dve.tensor_tensor_scan(most[:, :, h], g["pen"][:], e[:, :, h], carry_f[:, h:h + 1], ALU.add, ALU.max))
                                c_(dve.tensor_tensor_scan(back[:, ::-1, h], g["rpen"][:, ::-1], e[:, ::-1, h], carry_b[:, h:h + 1], ALU.add, ALU.max))
                            c_(dve.tensor_tensor(most[:], most[:], back[:], ALU.max))
                            c_(dve.tensor_tensor(most[:], most[:], es[:], ALU.max))
                            c_(dve.tensor_tensor(e[:], e[:], most[:], ALU.subtract))
                            c_(dve.tensor_tensor(es[:], es[:], most[:], ALU.subtract))
                            dve.sem_inc(exp_in, 1)
                            dve.wait_ge(exp_out, 2)
                            for h in range(HEADS):
                                c_(dve.tensor_tensor_scan(most[:, :, h], g["cont"][:], w_edge[:, :, h], 0.0, ALU.mult, ALU.add))
                            c_(dve.tensor_copy(edge[:, 0:HEADS], most[:, T - 1, :]))
                            dve.sem_inc(first_w, 1)
                            dve.wait_ge(carried, 1)
                            c_(dve.tensor_copy(carry_w[:], p_c[2][:, 0:HEADS]))
                            for h in range(HEADS):
                                c_(dve.tensor_tensor_scan(most[:, :, h], g["cont"][:], w_edge[:, :, h], carry_w[:, h:h + 1], ALU.mult, ALU.add))
                            c_(dve.tensor_tensor(most[:], most[:], w_self[:], ALU.add))
                            c_(dve.tensor_scalar(most[:], most[:], 1.0e-30, None, ALU.max))
                            c_(dve.reciprocal(w_inv[:], most[:]))

        attention("soft1", al1)
        rg1, ue1 = dram("rg1", (ROWS, D)), dram("ue1", (ROWS, D))
        edge_sum("gat1", "d", hb0, N, dst_runs["other"], HID, rg1, False, weights=w_edge)

        stat1 = sb("stat1", [P, 4])

        def attention_ends(tag, rg, table, width, ue, stat, blocks):
            with phase(nc, tag) as (sem, sb_, ps):
                g = dst_runs
                r_in = sb_("r_in", [P, B, D])
                hg = sb_("hg", [P, B, width])
                z = sb_("z", [P, B, D])
                zt = sb_("zt", [P, 2, 2, P])
                u = sb_("u", [P, B, D])
                sq = sb_("sq", [P, 2, D])
                idx = sb_("idx", [P, B], I32)
                p_t = [ps(f"t{k}", [P, 2, P]) for k in range(2)]
                p_y = [ps(f"y{k}", [P, 512]) for k in range(2)]
                p_s = ps("s", [P, 512])
                loaded, got, stored = (sem.many(n, B) for n in ("loaded", "got", "stored"))
                fed, own, z_made, turned, copied, product, made, squared, summed = (sem(n) for n in
                    ("fed", "own", "z_made", "turned", "copied", "product", "made", "squared", "summed"))
                gate = sem("gate")
                with nc.Block() as block:
                    @block.sync
                    def _(sp):
                        def load(i, b):
                            wait(sp, z_made, i * B + (b + 1 - B))
                            sp.dma_start(r_in[:, b, :], rg[bass.ds(i * (B * P) + b * P, P), :]).then_inc(loaded[b], 16)

                        def store(i, b):
                            sp.wait_ge(made, i * B + (b + 1))
                            sp.dma_start(ue[bass.ds(i * (B * P) + b * P, P), :], u[:, b, :]).then_inc(stored[b], 16)

                        columns(sp, [(load, 0), (store, 8)])
                        for q in stored:
                            sp.wait_ge(q, 16 * STEPS)

                    @block.gpsimd
                    def _(pool):
                        last = pool.to_reg(N - 1)
                        feed = Feed(pool, gate, fed, idx, g["node"], got)

                        def gather(i, b):
                            wait(pool, z_made, i * B + (b + 1 - B))
                            pool.indirect_dma_start(hg[:, b, :], None, table, feed.at(b), bounds_check=last, oob_is_err=False).then_inc(got[b], 16)

                        indexed(pool, gather, [feed])

                    @block.vector
                    def _(dve):
                        c_ = Chain(dve, own, gate)
                        heads = lambda x: x.rearrange("p (h c) -> p h c", c=HID)
                        by_head = lambda x, t: x[:, bass.ds(t, 1), :].rearrange("p a h -> p (a h)").unsqueeze(2).to_broadcast([P, HEADS, HID])

                        def mix(i, b):
                            t = i * B + b
                            dve.wait_ge(got[b], i * 16 + 16)
                            dve.wait_ge(loaded[b], i * 16 + 16)
                            wait(dve, turned if blocks is not None else made, i * B + (b + 1 - B))
                            own_row_ = heads(hg[:, b, :])
                            if width == HID:
                                own_row_ = own_row_.to_broadcast([P, HEADS, HID])
                            c_(dve.tensor_tensor(heads(z[:, b, :]), own_row_, by_head(w_self, t), ALU.mult))
                            dve.tensor_tensor(z[:, b, :], z[:, b, :], r_in[:, b, :], ALU.add).then_inc(z_made, 1)

                        def divide(i, b):
                            t = i * B + b
                            if blocks is not None:
                                dve.wait_ge(product, t + 1)
                                of = heads(p_y[b % 2][:, 0:D])
                            else:
                                dve.wait_ge(z_made, t + 1)
                                of = heads(z[:, b, :])
                            wait(dve, stored[b], i * 16)
                            wait(dve, summed, i * B + (b + 1 - B))
                            dve.tensor_tensor(heads(u[:, b, :]), of, by_head(w_inv, t), ALU.mult).then_inc(made, 1)

                        columns(dve, [(mix, 0), (divide, 2)], c_, B)
                        dve.wait_ge(summed, T)
                        c_(dve.tensor_copy(stat[:], p_s[:, 0:4]))

                    @block.scalar
                    def _(act):
                        def copy(i, b):
                            act.wait_ge(turned, i * B + (b + 1))
                            wait(act, product, i * B + (b - 1))
                            act.activation(zt[:, b % 2], p_t[b % 2][:], ACT.Copy).then_inc(copied, 1)

                        def square(i, b):
                            act.wait_ge(made, i * B + (b + 1))
                            wait(act, summed, i * B + (b - 1))
                            act.activation(sq[:, b % 2, :], u[:, b, :], ACT.Square).then_inc(squared, 1)

                        columns(act, ([(copy, 0)] if blocks is not None else []) + [(square, 2)])

                    @block.tensor
                    def _(pe):
                        def turn(i, b):
                            pe.wait_ge(z_made, i * B + (b + 1))
                            wait(pe, copied, i * B + (b - 1))
                            for c in range(2):
                                m = pe.transpose(p_t[b % 2][:, c, :], z[:, b, c * P:(c + 1) * P], ident[:])
                            m.then_inc(turned, 1)

                        def mul(i, b):
                            pe.wait_ge(copied, i * B + (b + 1))
                            wait(pe, made, i * B + (b - 1))
                            for c in range(2):
                                m = pe.matmul(p_y[b % 2][:, c * P:(c + 1) * P], zt[:, b % 2, c, :], blocks[:, c, :], start=True, stop=True)
                            m.then_inc(product, 1)

                        def add(i, b):
                            t = i * B + b
                            pe.wait_ge(squared, t + 1)
                            settle(pe, gate)
                            for k in range(4):
                                buf = u[:, b, (k % 2) * P:(k % 2 + 1) * P] if k < 2 else sq[:, b % 2, (k % 2) * P:(k % 2 + 1) * P]
                                m = pe.matmul(p_s[:, k:k + 1], buf, g["endm"][:, bass.ds(t, 1)], start=(isinstance(i, int) and i == 0 and b == 0 and k == 0),
                                              stop=False, skip_group_check=True)
                            m.then_inc(summed, 1)

                        columns(pe, ([(turn, 0), (mul, 1)] if blocks is not None else []) + [(add, 3)])

        attention_ends("gat1_ends", rg1, hb0, HID, ue1, stat1, wbd)

        scale1, shift1 = sb("scale1", [P, 2]), sb("shift1", [P, 2])
        with phase(nc, "norm1") as (sem, sb_, ps):
            gw = sb_("gw", [HID, D])
            cols1 = sb_("cols1", [P, 3, 2])
            tmp = sb_("tmp", [P, 6, 2])
            stat = sb_("stat", [P, 4])
            p_w = ps("w", [HID, 512])
            p_s = ps("s", [P, 512])
            loaded, own, gw_made, prod_made, done = (sem(n) for n in ("loaded", "own", "gw_made", "prod_made", "done"))
            gate = sem("gate")
            with nc.Block() as block:
                @block.sync
                def _(sp):
                    for k, n in enumerate(("L2_gnn_g1", "L2_gnn_beta1", "L2_gnn_b1")):
                        for c in range(2):
                            sp.dma_start(cols1[:, k, c:c + 1], a[n][c * P:(c + 1) * P].rearrange("(n o) -> n o", o=1)).then_inc(loaded, 16)
                    sp.wait_ge(loaded, 16 * 6)

                @block.tensor
                def _(pe):
                    pe.matmul(p_w[:, 0:D], gram[:, 0:HID], wg1[:], start=True, stop=True).then_inc(gw_made, 1)
                    pe.wait_ge(prod_made, 1)
                    for c in range(2):
                        pe.matmul(p_s[:, c:c + 1], wg1[:, c * P:(c + 1) * P], gram[:, HID:HID + 1], start=(c == 0), stop=False, skip_group_check=True)
                    for c in range(2):
                        m = pe.matmul(p_s[:, 2 + c:3 + c], gw[:, c * P:(c + 1) * P], ones[0:HID, 0:1], start=False, stop=(c == 1), skip_group_check=True)
                    m.then_inc(done, 1)

                @block.vector
                def _(dve):
                    c_ = Chain(dve, own, gate)
                    dve.wait_ge(gw_made, 1)
                    c_(dve.tensor_tensor(gw[:], p_w[:, 0:D], wg1[:], ALU.mult))
                    dve.sem_inc(prod_made, 1)
                    dve.wait_ge(done, 1)
                    dve.wait_ge(loaded, 16 * 6)
                    c_(dve.tensor_tensor(stat[:], p_s[:, 0:4], stat1[:], ALU.add))
                    batch_scale(c_, stat[:, 0:2], stat[:, 2:4], cols1[:, 0, :], cols1[:, 1, :], cols1[:, 2, :], scale1[:], shift1[:],
                                [tmp[:, k, :] for k in range(6)])

        wide2 = D + 2 * HEADS
        hh, al2 = dram("hh", (N, D)), dram("al2", (N, 2 * HEADS))
        stat2a, stat2 = sb("stat2a", [P, 4]), sb("stat2", [P, 4])
        with phase(nc, "sixth") as (sem, sb_, ps):
            sc = sb_("sc", [P, 2, J, 2])
            h_in = sb_("h_in", [P, 2, J, HID])
            ht = sb_("ht", [HID, 2, J, P])
            z, low, ex, e1 = (sb_(n, [P, 2, 2, J, P]) for n in ("z", "low", "ex", "e1"))
            ho = sb_("ho", [P, 2, J, D])
            sq = sb_("sq", [P, 2, J, D])
            al = sb_("al", [P, 2, J, 2 * HEADS])
            p_t = ps("t", [HID, 4, P])
            p_u = [ps(f"u{c}", [P, 4, P]) for c in range(2)]
            p_h = ps("h", [P, J, 512])
            p_s = ps("s", [P, 512])
            got_h, got_s, st1, st2 = (sem.many(n, 2) for n in ("got_h", "got_s", "st1_", "st2_"))
            turned, copied, u_made, z_made, low_made, exped, e_made, h_made, taken, squared, summed, own = (sem(n) for n in
                ("turned", "copied", "u_made", "z_made", "low_made", "exped", "e_made", "h_made", "taken", "squared", "summed", "own"))
            gate = sem("gate")
            with nc.Block() as block:
                @block.sync
                def _(sp):
                    def load(i, s, p, j):
                        wait(sp, turned, i * 2 + (s - 1))
                        sp.dma_start(h_in[0:p, s, 0:j, :], group(hb0, i, s, p, j)).then_inc(got_h[s], 16)

                    def load_scale(i, s, p, j):
                        wait(sp, summed, i * 2 + (s - 1))
                        sp.dma_start(sc[0:p, s, 0:j, :], group(dm, i, s, p, j)).then_inc(got_s[s], 16)

                    def store(i, s, p, j):
                        sp.wait_ge(taken, i * 2 + (s + 1))
                        sp.dma_start(group(hh, i, s, p, j), ho[0:p, s, 0:j, :]).then_inc(st1[s], 16)
                        sp.dma_start(group(al2, i, s, p, j), al[0:p, s, 0:j, :]).then_inc(st2[s], 16)

                    pairs(sp, [(load, 0), (load_scale, 2), (store, 4)])
                    for q in (st1, st2):
                        sp.wait_ge(q[0], 16 * (PAIRS + 1))
                        sp.wait_ge(q[1], 16 * PAIRS)

                @block.tensor
                def _(pe):
                    def turn(i, s, p, j):
                        pe.wait_ge(got_h[s], i * 16 + 16)
                        wait(pe, copied, i * 2 + s)
                        settle(pe, gate)
                        for k in range(j):
                            m = pe.transpose(p_t[:, k, 0:p], h_in[0:p, s, k, :], ident[0:p, 0:p])
                        m.then_inc(turned, 1)

                    def mul_u(i, s, p, j):
                        pe.wait_ge(copied, i * 2 + (s + 1))
                        wait(pe, z_made, i * 2 + s)
                        rows = ht[:, s, 0, 0:p] if j == 1 else ht[:, s].rearrange("p j q -> p (j q)")
                        for c in range(2):
                            to = p_u[c][:, 0, 0:p] if j == 1 else p_u[c][:, 0:j, :].rearrange("p j q -> p (j q)")
                            m = pe.matmul(to, wg1[:, c * P:(c + 1) * P], rows, start=True, stop=True)
                        m.then_inc(u_made, 1)

                    def mul_h(i, s, p, j):
                        pe.wait_ge(e_made, i * 2 + (s + 1))
                        wait(pe, taken, i * 2 + s)
                        for k in range(j):
                            for c in range(2):
                                m = pe.matmul(p_h[0:p, k, 0:wide2], e1[:, s, c, k, 0:p], wg2[:, c, :], start=(c == 0), stop=(c == 1))
                        m.then_inc(h_made, 1)

                    def add(i, s, p, j):
                        pe.wait_ge(squared, i * 2 + (s + 1))
                        pe.wait_ge(got_s[s], i * 16 + 16)
                        settle(pe, gate)
                        for k in range(j):
                            for c in range(4):
                                buf = (ho, sq)[c // 2]
                                m = pe.matmul(p_s[:, c:c + 1], buf[0:p, s, k, (c % 2) * P:(c % 2 + 1) * P], sc[0:p, s, k, 1:2],
                                              start=(isinstance(i, int) and i == 0 and s == 0 and k == 0 and c == 0),
                                              stop=(p == TAIL), skip_group_check=True)
                        m.then_inc(summed, 1)

                    pairs(pe, [(turn, 0), (mul_u, 1), (mul_h, 2), (add, 3)])

                @block.scalar
                def _(act):
                    def copy(i, s, p, j):
                        act.wait_ge(turned, i * 2 + (s + 1))
                        wait(act, u_made, i * 2 + (s - 1))
                        act.activation(ht[:, s, 0:j, 0:p], p_t[:, 0:j, 0:p], ACT.Copy).then_inc(copied, 1)

                    def norm(i, s, p, j):
                        act.wait_ge(u_made, i * 2 + (s + 1))
                        wait(act, e_made, i * 2 + (s - 1))
                        for c in range(2):
                            m = act.activation(z[:, s, c, 0:j, 0:p], p_u[c][:, 0:j, 0:p], ACT.Identity, scale=scale1[:, c:c + 1], bias=shift1[:, c:c + 1])
                        m.then_inc(z_made, 1)

                    def exp(i, s, p, j):
                        act.wait_ge(low_made, i * 2 + (s + 1))
                        wait(act, e_made, i * 2 + (s - 1))
                        for c in range(2):
                            m = act.activation(ex[:, s, c, 0:j, 0:p], low[:, s, c, 0:j, 0:p], ACT.Exp)
                        m.then_inc(exped, 1)

                    def square(i, s, p, j):
                        act.wait_ge(taken, i * 2 + (s + 1))
                        wait(act, summed, i * 2 + (s - 1))
                        act.activation(sq[0:p, s, 0:j, :], ho[0:p, s, 0:j, :], ACT.Square).then_inc(squared, 1)

                    pairs(act, [(copy, 0), (square, 3), (norm, 1), (exp, 1)])

                @block.vector
                def _(dve):
                    def fall_(i, s, p, j):
                        dve.wait_ge(z_made, i * 2 + (s + 1))
                        wait(dve, exped, i * 2 + (s - 1))
                        for c in range(2):
                            m = dve.tensor_scalar(low[:, s, c, 0:j, 0:p], z[:, s, c, 0:j, 0:p], 0.0, None, ALU.min)
                        m.then_inc(low_made, 1)

                    def elu(i, s, p, j):
                        dve.wait_ge(exped, i * 2 + (s + 1))
                        wait(dve, h_made, i * 2 + (s - 1))
                        for c in range(2):
                            m = dve.scalar_tensor_tensor(e1[:, s, c, 0:j, 0:p], ex[:, s, c, 0:j, 0:p], -1.0, z[:, s, c, 0:j, 0:p], ALU.add, ALU.max)
                        m.then_inc(e_made, 1)

                    def take(i, s, p, j):
                        dve.wait_ge(h_made, i * 2 + (s + 1))
                        wait(dve, st1[s], i * 16)
                        wait(dve, st2[s], i * 16)
                        wait(dve, summed, i * 2 + (s - 1))
                        dve.tensor_copy(ho[0:p, s, 0:j, :], p_h[0:p, 0:j, 0:D])
                        dve.tensor_copy(al[0:p, s, 0:j, :], p_h[0:p, 0:j, D:wide2]).then_inc(taken, 1)

                    pairs(dve, [(fall_, 1), (elu, 1), (take, 2)])
                    dve.wait_ge(summed, 2 * PAIRS + 1)
                    dve.tensor_copy(stat2a[:], p_s[:, 0:4]).then_inc(own, 1)

        with phase(nc, "hh_ends") as (sem, sb_, ps):
            g = dst_runs
            r_in = sb_("r_in", [P, B, D])
            z, low, ex, e1 = (sb_(n, [P, 2, 2, P]) for n in ("z", "low", "ex", "e1"))
            ho = sb_("ho", [P, B, D])
            al = sb_("al", [P, B, 2 * HEADS])
            put1, put2 = (sb_(n, [P, B], I32) for n in ("put1", "put2"))
            p_t = [ps(f"t{k}", [P, 4, P]) for k in range(2)]
            p_h = [ps(f"h{k}", [P, 512]) for k in range(2)]
            loaded, st1, st2 = (sem.many(n, B) for n in ("loaded", "st1_", "st2_"))
            fed1, fed2, turned, z_made, low_made, exped, e_made, h_made, taken = (sem(n) for n in
                ("fed1", "fed2", "turned", "z_made", "low_made", "exped", "e_made", "h_made", "taken"))
            gate = sem("gate")
            with nc.Block() as block:
                @block.sync
                def _(sp):
                    def load(i, b):
                        wait(sp, turned, i * B + (b + 1 - B))
                        sp.dma_start(r_in[:, b, :], ue1[bass.ds(i * (B * P) + b * P, P), :]).then_inc(loaded[b], 16)

                    columns(sp, [(load, 0)])

                @block.tensor
                def _(pe):
                    def turn(i, b):
                        pe.wait_ge(loaded[b], i * 16 + 16)
                        wait(pe, z_made, i * B + (b - 1))
                        for c in range(2):
                            m = pe.transpose(p_t[b % 2][:, c, :], r_in[:, b, c * P:(c + 1) * P], ident[:])
                        m.then_inc(turned, 1)

                    def mul(i, b):
                        pe.wait_ge(e_made, i * B + (b + 1))
                        wait(pe, taken, i * B + (b - 1))
                        for c in range(2):
                            m = pe.matmul(p_h[b % 2][:, 0:wide2], e1[:, b % 2, c, :], wg2[:, c, :], start=(c == 0), stop=(c == 1))
                        m.then_inc(h_made, 1)

                    columns(pe, [(turn, 0), (mul, 2)])

                @block.scalar
                def _(act):
                    def norm(i, b):
                        act.wait_ge(turned, i * B + (b + 1))
                        wait(act, e_made, i * B + (b - 1))
                        for c in range(2):
                            m = act.activation(z[:, b % 2, c, :], p_t[b % 2][:, c, :], ACT.Identity, scale=scale1[:, c:c + 1], bias=shift1[:, c:c + 1])
                        m.then_inc(z_made, 1)

                    def exp(i, b):
                        act.wait_ge(low_made, i * B + (b + 1))
                        wait(act, e_made, i * B + (b - 1))
                        act.activation(ex[:, b % 2], low[:, b % 2], ACT.Exp).then_inc(exped, 1)

                    columns(act, [(norm, 0), (exp, 1)])

                @block.vector
                def _(dve):
                    def fall_(i, b):
                        dve.wait_ge(z_made, i * B + (b + 1))
                        wait(dve, exped, i * B + (b - 1))
                        dve.tensor_scalar(low[:, b % 2], z[:, b % 2], 0.0, None, ALU.min).then_inc(low_made, 1)

                    def elu(i, b):
                        dve.wait_ge(exped, i * B + (b + 1))
                        wait(dve, h_made, i * B + (b - 1))
                        dve.scalar_tensor_tensor(e1[:, b % 2], ex[:, b % 2], -1.0, z[:, b % 2], ALU.add, ALU.max).then_inc(e_made, 1)

                    def take(i, b):
                        dve.wait_ge(h_made, i * B + (b + 1))
                        wait(dve, st1[b], i * 16)
                        wait(dve, st2[b], i * 16)
                        dve.tensor_copy(ho[:, b, :], p_h[b % 2][:, 0:D])
                        dve.tensor_copy(al[:, b, :], p_h[b % 2][:, D:wide2]).then_inc(taken, 1)

                    columns(dve, [(fall_, 0), (elu, 1), (take, 2)])

                @block.gpsimd
                def _(pool):
                    last = pool.to_reg(N - 1)
                    feed1 = Feed(pool, gate, fed1, put1, g["put"], st1)
                    feed2 = Feed(pool, gate, fed2, put2, g["put"], st2)

                    def scatter(i, b):
                        pool.wait_ge(taken, i * B + (b + 1))
                        pool.indirect_dma_start(hh, feed1.at(b), ho[:, b, :], None, bounds_check=last, oob_is_err=False).then_inc(st1[b], 16)
                        pool.indirect_dma_start(al2, feed2.at(b), al[:, b, :], None, bounds_check=last, oob_is_err=False).then_inc(st2[b], 16)

                    indexed(pool, None, [], scatter, [feed1, feed2])
                    for q in st1 + st2:
                        pool.wait_ge(q, 16 * STEPS)

        attention("soft2", al2)
        rg2, ue2 = dram("rg2", (ROWS, D)), dram("ue2", (ROWS, D))
        edge_sum("gat2", "d", hh, N, dst_runs["other"], D, rg2, False, weights=w_edge)
        attention_ends("gat2_ends", rg2, hh, D, ue2, stat2, None)

        def batch_norm(tag, stats, gamma, beta, b, scale, shift, rows):
            with phase(nc, tag) as (sem, sb_, ps):
                tmp = sb_("tmp", [P, 6, 2])
                cols = sb_("cols", [P, 3, 2])
                stat = sb_("stat", [P, 4])
                diag = sb_("diag", [P, 4, P])
                p_r = ps("r", [P, 512])
                loaded, own, diag_made, rowed = (sem(n) for n in ("loaded", "own", "diag_made", "rowed"))
                params = [gamma, beta] + ([b] if b is not None else [])
                gate = sem("gate")
                with nc.Block() as block:
                    @block.sync
                    def _(sp):
                        for k, x in enumerate(params):
                            for c in range(2):
                                sp.dma_start(cols[:, k, c:c + 1], x[c * P:(c + 1) * P].rearrange("(n o) -> n o", o=1)).then_inc(loaded, 16)
                        sp.wait_ge(loaded, 32 * len(params))

                    @block.tensor
                    def _(pe):
                        pe.wait_ge(diag_made, 1)
                        for k in range(4):
                            m = pe.matmul(p_r[:, k * P:(k + 1) * P], ones[:], diag[:, k, :], start=True, stop=True)
                        m.then_inc(rowed, 1)

                    @block.vector
                    def _(dve):
                        c_ = Chain(dve, own, gate)
                        dve.wait_ge(loaded, 32 * len(params))
                        total = stats[0]
                        if len(stats) > 1:
                            c_(dve.tensor_tensor(stat[:], stats[0][:], stats[1][:], ALU.add))
                            total = stat
                        batch_scale(c_, total[:, 0:2], total[:, 2:4], cols[:, 0, :], cols[:, 1, :], cols[:, 2, :] if b is not None else zeros[:, 0:2],
                                    scale[:], shift[:], [tmp[:, k, :] for k in range(6)])
                        for k in range(4):
                            c_(dve.tensor_scalar(diag[:, k, :], ident[:], (scale, shift)[k // 2][:, k % 2:k % 2 + 1], None, ALU.mult))
                        dve.sem_inc(diag_made, 1)
                        dve.wait_ge(rowed, 1)
                        c_(dve.tensor_copy(rows[:].rearrange("p k c -> p (k c)"), p_r[:]))

        scale2, shift2, rows2 = sb("scale2", [P, 2]), sb("shift2", [P, 2]), sb("rows2", [P, 2, D])
        batch_norm("norm2", [stat2a, stat2], a["L2_gnn_g2"], a["L2_gnn_beta2"], a["L2_gnn_b2"], scale2, shift2, rows2)

        x3 = dram("x3", (N, D))
        with phase(nc, "seventh") as (sem, sb_, ps):
            h_in, x_in, t, r, v, xo = (sb_(n, [P, 2, JB, D]) for n in ("h_in", "x_in", "t", "r", "v", "xo"))
            st = norm_slots(sb_, "n", JB)
            got_h, got_x, stored = (sem.many(n, 2) for n in ("got_h", "got_x", "stored"))
            own, scaled, t_made, exped, stats, made = (sem(n) for n in ("own", "scaled", "t_made", "exped", "stats", "made"))
            sunk, gate = sem("sunk"), sem("gate")
            with nc.Block() as block:
                @block.sync
                def _(sp):
                    def load(i, s, p, j):
                        wait(sp, t_made, i * 2 + (s - 1))
                        sp.dma_start(h_in[0:p, s, 0:j, :], group(hh, i, s, p, j)).then_inc(got_h[s], 16)
                        wait(sp, stats, i * 2 + (s - 1))
                        sp.dma_start(x_in[0:p, s, 0:j, :], group(x2, i, s, p, j)).then_inc(got_x[s], 16)

                    def store(i, s, p, j):
                        sp.wait_ge(made, i * 2 + (s + 1))
                        sp.dma_start(group(x3, i, s, p, j), xo[0:p, s, 0:j, :]).then_inc(stored[s], 16)

                    pairs(sp, [(load, 0), (store, 3)], j=JB)
                    sp.wait_ge(stored[0], 16 * (pair_count(JB) + 1))
                    sp.wait_ge(stored[1], 16 * pair_count(JB))

                @block.gpsimd
                def _(pool):
                    def norm(i, s, p, j):
                        pool.wait_ge(got_h[s], i * 16 + 16)
                        wait(pool, stats, i * 2 + (s - 1))
                        row = lambda k: rows2[0:p, k, :].unsqueeze(1).to_broadcast([p, j, D])
                        h = h_in[0:p, s, 0:j, :]
                        pool.tensor_tensor(h, h, row(0), ALU.mult).then_inc(scaled, 1)
                        pool.wait_ge(scaled, i * 2 + (s + 1))
                        pool.tensor_tensor(t[0:p, s, 0:j, :], h, row(1), ALU.add).then_inc(t_made, 1)

                    pairs(pool, [(norm, 0)], j=JB)

                @block.scalar
                def _(act):
                    def exp(i, s, p, j):
                        act.wait_ge(t_made, i * 2 + (s + 1))
                        wait(act, stats, i * 2 + (s - 1))
                        at = r[0:p, s, 0:j, :]
                        act.activation(at, t[0:p, s, 0:j, :], ACT.Relu, scale=-1.0).then_inc(sunk, 1)
                        act.wait_ge(sunk, i * 2 + (s + 1))
                        act.activation(at, at, ACT.Exp, scale=-1.0).then_inc(exped, 1)

                    def norm(i, s, p, j):
                        act.wait_ge(stats, i * 2 + (s + 1))
                        wait(act, stored[s], i * 16)
                        normalize(act, v[:, s], xo[:, s], st, s, p, j).then_inc(made, 1)

                    pairs(act, [(exp, 0), (norm, 2)], j=JB)

                @block.vector
                def _(dve):
                    c_ = Chain(dve, own, gate)

                    def rest(i, s, p, j):
                        dve.wait_ge(exped, i * 2 + (s + 1))
                        dve.wait_ge(got_x[s], i * 16 + 16)
                        wait(dve, made, i * 2 + (s - 1))
                        at = v[0:p, s, 0:j, :]
                        c_(dve.scalar_tensor_tensor(at, r[0:p, s, 0:j, :], -1.0, t[0:p, s, 0:j, :], ALU.add, ALU.max))
                        c_(dve.tensor_tensor(at, at, x_in[0:p, s, 0:j, :], ALU.add))
                        norm_stats(c_, v[:, s], st, s, p, j)
                        dve.sem_inc(stats, 1)

                    pairs(dve, [(rest, 1)], c_, 2 * (2 + 2 * JB + 13), j=JB)

        def node_ends(tag, g, rows_table, gathered, target, rows, elu):
            with phase(nc, tag) as (sem, sb_, ps):
                r_in = sb_("r_in", [P, B, D])
                xg = sb_("xg", [P, B, D])
                t = sb_("t", [P, B, D])
                low = sb_("low", [P, B, D]) if elu else None
                xo = sb_("xo", [P, B, D])
                idx, put = sb_("idx", [P, B], I32), sb_("put", [P, B], I32)
                st = norm_buffers(sb_, HALF)
                loaded, got, stored = (sem.many(n, B) for n in ("loaded", "got", "stored"))
                fed, fed_put, own, t_made, sunk, exped, made = (sem(n) for n in ("fed", "fed_put", "own", "t_made", "sunk", "exped", "made"))
                gate = sem("gate")
                with nc.Block() as block:
                    @block.sync
                    def _(sp):
                        def load(i, b):
                            wait(sp, t_made, i * 2 + (b // HALF - 1))
                            sp.dma_start(r_in[:, b, :], rows_table[bass.ds(i * (B * P) + b * P, P), :]).then_inc(loaded[b], 16)

                        columns(sp, [(load, 0)])

                    @block.gpsimd
                    def _(pool):
                        last = pool.to_reg(N - 1)
                        feed = Feed(pool, gate, fed, idx, g["node"], got)
                        feed_put = Feed(pool, gate, fed_put, put, g["put"], stored)

                        def gather(i, b):
                            wait(pool, made, i * B + (b + 1 - B))
                            pool.indirect_dma_start(xg[:, b, :], None, gathered, feed.at(b), bounds_check=last, oob_is_err=False).then_inc(got[b], 16)

                        def scatter(i, b):
                            pool.wait_ge(made, i * B + (b + 1))
                            pool.indirect_dma_start(target, feed_put.at(b), xo[:, b, :], None, bounds_check=last, oob_is_err=False).then_inc(stored[b], 16)

                        indexed(pool, gather, [feed], scatter, [feed_put], behind=2)
                        for q in stored:
                            pool.wait_ge(q, 16 * STEPS)

                    @block.scalar
                    def _(act):
                        def exp(i, b):
                            if b % HALF == HALF - 1:
                                n = i * 2 + (b + 1) // HALF
                                act.wait_ge(t_made, n)
                                wait(act, made, i * B + (b + 1 - B))
                                lows = low[:, b + 1 - HALF:b + 1, :]
                                act.activation(lows, t[:, b + 1 - HALF:b + 1, :], ACT.Relu, scale=-1.0).then_inc(sunk, 1)
                                act.wait_ge(sunk, n)
                                act.activation(lows, lows, ACT.Exp, scale=-1.0).then_inc(exped, 1)

                        if elu:
                            columns(act, [(exp, 0)])

                    @block.vector
                    def _(dve):
                        c_ = Chain(dve, own, gate)

                        def norm(i, b):
                            if b % HALF != HALF - 1:
                                return
                            lo, hi = b + 1 - HALF, b + 1
                            for q in range(lo, hi):
                                dve.wait_ge(loaded[q], i * 16 + 16)
                            r = r_in[:, lo:hi, :]
                            row = lambda k: rows[:, k, :].unsqueeze(1).to_broadcast([P, HALF, D])
                            c_(dve.tensor_tensor(r, r, row(0), ALU.mult))
                            c_(dve.tensor_tensor(t[:, lo:hi, :], r, row(1), ALU.add))
                            dve.sem_inc(t_made, 1)

                        def rest(i, b):
                            if b % HALF != HALF - 1:
                                return
                            lo, hi = b + 1 - HALF, b + 1
                            if elu:
                                dve.wait_ge(exped, i * 2 + hi // HALF)
                            for q in range(lo, hi):
                                dve.wait_ge(got[q], i * 16 + 16)
                                wait(dve, stored[q], i * 16)
                            r, x = t[:, lo:hi, :], xg[:, lo:hi, :]
                            if elu:
                                c_(dve.scalar_tensor_tensor(r, low[:, lo:hi, :], -1.0, r, ALU.add, ALU.max))
                                c_(dve.tensor_tensor(r, r, x, ALU.add))
                            else:
                                c_(dve.scalar_tensor_tensor(r, r, 0.0, x, ALU.max, ALU.add))
                            layer_norm(c_, r, xo[:, lo:hi, :], st, P, HALF)
                            dve.sem_inc(made, HALF)

                        columns(dve, [(norm, 0), (rest, HALF if elu else 0)], c_, 2 * (2 + (2 if elu else 1) + 3 * HALF + 12))

        node_ends("x3_ends", dst_runs, ue2, x2, x3, rows2, True)

        top = [dram(f"top{l}", (ROWS + 1, D)) for l in range(3)]
        wt, wp = sb("wt", [P, 3, 2, D]), sb("wp", [P, 3, 2, D])
        fixes = sb("fixes", [P, 1])
        whole_row = sb("whole_row", [P, P])
        with phase(nc, "maps") as (sem, sb_, ps):
            raw = sb_("raw", [P, 6, 2, D])
            diag = sb_("diag", [P, P])
            p_m = [ps(f"m{k}", [P, 2, D]) for k in range(6)]
            p_w = ps("w", [P, 512])
            loaded, own, turned, diag_made, rowed, stored = (sem(n) for n in ("loaded", "own", "turned", "diag_made", "rowed", "stored"))
            with nc.Block() as block:
                @block.sync
                def _(sp):
                    for l in range(3):
                        for k, n in enumerate(("L3_gnn_thetas", "L3_gnn_phis")):
                            sp.dma_start(raw[:, 2 * l + k], a[n][l].rearrange("(c p) f -> p c f", p=P)).then_inc(loaded, 16)
                    for table in top:
                        sp.dma_start(table[ROWS:ROWS + 1, :], zeros[0:1, 0:D]).then_inc(stored, 16)
                    sp.wait_ge(stored, 48)

                @block.tensor
                def _(pe):
                    pe.wait_ge(diag_made, 1)
                    pe.matmul(p_w[:, 0:P], ones[:], diag[:], start=True, stop=True).then_inc(rowed, 1)
                    pe.wait_ge(loaded, 96)
                    for m in range(6):
                        for c in range(2):
                            for f in range(2):
                                q = pe.transpose(p_m[m][:, f, c * P:(c + 1) * P], raw[:, m, c, f * P:(f + 1) * P], ident[:])
                    q.then_inc(turned, 1)

                @block.vector
                def _(dve):
                    dve.tensor_scalar(diag[:], ident[:], src_runs["whole"][:, 0:1], None, ALU.mult).then_inc(diag_made, 1)
                    dve.tensor_scalar(fixes[:], src_runs["fix_row"][:], float(ROWS), None, ALU.is_lt).then_inc(own, 1)
                    dve.wait_ge(rowed, 1)
                    dve.tensor_copy(whole_row[:], p_w[:, 0:P]).then_inc(own, 1)
                    dve.wait_ge(turned, 1)
                    for m in range(6):
                        dve.tensor_copy((wt, wp)[m % 2][:, m // 2], p_m[m][:]).then_inc(own, 1)
                    dve.wait_ge(own, 8)

        stat3 = sb("stat3", [P, 4])
        scale3, shift3, rows3 = sb("scale3", [P, 2]), sb("shift3", [P, 2]), sb("rows3", [P, 2, D])

        def edge_max(l, table, rows, own_index, other_index, target):
            g = src_runs
            with phase(nc, f"max{l}") as (sem, sb_, ps):
                xi, xj = sb_("xi", [P, B, D]), sb_("xj", [P, B, D])
                xt = sb_("xt", [P, HALF, 2, 2, P])
                dt = sb_("dt", [P, HALF, 2, P])
                total = sb_("total", [P, B, D])
                sq = sb_("sq", [P, 2, D])
                idx_i, idx_j = sb_("idx_i", [P, B], I32), sb_("idx_j", [P, B], I32)
                fix, fixed, fixed_sq = (sb_(n, [P, D]) for n in ("fix", "fixed", "fixed_sq"))
                flat = sb_("flat", [P, 2, P])
                state = sb_("state", [P, 2, P + 1])
                p_t = [ps(f"t{k}", [P, 2, 2, P]) for k in range(2)]
                p_y = [ps(f"y{k}", [P, 512]) for k in range(2)]
                p_s, p_f, p_c = ps("s", [P, 512]), ps("f", [P, 2, P]), ps("c", [P, 2, P])
                got_i, got_j, stored = (sem.many(n, B) for n in ("got_i", "got_j", "stored"))
                fed_i, fed_j, own, turned, copied, diffed, product, topped, squared, summed = (sem(n) for n in
                    ("fed_i", "fed_j", "own", "turned", "copied", "diffed", "product", "topped", "squared", "summed"))
                blank, fix_got, fix_ready, f_turned, f_scanned, f_back, f_squared = (sem(n) for n in
                    ("blank", "fix_got", "fix_ready", "f_turned", "f_scanned", "f_back", "f_squared"))
                gate = sem("gate")
                with nc.Block() as block:
                    @block.gpsimd
                    def _(pool):
                        last = pool.to_reg(rows - 1)
                        last_out = pool.to_reg(ROWS - 1)
                        feed_i = Feed(pool, gate, fed_i, idx_i, own_index, got_i)
                        feed_j = Feed(pool, gate, fed_j, idx_j, other_index, got_j)

                        def gather(i, b):
                            wait(pool, turned, i * B + (b + 1 - B))
                            pool.indirect_dma_start(xi[:, b, :], None, table, feed_i.at(b), bounds_check=last, oob_is_err=False).then_inc(got_i[b], 16)
                            pool.indirect_dma_start(xj[:, b, :], None, table, feed_j.at(b), bounds_check=last, oob_is_err=False).then_inc(got_j[b], 16)

                        indexed(pool, gather, [feed_i, feed_j])
                        for s in stored:
                            pool.wait_ge(s, 16 * STEPS)
                        pool.wait_ge(blank, 1)
                        at = bass.IndirectOffsetOnAxis(g["fix_row"][:, 0:1], 0)
                        pool.indirect_dma_start(fix[:], None, target, at, bounds_check=last_out, oob_is_err=False).then_inc(fix_got, 16)
                        pool.wait_ge(fix_ready, 1)
                        pool.indirect_dma_start(target, at, fixed[:], None, bounds_check=last_out, oob_is_err=False).then_inc(fix_got, 16)
                        pool.wait_ge(fix_got, 32)

                    @block.sync
                    def _(sp):
                        def store(i):
                            for b in range(B):
                                sp.wait_ge(topped, i * B + (b + 1))
                                sp.dma_start(target[bass.ds(i * (B * P) + b * P, P), :], total[:, b, :]).then_inc(stored[b], 16)

                        steps(sp, STEPS, store)

                    @block.tensor
                    def _(pe):
                        def turn(i, b):
                            pe.wait_ge(got_i[b], i * 16 + 16)
                            pe.wait_ge(got_j[b], i * 16 + 16)
                            wait(pe, copied, i * B + (b - 1))
                            for c in range(2):
                                for k, x in enumerate((xi, xj)):
                                    m = pe.transpose(p_t[b % 2][:, c, k, :], x[:, b, c * P:(c + 1) * P], ident[:])
                            m.then_inc(turned, 1)

                        def mul(i, b):
                            pe.wait_ge(diffed, i * B + (b + 1))
                            wait(pe, topped, i * B + (b - 1))
                            for c in range(2):
                                pe.matmul(p_y[b % 2][:, 0:D], xt[:, b % HALF, c, 0, :], wp[:, l, c, :], start=(c == 0), stop=False)
                            for c in range(2):
                                m = pe.matmul(p_y[b % 2][:, 0:D], dt[:, b % HALF, c, :], wt[:, l, c, :], start=False, stop=(c == 1))
                            m.then_inc(product, 1)

                        def add(i, b):
                            t = i * B + b
                            pe.wait_ge(squared, t + 1)
                            settle(pe, gate)
                            for k in range(4):
                                buf = total[:, b, (k % 2) * P:(k % 2 + 1) * P] if k < 2 else sq[:, b % 2, (k % 2) * P:(k % 2 + 1) * P]
                                m = pe.matmul(p_s[:, k:k + 1], buf, g["inner"][:, bass.ds(t, 1)], start=(isinstance(i, int) and i == 0 and b == 0 and k == 0),
                                              stop=False, skip_group_check=True)
                            m.then_inc(summed, 1)

                        columns(pe, [(turn, 0), (mul, 2), (add, 5)])
                        pe.wait_ge(topped, T)
                        for c in range(2):
                            m = pe.transpose(p_f[:, c, :], total[:, B - 1, c * P:(c + 1) * P], ident[:])
                        m.then_inc(f_turned, 1)
                        pe.wait_ge(f_scanned, 1)
                        for c in range(2):
                            m = pe.transpose(p_c[:, c, :], state[:, c, 0:P], ident[:])
                        m.then_inc(f_back, 1)
                        pe.wait_ge(f_squared, 1)
                        for k in range(4):
                            buf = (fixed, fixed_sq)[k // 2][:, (k % 2) * P:(k % 2 + 1) * P]
                            m = pe.matmul(p_s[:, k:k + 1], buf, fixes[:], start=False, stop=(k == 3), skip_group_check=True)
                        m.then_inc(summed, 1)

                    @block.scalar
                    def _(act):
                        def copy(i, b):
                            act.wait_ge(turned, i * B + (b + 1))
                            wait(act, product, i * B + (b + 1 - HALF))
                            if l == 0:
                                act.activation(xt[:, b % HALF], p_t[b % 2][:], ACT.Copy).then_inc(copied, 1)
                            else:
                                for c in range(2):
                                    m = act.activation(xt[:, b % HALF, c], p_t[b % 2][:, c], ACT.Relu, scale=scale3[:, c:c + 1], bias=shift3[:, c:c + 1])
                                m.then_inc(copied, 1)

                        def square(i, b):
                            act.wait_ge(topped, i * B + (b + 1))
                            wait(act, summed, i * B + (b - 1))
                            act.activation(sq[:, b % 2, :], total[:, b, :], ACT.Square).then_inc(squared, 1)

                        columns(act, [(copy, 0), (square, 4)])
                        act.wait_ge(fix_ready, 1)
                        act.activation(fixed_sq[:], fixed[:], ACT.Square).then_inc(f_squared, 1)

                    @block.vector
                    def _(dve):
                        c_ = Chain(dve, own, gate)
                        c_(dve.memset(total[:, B - 1, :], 0.0))
                        c_(dve.memset(state[:], 0.0))
                        dve.memset(fix[:], 0.0).then_inc(blank, 1)

                        def diff(i, b):
                            dve.wait_ge(copied, i * B + (b + 1))
                            wait(dve, product, i * B + (b + 1 - HALF))
                            dve.tensor_tensor(dt[:, b % HALF], xt[:, b % HALF, :, 1, :], xt[:, b % HALF, :, 0, :], ALU.subtract).then_inc(diffed, 1)

                        def most(i, b):
                            t = i * B + b
                            dve.wait_ge(product, t + 1)
                            wait(dve, stored[b], i * 16)
                            wait(dve, summed, i * B + (b + 1 - B))
                            wait(dve, topped, t)
                            dve.scalar_tensor_tensor(total[:, b, :], total[:, (b - 1) % B, :], g["cont"][:, bass.ds(t, 1)],
                                                     p_y[b % 2][:, 0:D], ALU.mult, ALU.max).then_inc(topped, 1)

                        columns(dve, [(diff, 0), (most, 3)])
                        dve.wait_ge(f_turned, 1)
                        c_(dve.tensor_copy(flat[:], p_f[:]))
                        for c in range(2):
                            c_(dve.tensor_tensor_scan(state[:, c, 1:P + 1], whole_row[:], flat[:, c, :], 0.0, ALU.add, ALU.max))
                        dve.sem_inc(f_scanned, 1)
                        dve.wait_ge(f_back, 1)
                        dve.wait_ge(fix_got, 16)
                        dve.tensor_tensor(fixed[:], fix[:], p_c[:].rearrange("p c q -> p (c q)"), ALU.max).then_inc(fix_ready, 1)
                        dve.wait_ge(summed, T + 1)
                        c_(dve.tensor_copy(stat3[:], p_s[:, 0:4]))

            batch_norm(f"norm3_{l}", [stat3], a["L3_gnn_gammas"][l], a["L3_gnn_betas"][l], None, scale3, shift3, rows3)

        edge_max(0, x3, N, src_runs["node"], src_runs["other"], top[0])
        edge_max(1, top[0], ROWS + 1, own_row, other_row, top[1])
        edge_max(2, top[1], ROWS + 1, own_row, other_row, top[2])

        with phase(nc, "last") as (sem, sb_, ps):
            x_in, v, xo = (sb_(n, [P, 2, JB, D]) for n in ("x_in", "v", "xo"))
            floor = sb_("floor", [P, D])
            st = norm_slots(sb_, "n", JB)
            got, stored = sem.many("got", 2), sem.many("stored", 2)
            own, made, floored, v_made, stats = (sem(n) for n in ("own", "made", "floored", "v_made", "stats"))
            gate = sem("gate")
            with nc.Block() as block:
                @block.sync
                def _(sp):
                    def load(i, s, p, j):
                        wait(sp, v_made, i * 2 + (s - 1))
                        sp.dma_start(x_in[0:p, s, 0:j, :], group(x3, i, s, p, j)).then_inc(got[s], 16)

                    def store(i, s, p, j):
                        sp.wait_ge(made, i * 2 + (s + 1))
                        sp.dma_start(group(out, i, s, p, j), xo[0:p, s, 0:j, :]).then_inc(stored[s], 16)

                    pairs(sp, [(load, 0), (store, 3)], j=JB)
                    sp.wait_ge(stored[0], 16 * (pair_count(JB) + 1))
                    sp.wait_ge(stored[1], 16 * pair_count(JB))

                @block.gpsimd
                def _(pool):
                    pool.wait_ge(floored, 1)

                    def add(i, s, p, j):
                        pool.wait_ge(got[s], i * 16 + 16)
                        wait(pool, made, i * 2 + (s - 1))
                        pool.tensor_tensor(v[0:p, s, 0:j, :], x_in[0:p, s, 0:j, :], floor[0:p, :].unsqueeze(1).to_broadcast([p, j, D]), ALU.add).then_inc(v_made, 1)

                    pairs(pool, [(add, 0)], j=JB)

                @block.vector
                def _(dve):
                    c_ = Chain(dve, own, gate)
                    dve.tensor_scalar(floor[:], rows3[:, 1, :], 0.0, None, ALU.max).then_inc(floored, 1)

                    def node(i, s, p, j):
                        dve.wait_ge(v_made, i * 2 + (s + 1))
                        wait(dve, made, i * 2 + (s - 1))
                        norm_stats(c_, v[:, s], st, s, p, j)
                        dve.sem_inc(stats, 1)

                    pairs(dve, [(node, 0)], c_, 2 * (2 * JB + 13), j=JB)

                @block.scalar
                def _(act):
                    def norm(i, s, p, j):
                        act.wait_ge(stats, i * 2 + (s + 1))
                        wait(act, stored[s], i * 16)
                        normalize(act, v[:, s], xo[:, s], st, s, p, j).then_inc(made, 1)

                    pairs(act, [(norm, 0)], j=JB)

        node_ends("out_ends", src_runs, top[2], x3, out, rows3, False)


_NAMES = ['x', 'src', 'dst', 'L0_gnn_W1', 'L0_gnn_b1', 'L0_gnn_W2', 'L0_gnn_b2', 'L1_gnn_W1', 'L1_gnn_b1', 'L1_gnn_W2', 'L1_gnn_b2', 'L1_gnn_a', 'L2_gnn_W_gcn', 'L2_gnn_b_gcn', 'L2_gnn_g0', 'L2_gnn_beta0', 'L2_gnn_W1', 'L2_gnn_a_src1', 'L2_gnn_a_dst1', 'L2_gnn_b1', 'L2_gnn_g1', 'L2_gnn_beta1', 'L2_gnn_W2', 'L2_gnn_a_src2', 'L2_gnn_a_dst2', 'L2_gnn_b2', 'L2_gnn_g2', 'L2_gnn_beta2', 'L3_gnn_thetas', 'L3_gnn_phis', 'L3_gnn_gammas', 'L3_gnn_betas']


def kernel(**inputs):
    import numpy as np
    import concourse.bacc as bacc
    from concourse.bass_utils import run_bass_kernel_spmd

    nc = bacc.Bacc("TRN2", target_bir_lowering=False, num_devices=1)
    arrays, aps = {}, {}
    for name in _NAMES:
        array = np.ascontiguousarray(inputs[name])
        arrays[f"in_{name}"] = array
        aps[name] = nc.dram_tensor(f"in_{name}", array.shape, mybir.dt.from_np(array.dtype), kind="ExternalInput").ap()
    out = nc.dram_tensor("out", (N, D), F32, kind="ExternalOutput").ap()
    program(nc, aps, out)
    result = run_bass_kernel_spmd(nc, [arrays], core_ids=[0])
    return result.results[0]["out"]
```
